# Optimizing a Trainium2 kernel written in Bass

```python
import numpy as np
import jax
import jax.numpy as jnp

def _softmax(x, axis=-1):
    return jax.nn.softmax(x, axis=axis)

def _gelu(x):
    return jax.nn.gelu(x, approximate=True)

def _silu(x):
    return jax.nn.silu(x)

def _sigmoid(x):
    return jax.nn.sigmoid(x)

def _layernorm(x, axis=-1, eps=1e-05):
    m = jnp.mean(x, axis=axis, keepdims=True)
    v = jnp.var(x, axis=axis, keepdims=True)
    return (x - m) / jnp.sqrt(v + eps)

def _scatter_add(tgt, idx, src, axis=0):
    return tgt.at[idx].add(src)

def _segment_sum(src, seg, n):
    return jax.ops.segment_sum(src, seg, n)
kernel_name = 'mk_recurrent_d2_jaxref_r8_8e54d6'

def setup_inputs(seed: int=0):
    np.random.seed(seed)
    _w = jnp.asarray

    def _L0_attn_setup():
        import jax, jax.numpy as jnp
        import numpy as np
        D = 128
        H = 16
        HV = 4
        HD = D // H
        WIN = 64
        EPS = 1.1920929e-07

        def rms_norm(x, w):
            var = jnp.mean(x * x, axis=-1, keepdims=True)
            return x * jax.lax.rsqrt(var + EPS) * w
        key = jax.random.key(seed)
        ks = jax.random.split(key, 12)
        s = 0.02
        return {'x': jax.random.normal(ks[0], (1, 256, D), jnp.float32), 'w_q': jax.random.normal(ks[1], (D, D), jnp.float32) * s, 'b_q': jnp.zeros((D,), jnp.float32), 'w_k': jax.random.normal(ks[2], (D, D), jnp.float32) * s, 'b_k': jnp.zeros((D,), jnp.float32), 'w_v': jax.random.normal(ks[3], (D, HV * HD), jnp.float32) * s, 'b_v': jnp.zeros((HV * HD,), jnp.float32), 'rms_q_w': jnp.ones((HD,), jnp.float32), 'rms_k_w': jnp.ones((HD,), jnp.float32), 'w_o': jax.random.normal(ks[4], (D, D), jnp.float32) * s, 'b_o': jnp.zeros((D,), jnp.float32)}
    _L0_attn_in = _L0_attn_setup()

    def _L0_ffn_setup():
        import jax, jax.numpy as jnp
        import numpy as np
        DIM = 128
        NUM_EXPERTS = 8
        TOP_K = 2
        key = jax.random.key(seed)
        ks = jax.random.split(key, 7)
        s_in = 1.0 / np.sqrt(DIM)
        s_hid = 1.0 / np.sqrt(4 * DIM)
        x = jax.random.normal(ks[0], (2, 256, DIM), dtype=jnp.float32)
        gate_w = jax.random.normal(ks[1], (DIM, NUM_EXPERTS), dtype=jnp.float32) * s_in
        gate_b = jax.random.normal(ks[2], (NUM_EXPERTS,), dtype=jnp.float32) * 0.01
        w1 = jax.random.normal(ks[3], (NUM_EXPERTS, DIM, 4 * DIM), dtype=jnp.float32) * s_in
        b1 = jax.random.normal(ks[4], (NUM_EXPERTS, 4 * DIM), dtype=jnp.float32) * 0.01
        w2 = jax.random.normal(ks[5], (NUM_EXPERTS, 4 * DIM, DIM), dtype=jnp.float32) * s_hid
        b2 = jax.random.normal(ks[6], (NUM_EXPERTS, DIM), dtype=jnp.float32) * 0.01
        return {'x': x, 'gate_w': gate_w, 'gate_b': gate_b, 'w1': w1, 'b1': b1, 'w2': w2, 'b2': b2}
    _L0_ffn_in = _L0_ffn_setup()

    def _L1_attn_setup():
        import jax, jax.numpy as jnp
        import numpy as np
        HID = 128
        NH = 16
        HD = HID // NH
        WIN = 64
        EPS = 1e-05

        def layernorm(x, g, b):
            m = jnp.mean(x, axis=-1, keepdims=True)
            v = jnp.mean((x - m) ** 2, axis=-1, keepdims=True)
            return (x - m) / jnp.sqrt(v + EPS) * g + b

        def windowed_attention(q, k, v, window_size):
            bh, S, D = q.shape
            scale = float(D) ** (-0.5)
            w2, w4 = (window_size // 2, window_size // 4)
            out = jnp.zeros_like(q)
            for i in range(0, S, w2):
                start = max(0, i - w4)
                end = min(S, i + window_size - w4)
                qw = q[:, start:end] * scale
                kw = k[:, start:end]
                vw = v[:, start:end]
                attn = jax.nn.softmax(jnp.einsum('bqd,bkd->bqk', qw, kw), axis=-1)
                wo = jnp.einsum('bqk,bkd->bqd', attn, vw)
                if i == 0:
                    out = out.at[:, start:end].set(wo)
                else:
                    oe = min(i + w4, S)
                    n = oe - start
                    alphas = jnp.linspace(0.0, 1.0, n).reshape(1, -1, 1)
                    blended = (1 - alphas) * out[:, start:oe] + alphas * wo[:, :n]
                    out = out.at[:, start:oe].set(blended)
                    out = out.at[:, oe:end].set(wo[:, n:end - start])
            return out
        key = jax.random.key(seed)
        ks = jax.random.split(key, 12)
        s = 0.02
        d = {'hidden_states': jax.random.normal(ks[0], (4, 256, HID), jnp.float32), 'ln1_g': jnp.ones((HID,), jnp.float32), 'ln1_b': jnp.zeros((HID,), jnp.float32), 'wq': jax.random.normal(ks[1], (HID, HID), jnp.float32) * s, 'bq': jnp.zeros((HID,), jnp.float32), 'wk': jax.random.normal(ks[2], (HID, HID), jnp.float32) * s, 'bk': jnp.zeros((HID,), jnp.float32), 'wv': jax.random.normal(ks[3], (HID, HID), jnp.float32) * s, 'bv': jnp.zeros((HID,), jnp.float32), 'wproj': jax.random.normal(ks[4], (HID, HID), jnp.float32) * s, 'bproj': jnp.zeros((HID,), jnp.float32), 'ln2_g': jnp.ones((HID,), jnp.float32), 'ln2_b': jnp.zeros((HID,), jnp.float32), 'w1': jax.random.normal(ks[5], (HID, 4 * HID), jnp.float32) * s, 'b1': jnp.zeros((4 * HID,), jnp.float32), 'w2': jax.random.normal(ks[6], (4 * HID, HID), jnp.float32) * s, 'b2': jnp.zeros((HID,), jnp.float32)}
        return d
    _L1_attn_in = _L1_attn_setup()

    def _L1_ffn_setup():
        import jax, jax.numpy as jnp
        import numpy as np
        D_MODEL = 128
        D_FF = 512
        NUM_EXPERTS = 8
        key = jax.random.key(seed)
        ks = jax.random.split(key, 8)
        scale_in = 1.0 / np.sqrt(D_MODEL)
        scale_ff = 1.0 / np.sqrt(D_FF)
        x = jax.random.normal(ks[0], (4, 256, D_MODEL), dtype=jnp.float32)
        gate_w = jax.random.uniform(ks[1], (NUM_EXPERTS, D_MODEL), jnp.float32, -scale_in, scale_in)
        gate_b = jax.random.uniform(ks[2], (NUM_EXPERTS,), jnp.float32, -scale_in, scale_in)
        expert_bias = jnp.zeros((NUM_EXPERTS,), dtype=jnp.float32)
        w1 = jax.random.uniform(ks[3], (NUM_EXPERTS, D_MODEL, D_FF), jnp.float32, -scale_in, scale_in)
        b1 = jax.random.uniform(ks[4], (NUM_EXPERTS, D_FF), jnp.float32, -scale_in, scale_in)
        w2 = jax.random.uniform(ks[5], (NUM_EXPERTS, D_FF, D_MODEL), jnp.float32, -scale_ff, scale_ff)
        b2 = jax.random.uniform(ks[6], (NUM_EXPERTS, D_MODEL), jnp.float32, -scale_ff, scale_ff)
        return {'x': x, 'gate_w': gate_w, 'gate_b': gate_b, 'expert_bias': expert_bias, 'w1': w1, 'b1': b1, 'w2': w2, 'b2': b2}
    _L1_ffn_in = _L1_ffn_setup()
    _d = {'L0_attn_x': _L0_attn_in['x'], 'L0_attn_w_q': _L0_attn_in['w_q'], 'L0_attn_b_q': _L0_attn_in['b_q'], 'L0_attn_w_k': _L0_attn_in['w_k'], 'L0_attn_b_k': _L0_attn_in['b_k'], 'L0_attn_w_v': _L0_attn_in['w_v'], 'L0_attn_b_v': _L0_attn_in['b_v'], 'L0_attn_rms_q_w': _L0_attn_in['rms_q_w'], 'L0_attn_rms_k_w': _L0_attn_in['rms_k_w'], 'L0_attn_w_o': _L0_attn_in['w_o'], 'L0_attn_b_o': _L0_attn_in['b_o'], 'L0_ffn_gate_w': _L0_ffn_in['gate_w'], 'L0_ffn_gate_b': _L0_ffn_in['gate_b'], 'L0_ffn_w1': _L0_ffn_in['w1'], 'L0_ffn_b1': _L0_ffn_in['b1'], 'L0_ffn_w2': _L0_ffn_in['w2'], 'L0_ffn_b2': _L0_ffn_in['b2'], 'L1_attn_ln1_g': _L1_attn_in['ln1_g'], 'L1_attn_ln1_b': _L1_attn_in['ln1_b'], 'L1_attn_wq': _L1_attn_in['wq'], 'L1_attn_bq': _L1_attn_in['bq'], 'L1_attn_wk': _L1_attn_in['wk'], 'L1_attn_bk': _L1_attn_in['bk'], 'L1_attn_wv': _L1_attn_in['wv'], 'L1_attn_bv': _L1_attn_in['bv'], 'L1_attn_wproj': _L1_attn_in['wproj'], 'L1_attn_bproj': _L1_attn_in['bproj'], 'L1_attn_ln2_g': _L1_attn_in['ln2_g'], 'L1_attn_ln2_b': _L1_attn_in['ln2_b'], 'L1_attn_w1': _L1_attn_in['w1'], 'L1_attn_b1': _L1_attn_in['b1'], 'L1_attn_w2': _L1_attn_in['w2'], 'L1_attn_b2': _L1_attn_in['b2'], 'L1_ffn_gate_w': _L1_ffn_in['gate_w'], 'L1_ffn_gate_b': _L1_ffn_in['gate_b'], 'L1_ffn_expert_bias': _L1_ffn_in['expert_bias'], 'L1_ffn_w1': _L1_ffn_in['w1'], 'L1_ffn_b1': _L1_ffn_in['b1'], 'L1_ffn_w2': _L1_ffn_in['w2'], 'L1_ffn_b2': _L1_ffn_in['b2']}
    _x0 = _d['L0_attn_x']
    _d['L0_attn_x'] = jax.random.normal(jax.random.fold_in(jax.random.key(seed), 1), (4, 512, 128), dtype=_x0.dtype)
    del _x0
    return _d

def reference(L0_attn_x, L0_attn_w_q, L0_attn_b_q, L0_attn_w_k, L0_attn_b_k, L0_attn_w_v, L0_attn_b_v, L0_attn_rms_q_w, L0_attn_rms_k_w, L0_attn_w_o, L0_attn_b_o, L0_ffn_gate_w, L0_ffn_gate_b, L0_ffn_w1, L0_ffn_b1, L0_ffn_w2, L0_ffn_b2, L1_attn_ln1_g, L1_attn_ln1_b, L1_attn_wq, L1_attn_bq, L1_attn_wk, L1_attn_bk, L1_attn_wv, L1_attn_bv, L1_attn_wproj, L1_attn_bproj, L1_attn_ln2_g, L1_attn_ln2_b, L1_attn_w1, L1_attn_b1, L1_attn_w2, L1_attn_b2, L1_ffn_gate_w, L1_ffn_gate_b, L1_ffn_expert_bias, L1_ffn_w1, L1_ffn_b1, L1_ffn_w2, L1_ffn_b2):

    def _L0_attn_ref(x, w_q, b_q, w_k, b_k, w_v, b_v, rms_q_w, rms_k_w, w_o, b_o):
        import jax, jax.numpy as jnp
        import numpy as np
        D = 128
        H = 16
        HV = 4
        HD = D // H
        WIN = 64
        EPS = 1.1920929e-07

        def rms_norm(x, w):
            var = jnp.mean(x * x, axis=-1, keepdims=True)
            return x * jax.lax.rsqrt(var + EPS) * w
        B, T, _ = x.shape
        q = (x @ w_q + b_q).reshape(B, T, H, HD).transpose(0, 2, 1, 3)
        k = (x @ w_k + b_k).reshape(B, T, H, HD).transpose(0, 2, 1, 3)
        v = (x @ w_v + b_v).reshape(B, T, HV, HD).transpose(0, 2, 1, 3)
        q = rms_norm(q, rms_q_w)
        k = rms_norm(k, rms_k_w)
        attn = jnp.einsum('bhtd,bhsd->bhts', q, k) / np.sqrt(HD).astype(np.float32)
        i = jnp.arange(T)[:, None]
        j = jnp.arange(T)[None, :]
        mask = ((j <= i) & (j >= i - WIN)).astype(attn.dtype)
        masked_attn = attn * mask
        gene_means = jnp.mean(jax.nn.sigmoid(masked_attn), axis=-1)
        denom = gene_means + 0.5
        sum_inv = jnp.sum(1.0 / denom, axis=2, keepdims=True)
        gene_fitness = 1.0 / (denom * sum_inv)
        weighted = masked_attn * gene_fitness[..., None]
        logits = weighted + (1.0 - mask) * -10000000000.0
        attn_w = jax.nn.softmax(logits, axis=-1)
        v_full = jnp.repeat(v, H // HV, axis=1)
        out = jnp.einsum('bhts,bhsd->bhtd', attn_w, v_full)
        out = out.transpose(0, 2, 1, 3).reshape(B, T, D)
        return out @ w_o + b_o

    def _L0_ffn_ref(x, gate_w, gate_b, w1, b1, w2, b2):
        import jax, jax.numpy as jnp
        import numpy as np
        DIM = 128
        NUM_EXPERTS = 8
        TOP_K = 2
        B, N, C = x.shape
        flat_x = x.reshape(-1, C)
        logits = flat_x @ gate_w + gate_b
        _, topk_idx = jax.lax.top_k(logits, TOP_K)
        e_star = jnp.max(topk_idx, axis=-1)
        out = jnp.zeros_like(flat_x)
        for i in range(NUM_EXPERTS):
            h = jax.nn.gelu(flat_x @ w1[i] + b1[i], approximate=False)
            y = h @ w2[i] + b2[i]
            out = jnp.where((e_star == i)[:, None], y, out)
        return (TOP_K * out).reshape(B, N, C)

    def _L1_attn_ref(hidden_states, ln1_g, ln1_b, wq, bq, wk, bk, wv, bv, wproj, bproj, ln2_g, ln2_b, w1, b1, w2, b2):
        import jax, jax.numpy as jnp
        import numpy as np
        HID = 128
        NH = 16
        HD = HID // NH
        WIN = 64
        EPS = 1e-05

        def layernorm(x, g, b):
            m = jnp.mean(x, axis=-1, keepdims=True)
            v = jnp.mean((x - m) ** 2, axis=-1, keepdims=True)
            return (x - m) / jnp.sqrt(v + EPS) * g + b

        def windowed_attention(q, k, v, window_size):
            bh, S, D = q.shape
            scale = float(D) ** (-0.5)
            w2, w4 = (window_size // 2, window_size // 4)
            out = jnp.zeros_like(q)
            for i in range(0, S, w2):
                start = max(0, i - w4)
                end = min(S, i + window_size - w4)
                qw = q[:, start:end] * scale
                kw = k[:, start:end]
                vw = v[:, start:end]
                attn = jax.nn.softmax(jnp.einsum('bqd,bkd->bqk', qw, kw), axis=-1)
                wo = jnp.einsum('bqk,bkd->bqd', attn, vw)
                if i == 0:
                    out = out.at[:, start:end].set(wo)
                else:
                    oe = min(i + w4, S)
                    n = oe - start
                    alphas = jnp.linspace(0.0, 1.0, n).reshape(1, -1, 1)
                    blended = (1 - alphas) * out[:, start:oe] + alphas * wo[:, :n]
                    out = out.at[:, start:oe].set(blended)
                    out = out.at[:, oe:end].set(wo[:, n:end - start])
            return out
        B, S, _ = hidden_states.shape
        residual = hidden_states
        x = layernorm(hidden_states, ln1_g, ln1_b)
        q = (x @ wq + bq).reshape(B, S, NH, HD).transpose(0, 2, 1, 3).reshape(B * NH, S, HD)
        k = (x @ wk + bk).reshape(B, S, NH, HD).transpose(0, 2, 1, 3).reshape(B * NH, S, HD)
        v = (x @ wv + bv).reshape(B, S, NH, HD).transpose(0, 2, 1, 3).reshape(B * NH, S, HD)
        ctx = windowed_attention(q, k, v, WIN)
        ctx = ctx.reshape(B, NH, S, HD).transpose(0, 2, 1, 3).reshape(B, S, HID)
        out = ctx @ wproj + bproj + residual
        residual2 = out
        h = layernorm(out, ln2_g, ln2_b)
        h = jax.nn.gelu(h @ w1 + b1, approximate=False)
        h = h @ w2 + b2
        return h + residual2

    def _L1_ffn_ref(x, gate_w, gate_b, expert_bias, w1, b1, w2, b2):
        import jax, jax.numpy as jnp
        import numpy as np
        D_MODEL = 128
        D_FF = 512
        NUM_EXPERTS = 8
        gate_logits = jnp.einsum('bsd,ed->bse', x, gate_w) + gate_b + expert_bias
        top_idx = jnp.argmax(gate_logits, axis=-1)
        out = jnp.zeros_like(x)
        for e in range(NUM_EXPERTS):
            mask = (top_idx == e)[..., None].astype(x.dtype)
            h = jax.nn.relu(jnp.einsum('bsd,df->bsf', x, w1[e]) + b1[e])
            y = jnp.einsum('bsf,fd->bsd', h, w2[e]) + b2[e]
            out = out + mask * y
        return out
    x = L0_attn_x
    xn = _layernorm(x, axis=-1)
    s = _L0_attn_ref(xn, L0_attn_w_q, L0_attn_b_q, L0_attn_w_k, L0_attn_b_k, L0_attn_w_v, L0_attn_b_v, L0_attn_rms_q_w, L0_attn_rms_k_w, L0_attn_w_o, L0_attn_b_o)
    g = _silu(_L0_ffn_ref(xn, L0_ffn_gate_w, L0_ffn_gate_b, L0_ffn_w1, L0_ffn_b1, L0_ffn_w2, L0_ffn_b2))
    x = x + s * g
    xn = _layernorm(x, axis=-1)
    s = _L1_attn_ref(xn, L1_attn_ln1_g, L1_attn_ln1_b, L1_attn_wq, L1_attn_bq, L1_attn_wk, L1_attn_bk, L1_attn_wv, L1_attn_bv, L1_attn_wproj, L1_attn_bproj, L1_attn_ln2_g, L1_attn_ln2_b, L1_attn_w1, L1_attn_b1, L1_attn_w2, L1_attn_b2)
    g = _silu(_L1_ffn_ref(xn, L1_ffn_gate_w, L1_ffn_gate_b, L1_ffn_expert_bias, L1_ffn_w1, L1_ffn_b1, L1_ffn_w2, L1_ffn_b2))
    x = x + s * g
    return x

_drawn_inputs = setup_inputs


def setup_inputs(seed=0):
    import zlib

    import numpy as np

    out = dict(_drawn_inputs(seed))
    spreads = {'L0_attn_b_q': (0.0, 0.8),
     'L0_attn_b_k': (0.0, 0.8),
     'L0_attn_b_v': (0.0, 0.366),
     'L0_attn_rms_q_w': (1.0, 0.6),
     'L0_attn_rms_k_w': (1.0, 0.6),
     'L0_attn_b_o': (0.0, 0.1),
     'L1_attn_ln1_g': (1.0, 0.6),
     'L1_attn_ln1_b': (0.0, 0.8),
     'L1_attn_bq': (0.0, 0.8),
     'L1_attn_bk': (0.0, 0.8),
     'L1_attn_bv': (0.0, 0.8),
     'L1_attn_bproj': (0.0, 0.674),
     'L1_attn_ln2_g': (1.0, 0.6),
     'L1_attn_ln2_b': (0.0, 0.8),
     'L1_attn_b1': (0.0, 0.8),
     'L1_attn_b2': (0.0, 0.672),
     'L1_ffn_expert_bias': (0.0, 0.1)}
    factors = {'L0_attn_w_q': 8.0,
     'L0_attn_w_k': 8.0,
     'L0_attn_w_v': 4.204,
     'L0_ffn_gate_b': 6.333,
     'L0_ffn_b1': 8.0,
     'L0_ffn_b2': 8.0,
     'L1_attn_wq': 8.0,
     'L1_attn_wk': 8.0,
     'L1_attn_wv': 8.0,
     'L1_attn_wproj': 8.0,
     'L1_attn_w1': 8.0,
     'L1_attn_w2': 7.669,
     'L1_ffn_b1': 5.364,
     'L1_ffn_b2': 4.315}
    for name, (base, spread) in spreads.items():
        noise = np.random.default_rng([zlib.crc32(name.encode()), seed]).standard_normal(out[name].shape)
        drawn = base * np.exp(spread * noise) if base else spread * noise
        out[name] = jnp.asarray(drawn.astype(out[name].dtype))
    for name, factor in factors.items():
        out[name] = (out[name] * factor).astype(out[name].dtype)
    return out
```

```python
from contextlib import ExitStack

import concourse.bass as bass
import numpy as np
from concourse import mybir

F32 = mybir.dt.float32
BF16 = mybir.dt.bfloat16
ALU = mybir.AluOpType
ACT = mybir.ActivationFunctionType
AX = mybir.AxisListType

P = 128
D = 128
B, T = 4, 512
NT = T // P
NTT = B * NT
H, HD = 16, 8
NU = T // 64
NE, DF = 8, 512
FC = DF // P
WIN = 64
ROT = 16
SPLIT = 6 * HD
BIG = 1e10
LN_EPS = 1e-5
RMS_EPS = 1.1920929e-07


class Steps:

    def __init__(self, eng, sem):
        self.eng, self.sem, self.n = eng, sem, 0

    def __call__(self, ins):
        self.n += 1
        ins.then_inc(self.sem, 1)
        self.eng.wait_ge(self.sem, self.n)

    def restart(self):
        self.eng.sem_clear(self.sem)
        self.n = 0


def block_kernel(nc, a, out, dbg):
    with ExitStack() as ctx:
        def sb(name, shape, dt=F32):
            return ctx.enter_context(nc.sbuf_tensor(name, shape, dt))

        def sem(name):
            return ctx.enter_context(nc.semaphore(name))

        arrived = sem("arrived")
        go = {e: sem(f"go_{e}") for e in ("vector", "scalar", "gpsimd", "tensor")}

        class Phase:

            def __init__(self, vec, act, pool, pe, first, last, n, sync=None):
                self.vec, self.act, self.pool, self.pe = vec, act, pool, pe
                self.first, self.last, self.n, self.sync = first, last, n, sync

        def turns(eng, name, n):
            with eng.Fori(0, n) as i:
                yield i
                eng.drain().then_inc(arrived, 1)
                eng.wait_ge(go[name], 1)
                eng.sem_clear(go[name])

        def clear_when_met(sp, first, last):
            sp.wait_ge(arrived, 4)
            sp.sem_clear(range(first.num, last.num + 1))
            sp.sem_clear(arrived)
            for e in go.values():
                sp.sem_inc(e, 1)

        ps_score = ctx.enter_context(nc.psum_tensor("ps_score", [P, 2, 1024], F32))
        ps_turn = ctx.enter_context(nc.psum_tensor("ps_turn", [P, 2, 512], F32))
        ps_proj = ctx.enter_context(nc.psum_tensor("ps_proj", [P, 2, 512], F32))

        x = sb("x", [P, NTT * D])
        xn = sb("xn", [P, NTT * D])
        xnT = sb("xnT", [P, B * T])
        xlT = sb("xlT", [P, B * T])
        s_out = sb("s_out", [P, NTT * D])
        moe = sb("moe", [P, NTT * D])
        gate = sb("gate", [P, NTT, NE])
        ident = sb("ident", [P, P])
        identb = sb("identb", [P, P], BF16)
        ones = sb("ones", [P, P])
        neghalf = sb("neghalf", [P, 256])
        maskq = sb("maskq", [P, 4, 512], BF16)
        maskk = sb("maskk", [P, 5, 512], BF16)
        tab = sb("tab", [P, 64])
        iota8 = sb("iota8", [P, NTT, NE])
        pick8 = sb("pick8", [P, NTT, NE])
        pick8b = sb("pick8b", [P, NTT, NE])
        best = sb("best", [P, NTT])
        pickA = sb("pickA", [P, NTT])
        pickB = sb("pickB", [P, NTT])

        stats = sb("stats", [P, NT, 6])
        mv = sb("mv", [P, NT, 2])
        var = sb("var", [P, NT])
        rstd = sb("rstd", [P, NT])
        xs = sb("xs", [P, NT * D])
        xsT = sb("xsT", [P, T])
        xT = sb("xT", [P, 64 + T + 64])
        q4 = sb("q4", [P, NT * H, HD])
        k4 = sb("k4", [P, NT * H, HD])
        sq = sb("sq", [P, NT * H, HD])
        rest = sb("rest", [P, NT * H, HD])
        ss = sb("ss", [P, 2, NT * H])
        rr = sb("rr", [P, 2, NT * H])
        eq = sb("eq", [P, NT, H, 64], BF16)
        ek = sb("ek", [P, NT, H, 64], BF16)
        qT = sb("qT", [P, 8, T], BF16)
        kT = sb("kT", [P, 8, 64 + T + 64], BF16)
        v = sb("v", [P, NU, H * 36])
        th = sb("th", [P, 2, 1024])
        pT = sb("pT", [P, 2, 1024])
        gm = sb("gm", [P, NT, H * 4])
        tsum = sb("tsum", [P, NT, H])
        inv = sb("inv", [P, NT, H])
        fit = sb("fit", [P, NT, H])
        fits = sb("fits", [P, NT, H])
        sinv = sb("sinv", [P, H])
        shift = sb("shift", [P, NT, H * 4])
        shifts = sb("shifts", [P, NT, H * 4])
        shr = sb("shr", [P, NT, H * 4])
        eA = sb("eA", [P, NT, H, 4])
        eB = sb("eB", [P, NT, H, 4])
        mA = sb("mA", [P, NT * H])
        osb = sb("osb", [P, H * 36])
        cs = sb("cs", [P, H, 4])
        cs2 = sb("cs2", [P, H, 4])
        wtot = sb("wtot", [P, H])
        wtot2 = sb("wtot2", [P, H])
        wpv = sb("wpv", [P, H, 8, 4])
        head = sb("head", [P, D])
        headT = sb("headT", [P, P])
        o1 = sb("o1", [P, D])

        w1 = sb("w1", [P, 2, DF])
        w2 = sb("w2", [P, 2, FC * D])
        b2r = sb("b2r", [1, 2, D])
        hT = sb("hT", [P, 2, FC * 512])

        load = sem("load")


        LOADS = [0]

        def fetch(eng, dst, src):
            LOADS[0] += 16
            eng.dma_start(dst, src).then_inc(load, 16)

        W = {}
        for n, shape in (("L0_wqk", [P, 256]), ("L1_wqk", [P, 256]), ("L0_wv", [P, 32]), ("L1_wv", [P, 128]),
                         ("L0_wo", [P, D]), ("L1_wo", [P, D]), ("L0_gw", [P, NE]), ("L1_gw", [P, NE]),
                         ("L1_mw1", [P, DF]), ("L1_b1e", [P, NE * FC]), ("L0_b1e", [P, NE * FC]), ("L1_mb1", [P, FC])):
            W[n] = sb(n, shape)
        W["L1_mw2"] = sb("L1_mw2", [P, FC, D])
        ROWS = {"L0_bqk": 256, "L1_bqk": 256, "L0_bv": 32, "L1_bv": 128, "L0_bo": D, "L1_bo": D,
                "L0_gb": NE, "L1_gb": NE, "L1_eb": NE, "L1_mb2": D}
        for n, k in ROWS.items():
            W[n] = sb(n, [1, k])
        WIDE = {"L0_rms": 16, "L1_ln1g": D, "L1_ln1b": D, "L1_ln2g": D, "L1_ln2b": D}
        for n, k in WIDE.items():
            W[n] = sb(n, [P, k])
        rmsw = sb("rmsw", [P, 2, HD])

        x3 = a["x"].rearrange("b (t p) d -> p (b t) d", p=P)
        out3 = out.rearrange("b (t p) d -> p (b t) d", p=P)

        block = ctx.enter_context(nc.Block())

        tab_nm = tab[:, 0:4]
        tab_al = tab[:, 4:8]
        tab_al1 = tab[:, 8:12]
        tab_nA = tab[:, 12:16]
        tab_nB = tab[:, 16:20]
        tab_bd = tab[:, 20:24]
        tab_mod = tab[:, 24:28]

        dve_chain = sem("dve_chain")
        act_chain = sem("act_chain")
        pool_chain = sem("pool_chain")

        def sync_load(sp):
            fetch(sp, x[:, :].rearrange("p (n d) -> p n d", d=D), x3)
            for n in ("ident", "identb", "maskq", "maskk", "tab", "iota8"):
                t = {"ident": ident, "identb": identb, "maskq": maskq, "maskk": maskk, "tab": tab, "iota8": iota8}[n]
                src = a[n].bitcast(BF16) if n in ("identb", "maskq", "maskk") else a[n]
                fetch(sp, t[tuple(slice(None) for _ in t.shape)], src)
            for n, t in W.items():
                src = a[n]
                if n in ROWS or n in WIDE:
                    src = src.rearrange("(o n) -> o n", o=1)
                if n in WIDE:
                    src = src.broadcast_to([P, WIDE[n]])
                if n == "L1_mw2":
                    src = src.rearrange("(c p) n -> p c n", p=P)
                fetch(sp, t[tuple(slice(None) for _ in t.shape)], src)

        def loaded(eng):
            eng.wait_ge(load, LOADS_ALL)

        LOADS_ALL = 16 * (7 + len(W))

        made = sem("constants_made_2")

        def pool_const(po):
            po.memset(ones[:, :], 1.0).then_inc(made, 1)
            po.memset(neghalf[:, :], -0.5).then_inc(made, 1)
            po.memset(eq[:, :, :, :], 0.0).then_inc(made, 1)
            po.memset(ek[:, :, :, :], 0.0).then_inc(made, 1)
            po.memset(moe[:, :], 0.0).then_inc(made, 1)

        def consts(eng):
            eng.wait_ge(made, 5)

        def norm_phase(L, joined):
            s_var = sem(f"{L}_var")
            s_rstd = sem(f"{L}_rstd")
            s_xs = sem(f"{L}_xs")
            s_tr = sem(f"{L}_tr")
            s_xsT = sem(f"{L}_xsT")
            s_xnc = sem(f"{L}_xn_kept")
            s_gp = sem(f"{L}_gp")
            s_gate = sem(f"{L}_gate")
            xl = sb(f"xl{L}", [P, NT * D])
            s_xl = sem(f"{L}_xl")

            def vec(dv):
                st = Steps(dv, dve_chain)
                loaded(dv)
                if joined is not None:
                    dv.wait_ge(joined, 1)
                for i in turns(dv, "vector", B):
                    for r in range(1 + (L == 1)):
                        for t in range(NT):
                            src = x[:, bass.ds((i * NT + t) * D, D)] if r == 0 else xs[:, t * D:(t + 1) * D]
                            st(nc.vector.bn_stats(stats[:, t, :], src))
                            st(nc.vector.bn_aggr(mv[:, t, :], stats[:, t, :]))
                        nc.vector.tensor_scalar(var[:, :], mv[:, :, 1], LN_EPS, None, ALU.add).then_inc(s_var, 1)
                        if r > 0:
                            dv.wait_ge(s_tr, r)
                        dv.wait_ge(s_rstd, r + 1)
                        dst = xs if r == 0 else xl
                        for t in range(NT):
                            src = x[:, bass.ds((i * NT + t) * D, D)] if r == 0 else xs[:, t * D:(t + 1) * D]
                            ins = nc.vector.tensor_scalar(dst[:, t * D:(t + 1) * D], src, mv[:, t, 0:1],
                                                          rstd[:, t:t + 1], ALU.subtract, ALU.mult)
                            if r == 0 and t == NT - 1:
                                ins.then_inc(s_xs, 1)
                                dv.wait_ge(s_xs, 1)
                            else:
                                st(ins)
                        if r == 1:
                            x4 = xl[:, :].rearrange("p (t d) -> p t d", d=D)
                            st(nc.vector.tensor_tensor(x4, x4, W["L1_ln1g"][:, None, :].broadcast_to([P, NT, D]), ALU.mult))
                            nc.vector.tensor_tensor(x4, x4, W["L1_ln1b"][:, None, :].broadcast_to([P, NT, D]), ALU.add).then_inc(s_xl, 1)
                            dv.wait_ge(s_xl, 1)
                    st.restart()

            def pool(po):
                consts(po)
                for i in turns(po, "gpsimd", B):
                    for r in range(1 + (L == 1)):
                        po.wait_ge(s_var, r + 1)
                        nc.gpsimd.tensor_tensor(rstd[:, :], var[:, :], neghalf[:, 0:NT], ALU.pow).then_inc(s_rstd, 1)
                        if r == 0:
                            po.wait_ge(s_xs, 1)
                            nc.gpsimd.tensor_copy(xn[:, bass.ds(i * (NT * D), NT * D)], xs[:, :]).then_inc(s_xnc, 1)

            def pe(te):
                loaded(te)
                consts(te)
                for i in turns(te, "tensor", B):
                    te.wait_ge(s_xs, 1)
                    for t in range(NT):
                        ins = te.transpose(ps_turn[:, 0, t * P:(t + 1) * P], xs[:, t * D:(t + 1) * D], ident[:, :])
                    ins.then_inc(s_tr, 1)
                    te.wait_ge(s_xsT, 1)
                    for t in range(NT):
                        o = ps_proj[:, 0, t * NE:(t + 1) * NE]
                        te.matmul(o, xsT[:, t * P:(t + 1) * P], W[f"L{L}_gw"][:, :], start=True, stop=False)
                        if L == 1:
                            te.matmul(o, ones[0:1, :], W["L1_eb"][:, :], start=False, stop=False)
                        ins = te.matmul(o, ones[0:1, :], W[f"L{L}_gb"][:, :], start=False, stop=True)
                    ins.then_inc(s_gp, 1)
                    if L == 1:
                        te.wait_ge(s_xl, 1)
                        for t in range(NT):
                            ins = te.transpose(ps_turn[:, 1, t * P:(t + 1) * P], xl[:, t * D:(t + 1) * D], ident[:, :])
                        ins.then_inc(s_tr, 1)

            def act(ac):
                for i in turns(ac, "scalar", B):
                    ac.wait_ge(s_tr, 1)
                    nc.scalar.activation(xsT[:, :], ps_turn[:, 0, :], ACT.Copy).then_inc(s_xsT, 1)
                    nc.scalar.activation(xnT[:, bass.ds(i * T, T)], ps_turn[:, 0, :], ACT.Copy).then_inc(s_xsT, 1)
                    ac.wait_ge(s_gp, 1)
                    nc.scalar.activation(
                        gate[:, :, :].rearrange("p n e -> p (n e)")[:, bass.ds(i * (NT * NE), NT * NE)],
                        ps_proj[:, 0, 0:NT * NE], ACT.Copy).then_inc(s_gate, 1)
                    if L == 1:
                        ac.wait_ge(s_tr, 2)
                        nc.scalar.activation(xlT[:, bass.ds(i * T, T)], ps_turn[:, 1, :], ACT.Copy).then_inc(s_xsT, 1)
            return Phase(vec, act, pool, pe, s_var, s_xl, B)

        def attention_phase(L):
            NG = 1 if L == 0 else 4
            NK = SPLIT + 3 * NG
            KOFF = 64 if L == 0 else 32
            NV = 32 if L == 0 else 128
            srcT = xnT if L == 0 else xlT
            ev = 2 if L == 0 else 2
            s_xT = sem(f"{L}_xT")
            s_qkp = sem(f"{L}_qk_proj")
            s_qk = sem(f"{L}_qk")
            s_vp = sem(f"{L}_v_proj")
            s_v = sem(f"{L}_v")
            s_ms = sem(f"{L}_ms")
            s_rms = sem(f"{L}_rms")
            s_ek = sem(f"{L}_ek")
            s_dup = sem(f"{L}_dup")
            s_eq = sem(f"{L}_eq")
            s_turn = sem(f"{L}_turned")
            s_T = sem(f"{L}_T")
            s_pad = sem(f"{L}_pad")
            s_sc = sem(f"{L}_scores")
            s_th = sem(f"{L}_tanh")
            s_mx = sem(f"{L}_max")
            s_inv = sem(f"{L}_inv")
            s_sin = sem(f"{L}_suminv")
            s_dif = sem(f"{L}_dif")
            s_cof = sem(f"{L}_cof")
            s_st = sem(f"{L}_shifted")
            s_p = sem(f"{L}_probs")
            s_pv = sem(f"{L}_pv")
            s_hd = sem(f"{L}_head")
            s_osb = sem(f"{L}_osb")
            s_hT = sem(f"{L}_headT")
            s_hTs = sem(f"{L}_headTs")
            s_op = sem(f"{L}_oproj")
            s_o = sem(f"{L}_o")

            def natural(ap, g=None):
                return ap

            def pool(po):
                for i in turns(po, "gpsimd", B):
                    nc.gpsimd.tensor_copy(xT[:, 64:64 + T], srcT[:, bass.ds(i * T, T)]).then_inc(s_xT, 1)
                    nc.gpsimd.tensor_copy(xT[:, 0:64], srcT[:, bass.ds(i * T + T - 64, 64)]).then_inc(s_xT, 1)
                    nc.gpsimd.tensor_copy(xT[:, 64 + T:128 + T], srcT[:, bass.ds(i * T, 64)]).then_inc(s_xT, 1)
                    if L == 0:
                        po.wait_ge(s_ms, 1)
                        nc.gpsimd.tensor_tensor(rr[:, :, :], ss[:, :, :], neghalf[:, 0:128].rearrange(
                            "p (a b) -> p a b", a=2), ALU.pow).then_inc(s_rms, 1)
                    po.wait_ge(s_ek, 1)
                    ekv = ek[:, :, :, :].rearrange("p t h r -> p (t h) r")
                    nc.gpsimd.tensor_copy(ekv[:, :, 24:40], ekv[:, :, 0:16]).then_inc(s_dup, 1)
                    nc.gpsimd.tensor_copy(ekv[:, :, 40:48], ekv[:, :, 0:8]).then_inc(s_dup, 1)
                    po.wait_ge(s_T, NT)
                    nc.gpsimd.tensor_copy(kT[:, :, 0:64], kT[:, :, T:T + 64]).then_inc(s_pad, 1)
                    nc.gpsimd.tensor_copy(kT[:, :, 64 + T:128 + T], kT[:, :, 64:128]).then_inc(s_pad, 1)

            def vec(dv):
                st = Steps(dv, dve_chain)
                ekv = ek[:, :, :, :].rearrange("p t h r -> p (t h) r")
                eqv = eq[:, :, :, :].rearrange("p t h r -> p (t h) r")
                vv = v[:, :, 0:H * 36].rearrange("p u (h g e) -> p u h g e", g=4, e=9)
                if L == 0:
                    consts(dv)
                    st(nc.vector.memset(ekv[:, :, SPLIT:SPLIT + 3], 1.0))
                    st(nc.vector.memset(v[:, :, 0:36].rearrange("p u (h e) -> p u h e", e=9)[:, :, :, 8], 1.0))
                    st(nc.vector.tensor_scalar(rmsw[:, 0, :], W["L0_rms"][:, 0:8], float(1 / np.sqrt(np.float32(HD))), None, ALU.mult))
                    st(nc.vector.tensor_copy(rmsw[:, 1, :], W["L0_rms"][:, 8:16]))
                else:
                    for s in range(3):
                        st(nc.vector.tensor_copy(ekv[:, :, SPLIT + 4 * s:SPLIT + 4 * s + 4],
                                                 tab_mod[:, None, :].broadcast_to([P, NT * H, 4])))
                    for u in range(NU):
                        st(nc.vector.tensor_copy(vv[:, u, :, :, 8], tab_bd[:, None, :].broadcast_to([P, H, 4])))
                st.restart()

                def split_q(st, i, n):
                    st(nc.vector.tensor_copy(eqv[:, :, 0:24].rearrange("p h (c e) -> p h c e", c=3),
                                             q4[:, :, None, :].broadcast_to([P, NT * H, 3, HD])))
                    st(nc.vector.tensor_tensor(rest[:, :, :], q4[:, :, :], eqv[:, :, 0:8], ALU.subtract))
                    st(nc.vector.tensor_copy(eqv[:, :, 24:40].rearrange("p h (c e) -> p h c e", c=2),
                                             rest[:, :, None, :].broadcast_to([P, NT * H, 2, HD])))
                    nc.vector.tensor_tensor(eqv[:, :, 40:48], rest[:, :, :], eqv[:, :, 24:32], ALU.subtract).then_inc(s_eq, 1)
                    dv.wait_ge(s_eq, n)

                for i in turns(dv, "vector", B):
                    for c in range(2):
                        dv.wait_ge(s_vp, c + 1)
                        if L == 0:
                            nc.vector.tensor_copy(
                                v[:, 4 * c:4 * c + 4, 0:36].rearrange("p u (h e) -> p u h e", e=9)[:, :, :, 0:8],
                                ps_proj[:, c, 0:128].rearrange("p (u h e) -> p u h e", u=4, e=8)).then_inc(s_v, 1)
                        else:
                            for u in range(4):
                                o = ps_proj[:, c, u * 128:(u + 1) * 128].rearrange("p (h e) -> p h e", e=8)
                                for g in range(4):
                                    ins = nc.vector.tensor_scalar(vv[:, 4 * c + u, :, g, 0:8], o, tab_bd[:, g:g + 1],
                                                                  None, ALU.mult)
                            ins.then_inc(s_v, 1)
                    dv.wait_ge(s_qk, 2 * NT)
                    if L == 0:
                        for z, m in ((q4, 0), (k4, 1)):
                            st(nc.vector.tensor_tensor(sq[:, :, :], z[:, :, :], z[:, :, :], ALU.mult))
                            st(nc.vector.tensor_reduce(ss[:, m, :], sq[:, :, :], AX.X, ALU.add))
                        nc.vector.tensor_scalar(ss[:, :, :], ss[:, :, :], 1.0 / HD, RMS_EPS, ALU.mult, ALU.add).then_inc(s_ms, 1)
                        dv.wait_ge(s_rms, 1)
                        for z, m in ((q4, 0), (k4, 1)):
                            st(nc.vector.tensor_tensor(z[:, :, :], z[:, :, :], rr[:, m, :, None].broadcast_to([P, NT * H, HD]), ALU.mult))
                            st(nc.vector.tensor_tensor(z[:, :, :], z[:, :, :], rmsw[:, m:m + 1, :].broadcast_to([P, NT * H, HD]), ALU.mult))
                    else:
                        st(nc.vector.tensor_scalar(q4[:, :, :], q4[:, :, :], float(HD) ** -0.5, None, ALU.mult))
                    st(nc.vector.tensor_copy(ekv[:, :, 0:8], k4[:, :, :]))
                    st(nc.vector.tensor_tensor(rest[:, :, :], k4[:, :, :], ekv[:, :, 0:8], ALU.subtract))
                    st(nc.vector.tensor_copy(ekv[:, :, 8:16], rest[:, :, :]))
                    nc.vector.tensor_tensor(ekv[:, :, 16:24], rest[:, :, :], ekv[:, :, 8:16], ALU.subtract).then_inc(s_ek, 1)
                    split_q(st, i, 1)
                    for t in range(NT):
                        for hf in range(2):
                            n = 2 * t + hf
                            src = ps_score[:, n % 2, :]
                            if L == 0:
                                dv.wait_ge(s_th, n + 1)
                                st(nc.vector.tensor_reduce(tsum[:, t, 8 * hf:8 * hf + 8],
                                                           th[:, n % 2, :].rearrange("p (h k) -> p h k", k=128), AX.X, ALU.add))
                                nc.vector.tensor_reduce(gm[:, t, 8 * hf:8 * hf + 8],
                                                                src.rearrange("p (h k) -> p h k", k=128), AX.X, ALU.max).then_inc(s_mx, 1)
                            else:
                                dv.wait_ge(s_sc, n + 1)
                                nc.vector.tensor_reduce(gm[:, t, 32 * hf:32 * hf + 32],
                                                                src.rearrange("p (h k) -> p h k", k=32), AX.X, ALU.max).then_inc(s_mx, 1)
                    dv.wait_ge(s_mx, 2 * NT)
                    if L == 0:
                        for t in range(NT):
                            st(nc.vector.tensor_scalar(inv[:, t, :], tsum[:, t, :], tab_nm[:, t:t + 1], 1.0 / (2 * T), ALU.add, ALU.mult))
                        st(nc.vector.tensor_scalar(inv[:, :, :], inv[:, :, :], 1.0, None, ALU.add))
                        nc.vector.reciprocal(inv[:, :, :], inv[:, :, :]).then_inc(s_inv, 1)
                        dv.wait_ge(s_sin, 1)
                        st(nc.vector.tensor_reduce(sinv[:, :], ps_proj[:, 0, 0:NT * H].rearrange("p (t h) -> p h t", h=H), AX.X, ALU.add))
                        st(nc.vector.reciprocal(sinv[:, :], sinv[:, :]))
                        st(nc.vector.tensor_tensor(fit[:, :, :], inv[:, :, :], sinv[:, None, :].broadcast_to([P, NT, H]), ALU.mult))
                        st(nc.vector.scalar_tensor_tensor(out=shift[:, :, 0:H], in0=gm[:, :, 0:H], scalar=-1.0, in1=fit[:, :, :],
                                                          op0=ALU.mult, op1=ALU.mult))
                        for par in range(2):
                            st(nc.vector.tensor_copy(
                                fits[:, :, :].rearrange("p t (f j a) -> p (t f) j a", f=2, a=2)[:, :, :, par],
                                fit[:, :, :].rearrange("p t (f a j) -> p (t f) a j", f=2, a=2)[:, :, par, :]))
                            st(nc.vector.tensor_copy(
                                shifts[:, :, 0:H].rearrange("p t (f j a) -> p t f j a", f=2, a=2)[:, :, :, :, par],
                                shift[:, :, 0:H].rearrange("p t (f a j) -> p t f a j", f=2, a=2)[:, :, :, par, :]))
                        st(nc.vector.tensor_tensor(q4[:, :, :], q4[:, :, :], fits[:, :, :].rearrange("p t h -> p (t h)")[:, :, None].broadcast_to([P, NT * H, HD]), ALU.mult))
                        rows = [shifts[:, :, 0:H]]
                    else:
                        g3 = gm[:, :, :].rearrange("p t (h g) -> p (t h) g", g=4)
                        for n, (e_, nm) in enumerate(((eA, tab_nA), (eB, tab_nB))):
                            e3 = e_[:, :, :, :].rearrange("p t h g -> p (t h) g")
                            st(nc.vector.tensor_tensor(e3, g3, nm[:, None, :].broadcast_to([P, NT * H, 4]), ALU.add))
                            st(nc.vector.tensor_reduce(mA[:, :], e3, AX.X, ALU.max))
                            nc.vector.tensor_tensor(e3, e3, mA[:, :, None].broadcast_to([P, NT * H, 4]), ALU.subtract).then_inc(s_dif, 1)
                            dv.wait_ge(s_dif, n + 1)
                        for par in range(2):
                            for f in range(2):
                                for blk, base in ((0, 3), (1, 1)):
                                    sp_ = slice(64 * blk, 64 * blk + 64)
                                    dst = shifts[sp_, :, :].rearrange("p t (f j a g) -> p t f j a g", f=2, a=2, g=4)[:, :, f, :, par, :]
                                    src = gm[sp_, :, :].rearrange("p t (f a j g) -> p t f a j g", f=2, a=2, g=4)[:, :, f, par, :, :]
                                    k = 4 - base
                                    st(nc.vector.tensor_scalar(dst[:, :, :, base:4], src[:, :, :, 0:k], -1.0, None, ALU.mult))
                                    st(nc.vector.tensor_scalar(dst[:, :, :, 0:base], src[:, :, :, k:4], -1.0, None, ALU.mult))
                    sh = shifts[:, :, 0:H * NG].rearrange("p t (h g) -> p t h g", g=NG)
                    r3 = shr[:, :, 0:H * NG].rearrange("p t (h g) -> p t h g", g=NG)
                    part = [eq[:, :, :, SPLIT + NG * s:SPLIT + NG * (s + 1)] for s in range(3)]
                    dv.wait_ge(s_turn, 2 * NT)
                    st(nc.vector.tensor_copy(part[0], sh))
                    st(nc.vector.tensor_tensor(r3, sh, part[0], ALU.subtract))
                    st(nc.vector.tensor_copy(part[1], r3))
                    st(nc.vector.tensor_tensor(part[2], r3, part[1], ALU.subtract))
                    split_q(st, i, 2)
                    for t in range(NT):
                        dv.wait_ge(s_pv, 2 * t + 2)
                        if L == 0:
                            o = ps_turn[:, 0, 0:H * 9].rearrange("p (h e) -> p h e", e=9)
                            st(nc.vector.reciprocal(wtot[:, :], o[:, :, 8]))
                            if t > 0:
                                dv.wait_ge(s_hT, t)
                            nc.vector.tensor_tensor(head[:, :].rearrange("p (h e) -> p h e", e=8), o[:, :, 0:8],
                                                            wtot[:, :, None].broadcast_to([P, H, 8]), ALU.mult).then_inc(s_hd, 1)
                        else:
                            if t == 0:
                                dv.wait_ge(s_cof, 2)
                            st(nc.vector.tensor_copy(osb[:, 0:288], ps_turn[:, 0, 0:288]))
                            nc.vector.tensor_copy(osb[:, 288:576], ps_turn[:, 1, 0:288]).then_inc(s_osb, 1)
                            dv.wait_ge(s_osb, t + 1)
                            o = osb[:, :].rearrange("p (h g e) -> p h g e", g=4, e=9)
                            for n, (e_, al, c_, w_) in enumerate(((eA, tab_al1, cs, wtot), (eB, tab_al, cs2, wtot2))):
                                st(nc.vector.tensor_tensor(c_[:, :, :], e_[:, t, :, :], o[:, :, :, 8], ALU.mult))
                                st(nc.vector.tensor_reduce(w_[:, :], c_[:, :, :], AX.X, ALU.add))
                                st(nc.vector.reciprocal(w_[:, :], w_[:, :]))
                                st(nc.vector.tensor_scalar(w_[:, :], w_[:, :], al[:, t:t + 1], None, ALU.mult))
                                st(nc.vector.tensor_tensor(c_[:, :, :], e_[:, t, :, :], w_[:, :, None].broadcast_to([P, H, 4]), ALU.mult))
                            st(nc.vector.tensor_tensor(cs[:, :, :], cs[:, :, :], cs2[:, :, :], ALU.add))
                            st(nc.vector.tensor_tensor(wpv[:, :, :, :].rearrange("p h e g -> p h g e"), o[:, :, :, 0:8],
                                                       cs[:, :, :, None].broadcast_to([P, H, 4, 8]), ALU.mult))
                            if t > 0:
                                dv.wait_ge(s_hT, t)
                            nc.vector.tensor_reduce(head[:, :], wpv[:, :, :, :].rearrange("p h e g -> p (h e) g"), AX.X, ALU.add).then_inc(s_hd, 1)
                        dv.wait_ge(s_hd, t + 1)
                    st.restart()

            def pe(te):
                for i in turns(te, "tensor", B):
                    te.wait_ge(s_xT, 3)
                    for c in range(2):
                        for u in range(4):
                            p0 = 64 + 64 * (4 * c + u) - KOFF
                            o = ps_proj[:, c, u * NV:(u + 1) * NV]
                            te.matmul(o, xT[:, p0:p0 + P], W[f"L{L}_wv"][:, :], start=True, stop=False)
                            ins = te.matmul(o, ones[0:1, :], W[f"L{L}_bv"][:, :], start=False, stop=True)
                        ins.then_inc(s_vp, 1)
                    for t in range(NT):
                        if t < 2:
                            te.wait_ge(s_v, t + 1)
                        else:
                            te.wait_ge(s_qk, 2 * (t - 1))
                        o = ps_proj[:, t % 2, 0:256]
                        te.matmul(o, xT[:, 64 + t * P:64 + (t + 1) * P], W[f"L{L}_wqk"][:, :], start=True, stop=False)
                        te.matmul(o, ones[0:1, :], W[f"L{L}_bqk"][:, :], start=False, stop=True).then_inc(s_qkp, 1)

                    def turn(src, n, t):
                        if n >= 2:
                            te.wait_ge(s_T, n - 1)
                        dst = ps_turn[:, n % 2, :].bitcast(BF16)
                        for pr in range(8):
                            ins = te.transpose(dst[:, pr * P:(pr + 1) * P],
                                               src[:, t, 2 * pr:2 * pr + 2, :].rearrange("p h r -> p (h r)"), identb[:, :])
                        ins.then_inc(s_turn, 1)

                    te.wait_ge(s_dup, 2)
                    for t in range(NT):
                        turn(ek, t, t)
                    te.wait_ge(s_eq, 1)
                    for t in range(NT):
                        turn(eq, NT + t, t)
                    te.wait_ge(s_pad, 2)
                    te.wait_ge(s_T, 2 * NT)
                    for t in range(NT):
                        for hf in range(2):
                            n = 2 * t + hf
                            if n >= 2:
                                te.wait_ge(s_mx, n - 1)
                            bank = [ps_score[:, n % 2, 512 * par:512 * par + 512] for par in range(2)]
                            m = {0: {0: 0, 1: 1, 2: 1, 3: 1}, 1: {0: 2, 3: 3}}[L].get(t)
                            if m is not None:
                                for par in range(2):
                                    te.matmul(bank[par], identb[:, :], maskq[:, m, :], start=True, stop=False, skip_group_check=True)
                            for blk in range(2):
                                for j in range(4):
                                    for par in range(2):
                                        q0 = t * P + 64 * blk
                                        ins = te.matmul(bank[par][64 * blk:64 * blk + 64, j * P:(j + 1) * P],
                                                        qT[64 * par:64 * par + SPLIT, 4 * hf + j, q0:q0 + 64],
                                                        kT[64 * par:64 * par + SPLIT, 4 * hf + j, 64 + q0 - KOFF:64 + q0 - KOFF + P],
                                                        start=m is None, stop=True, skip_group_check=True)
                            ins.then_inc(s_sc, 1)
                    if L == 0:
                        te.wait_ge(s_inv, 1)
                        te.matmul(ps_proj[:, 0, 0:NT * H], ones[:, :], inv[:, :, :].rearrange("p t h -> p (t h)"), start=True, stop=True).then_inc(s_sin, 1)
                    te.wait_ge(s_eq, 2)
                    for t in range(NT):
                        turn(eq, 2 * NT + t, t)
                    te.wait_ge(s_T, 3 * NT)
                    te.wait_ge(s_mx, 2 * NT)

                    def probs(u):
                        if u >= 2:
                            te.wait_ge(s_p, u - 1)
                        bank = [ps_score[:, u % 2, 512 * par:512 * par + 512] for par in range(2)]
                        m = ({0: 0, 1: 1} if L == 0 else {0: 3, NU - 1: 4}).get(u, 2 if L == 0 else None)
                        if m is not None:
                            for par in range(2):
                                te.matmul(bank[par], identb[:, :], maskk[:, m, :], start=True, stop=False, skip_group_check=True)
                        for pr in range(8):
                            for par in range(2):
                                k0 = 64 + 64 * u - KOFF
                                ins = te.matmul(bank[par][:, pr * 64:pr * 64 + 64],
                                                kT[64 * par:64 * par + NK, pr, k0:k0 + P],
                                                qT[64 * par:64 * par + NK, pr, 64 * u:64 * u + 64],
                                                start=m is None, stop=True, skip_group_check=True)
                        ins.then_inc(s_st, 1)

                    def weigh(u):
                        te.wait_ge(s_p, u + 1)
                        t, blk = u // 2, u % 2
                        if blk == 0 and t >= 1:
                            if t > 0:
                                te.wait_ge((s_hd if L == 0 else s_osb), t)
                        for h in range(H):
                            hf, par, j = h // 8, h // 4 % 2, h % 4
                            w_ = pT[:, u % 2, par * 512 + (4 * hf + j) * 64:par * 512 + (4 * hf + j) * 64 + 64]
                            if L == 0:
                                o = ps_turn[64 * blk:64 * blk + 64, 0, 9 * h:9 * h + 9]
                                r = v[:, u, 9 * (h // 4):9 * (h // 4) + 9]
                            else:
                                o = ps_turn[64 * blk:64 * blk + 64, hf, 36 * (h % 8):36 * (h % 8) + 36]
                                r = v[:, u, 36 * h:36 * h + 36]
                            ins = te.matmul(o, w_, r, start=True, stop=True)
                        ins.then_inc(s_pv, 1)

                    def project(t):
                        te.wait_ge(s_hd, t + 1)
                        if t >= 1:
                            if t > 0:
                                te.wait_ge(s_o, t)
                        te_ins = te.transpose(ps_proj[:, 0, 0:P], head[:, :], ident[:, :])
                        te_ins.then_inc(s_hT, 1)
                        te.wait_ge(s_hTs, t + 1)
                        te.matmul(ps_proj[:, 1, 0:D], headT[:, :], W[f"L{L}_wo"][:, :], start=True, stop=False)
                        te.matmul(ps_proj[:, 1, 0:D], ones[0:1, :], W[f"L{L}_bo"][:, :], start=False, stop=True).then_inc(s_op, 1)

                    probs(0)
                    for u in range(NU):
                        if u + 1 < NU:
                            probs(u + 1)
                        if u == 0:
                            te.wait_ge(s_v, 2)
                        weigh(u)
                        if u % 2 == 1 and u >= 3:
                            project(u // 2 - 1)
                    project(NT - 1)

            def act(ac):
                for i in turns(ac, "scalar", B):
                    for t in range(NT):
                        ac.wait_ge(s_qkp, t + 1)
                        nc.scalar.activation(q4[:, t * H:(t + 1) * H, :].rearrange("p h e -> p (h e)"), ps_proj[:, t % 2, 0:128], ACT.Copy).then_inc(s_qk, 1)
                        nc.scalar.activation(k4[:, t * H:(t + 1) * H, :].rearrange("p h e -> p (h e)"), ps_proj[:, t % 2, 128:256], ACT.Copy).then_inc(s_qk, 1)

                    def keep(n, dst):
                        ac.wait_ge(s_turn, n + 1)
                        nc.scalar.activation(dst, ps_turn[:, n % 2, :].bitcast(BF16).rearrange("p (r k) -> p r k", k=P), ACT.Copy).then_inc(s_T, 1)

                    for t in range(NT):
                        keep(t, kT[:, :, 64 + t * P:64 + (t + 1) * P])
                    for t in range(NT):
                        keep(NT + t, qT[:, :, t * P:(t + 1) * P])
                    if L == 0:
                        for n in range(2 * NT):
                            ac.wait_ge(s_sc, n + 1)
                            if n - 1 > 0:
                                ac.wait_ge(s_mx, n - 1)
                            nc.scalar.activation(th[:, n % 2, :], ps_score[:, n % 2, :], ACT.Tanh, scale=0.5).then_inc(s_th, 1)
                    else:
                        for n, e_ in enumerate((eA, eB)):
                            ac.wait_ge(s_dif, n + 1)
                            nc.scalar.activation(e_[:, :, :, :], e_[:, :, :, :], ACT.Exp).then_inc(s_cof, 1)
                    for t in range(NT):
                        keep(2 * NT + t, qT[:, :, t * P:(t + 1) * P])

                    def finish(t):
                        ac.wait_ge(s_hT, t + 1)
                        if t > 0:
                            ac.wait_ge(s_op, t)
                        nc.scalar.activation(headT[:, :], ps_proj[:, 0, 0:P], ACT.Copy).then_inc(s_hTs, 1)
                        ac.wait_ge(s_op, t + 1)
                        nc.scalar.activation(s_out[:, bass.ds((i * NT + t) * D, D)], ps_proj[:, 1, 0:D], ACT.Copy).then_inc(s_o, 1)

                    for u in range(NU):
                        ac.wait_ge(s_st, u + 1)
                        if u - 1 > 0:
                            ac.wait_ge(s_pv, u - 1)
                        nc.scalar.activation(pT[:, u % 2, :], ps_score[:, u % 2, :], ACT.Exp).then_inc(s_p, 1)
                        if u % 2 == 0 and u >= 4:
                            finish(u // 2 - 2)
                    finish(NT - 2)
                    finish(NT - 1)
            return Phase(vec, act, pool, pe, s_xT, s_o, B)

        def mlp_phase():
            s_var = sem("m_var")
            s_rstd = sem("m_rstd")
            s_h = sem("m_h")
            s_tr = sem("m_tr")
            s_hT = sem("m_hT")
            s_up = sem("m_up")
            s_act = sem("m_act")
            s_dn = sem("m_dn")
            s_out_ = sem("m_out")
            hx = sb("hx", [P, D])
            hxT = sb("hxT", [P, P])

            def vec(dv):
                st = Steps(dv, dve_chain)
                for i in turns(dv, "vector", B):
                    for t in range(NT):
                        at = bass.ds((i * NT + t) * D, D)
                        st(nc.vector.tensor_tensor(s_out[:, at], s_out[:, at], xn[:, at], ALU.add))
                        st(nc.vector.bn_stats(stats[:, 0, :], s_out[:, at]))
                        st(nc.vector.bn_aggr(mv[:, 0, :], stats[:, 0, :]))
                        nc.vector.tensor_scalar(var[:, 0:1], mv[:, 0, 1:2], LN_EPS, None, ALU.add).then_inc(s_var, 1)
                        dv.wait_ge(s_rstd, t + 1)
                        if t > 0:
                            dv.wait_ge(s_tr, t)
                        st(nc.vector.tensor_scalar(hx[:, :], s_out[:, at], mv[:, 0, 0:1], rstd[:, 0:1], ALU.subtract, ALU.mult))
                        st(nc.vector.tensor_tensor(hx[:, :], hx[:, :], W["L1_ln2g"][:, :], ALU.mult))
                        nc.vector.tensor_tensor(hx[:, :], hx[:, :], W["L1_ln2b"][:, :], ALU.add).then_inc(s_h, 1)
                        dv.wait_ge(s_h, t + 1)
                        dv.wait_ge(s_dn, t + 1)
                        nc.vector.tensor_tensor(s_out[:, at], s_out[:, at], ps_proj[:, 1, 0:D], ALU.add).then_inc(s_out_, 1)
                        dv.wait_ge(s_out_, t + 1)
                    st.restart()

            def pool(po):
                for i in turns(po, "gpsimd", B):
                    for t in range(NT):
                        po.wait_ge(s_var, t + 1)
                        nc.gpsimd.tensor_tensor(rstd[:, 0:1], var[:, 0:1], neghalf[:, 0:1], ALU.pow).then_inc(s_rstd, 1)

            def pe(te):
                for i in turns(te, "tensor", B):
                    for t in range(NT):
                        te.wait_ge(s_h, t + 1)
                        te.transpose(ps_proj[:, 0, 0:P], hx[:, :], ident[:, :]).then_inc(s_tr, 1)
                        te.wait_ge(s_hT, t + 1)
                        for c in range(FC):
                            o = ps_turn[:, 0, c * P:(c + 1) * P]
                            ins = te.matmul(o, W["L1_mw1"][:, c * P:(c + 1) * P], hxT[:, :], start=True, stop=True)
                        ins.then_inc(s_up, 1)
                        te.wait_ge(s_act, t + 1)
                        for c in range(FC):
                            te.matmul(ps_proj[:, 1, 0:D], hT[:, 0, c * P:(c + 1) * P], W["L1_mw2"][:, c, :], start=(c == 0), stop=False)
                        te.matmul(ps_proj[:, 1, 0:D], ones[0:1, :], W["L1_mb2"][:, :], start=False, stop=True).then_inc(s_dn, 1)

            def act(ac):
                st = Steps(ac, act_chain)
                for i in turns(ac, "scalar", B):
                    for t in range(NT):
                        ac.wait_ge(s_tr, t + 1)
                        nc.scalar.activation(hxT[:, :], ps_proj[:, 0, 0:P], ACT.Copy).then_inc(s_hT, 1)
                        ac.wait_ge(s_up, t + 1)
                        for c in range(FC):
                            ins = nc.scalar.activation(hT[:, 0, c * P:(c + 1) * P], ps_turn[:, 0, c * P:(c + 1) * P], ACT.Gelu,
                                                       bias=W["L1_mb1"][:, c:c + 1])
                        ins.then_inc(s_act, 1)
            return Phase(vec, act, pool, pe, s_var, s_out_, B)

        def moe_phase(L):
            s_w = [sem(f"e{L}_w{e}") for e in range(2)]
            s_up = sem(f"e{L}_up")
            s_h = sem(f"e{L}_h")
            s_y = sem(f"e{L}_y")
            s_acc = sem(f"e{L}_acc")
            e_w1, e_w2, e_b2 = a[f"L{L}_w1e"], a[f"L{L}_w2e"], a[f"L{L}_b2e"]

            def vec(dv):
                st = Steps(dv, dve_chain)

                def first_best(dst, src):
                    st(nc.vector.tensor_reduce(best[:, :], src, AX.X, ALU.max))
                    st(nc.vector.tensor_tensor(pick8[:, :, :], src, best[:, :, None].broadcast_to([P, NTT, NE]), ALU.is_equal))
                    st(nc.vector.tensor_scalar(pick8[:, :, :], pick8[:, :, :], -100.0, 100.0, ALU.mult, ALU.add))
                    st(nc.vector.tensor_tensor(pick8[:, :, :], pick8[:, :, :], iota8[:, :, :], ALU.add))
                    st(nc.vector.tensor_reduce(dst[:, :], pick8[:, :, :], AX.X, ALU.min))

                def onehot(dst, src):
                    st(nc.vector.tensor_tensor(dst[:, :, :], iota8[:, :, :], src[:, :, None].broadcast_to([P, NTT, NE]), ALU.is_equal))

                first_best(pickA, gate[:, :, :])
                if L == 0:
                    onehot(pick8b, pickA)
                    st(nc.vector.tensor_scalar(pick8b[:, :, :], pick8b[:, :, :], -3e38, None, ALU.mult))
                    st(nc.vector.tensor_tensor(pick8b[:, :, :], pick8b[:, :, :], gate[:, :, :], ALU.add))
                    first_best(pickB, pick8b[:, :, :])
                    st(nc.vector.tensor_tensor(pickA[:, :], pickA[:, :], pickB[:, :], ALU.max))
                onehot(pick8b, pickA)
                st(nc.vector.memset(moe[:, :], 0.0))
                st(nc.vector.tensor_copy(pick8[:, :, :].rearrange("p n e -> p (n e)").rearrange("p (e n) -> p e n", e=NE),
                                         pick8b[:, :, :].rearrange("p n e -> p e n")))
                pe8 = pick8[:, :, :].rearrange("p n e -> p (n e)")
                st.restart()
                for i in turns(dv, "vector", NE // 2):
                    for e in range(2):
                        for c in range(4):
                            dv.wait_ge(s_y, 4 * e + c + 1)
                            for t in range(4):
                                tt = 4 * c + t
                                ins = nc.vector.scalar_tensor_tensor(
                                    out=moe[:, tt * D:(tt + 1) * D], in0=ps_turn[:, c % 2, t * D:(t + 1) * D],
                                    scalar=pe8[:, bass.ds((i * 2 + e) * NTT + tt, 1)], in1=moe[:, tt * D:(tt + 1) * D],
                                    op0=ALU.mult, op1=ALU.add)
                            ins.then_inc(s_acc, 1)
                            dv.wait_ge(s_acc, 4 * e + c + 1)
                    st.restart()


            def sync(sp, i):
                if True:
                    for e in range(2):
                        ex = i * 2 + e
                        sp.dma_start(w1[:, e, :], e_w1[bass.ds(ex * P, P), :]).then_inc(s_w[e], 16)
                        sp.dma_start(w2[:, e, :].rearrange("p (c n) -> p c n", c=FC),
                                            e_w2[bass.ds(ex * DF, DF), :].rearrange("(c p) n -> p c n", p=P)).then_inc(s_w[e], 16)
                        sp.dma_start(b2r[:, e, :], e_b2[bass.ds(ex, 1), :]).then_inc(s_w[e], 16)

            def pe(te):
                for i in turns(te, "tensor", NE // 2):
                    for e in range(2):
                        te.wait_ge(s_w[e], 48)

                        def up(c, f):
                            n = (4 * e + c) * FC + f
                            if n >= 4:
                                te.wait_ge(s_h, n - 3)
                            te.matmul(ps_score[:, (n % 4) // 2, (n % 2) * 512:(n % 2) * 512 + 512],
                                              w1[:, e, f * P:(f + 1) * P], xnT[:, c * 512:(c + 1) * 512], start=True, stop=True).then_inc(s_up, 1)

                        def down(c):
                            te.wait_ge(s_h, (4 * e + c) * FC + FC)
                            if 4 * e + c - 1 > 0:
                                te.wait_ge(s_acc, 4 * e + c - 1)
                            for t in range(4):
                                o = ps_turn[:, c % 2, t * D:(t + 1) * D]
                                for f in range(FC):
                                    te.matmul(o, hT[:, c % 2, f * 512 + t * P:f * 512 + (t + 1) * P],
                                              w2[:, e, f * D:(f + 1) * D], start=(f == 0), stop=False)
                                ins = te.matmul(o, ones[0:1, :], b2r[:, e, :], start=False, stop=True)
                            ins.then_inc(s_y, 1)

                        for c in range(4):
                            for f in range(FC):
                                up(c, f)
                            if c >= 1:
                                down(c - 1)
                        down(3)

            def act(ac):
                for i in turns(ac, "scalar", NE // 2):
                    for e in range(2):
                        for c in range(4):
                            if 4 * e + c - 1 > 0:
                                ac.wait_ge(s_y, 4 * e + c - 1)
                            for f in range(FC):
                                n = (4 * e + c) * FC + f
                                ac.wait_ge(s_up, n + 1)
                                nc.scalar.activation(hT[:, c % 2, f * 512:(f + 1) * 512],
                                                            ps_score[:, (n % 4) // 2, (n % 2) * 512:(n % 2) * 512 + 512],
                                                            ACT.Gelu if L == 0 else ACT.Relu,
                                                            bias=W[f"L{L}_b1e"][:, bass.ds((i * 2 + e) * FC + f, 1)]).then_inc(s_h, 1)
            def pool(po):
                for _ in turns(po, "gpsimd", NE // 2):
                    pass
            return Phase(vec, act, pool, pe, s_w[0], s_acc, NE // 2, sync)

        def join_phase(L):
            s_e = sem(f"j{L}_e")
            s_x = sem(f"j{L}_x")
            k = 2.0 if L == 0 else 1.0

            def act(ac):
                nc.scalar.activation(xnT[:, :], moe[:, :], ACT.Exp, scale=-k).then_inc(s_e, 1)

            def vec(dv):
                st = Steps(dv, dve_chain)
                dv.wait_ge(s_e, 1)
                st(nc.vector.tensor_scalar(xnT[:, :], xnT[:, :], 1.0, None, ALU.add))
                st(nc.vector.reciprocal(xnT[:, :], xnT[:, :]))
                st(nc.vector.scalar_tensor_tensor(out=moe[:, :], in0=moe[:, :], scalar=k, in1=xnT[:, :], op0=ALU.mult, op1=ALU.mult))
                st(nc.vector.tensor_tensor(moe[:, :], moe[:, :], s_out[:, :], ALU.mult))
                nc.vector.tensor_tensor(x[:, :], x[:, :], moe[:, :], ALU.add).then_inc(s_x, 1)
                dv.wait_ge(s_x, 1)
                st.restart()
            return act, vec, s_x

        norm0, attn0, moe0 = norm_phase(0, None), attention_phase(0), moe_phase(0)
        join0_act, join0_vec, joined0 = join_phase(0)
        norm1, attn1, mlp1, moe1 = norm_phase(1, joined0), attention_phase(1), mlp_phase(), moe_phase(1)
        join1_act, join1_vec, joined1 = join_phase(1)
        stored = sem("stored")

        @block.sync
        def _(sp):
            sync_load(sp)
            for ph in (norm0, attn0, moe0, norm1, attn1, mlp1, moe1):
                with sp.Fori(0, ph.n) as i:
                    if ph.sync is not None:
                        ph.sync(sp, i)
                    clear_when_met(sp, ph.first, ph.last)
            sp.wait_ge(joined1, 1)
            sp.dma_start(out3, x[:, :].rearrange("p (n d) -> p n d", d=D)).then_inc(stored, 16)
            sp.wait_ge(stored, 16)

        @block.vector
        def _(dv):
            norm0.vec(dv)
            attn0.vec(dv)
            moe0.vec(dv)
            join0_vec(dv)
            norm1.vec(dv)
            attn1.vec(dv)
            mlp1.vec(dv)
            moe1.vec(dv)
            join1_vec(dv)

        @block.scalar
        def _(ac):
            norm0.act(ac)
            attn0.act(ac)
            moe0.act(ac)
            join0_act(ac)
            norm1.act(ac)
            attn1.act(ac)
            mlp1.act(ac)
            moe1.act(ac)
            join1_act(ac)

        @block.gpsimd
        def _(po):
            pool_const(po)
            norm0.pool(po)
            attn0.pool(po)
            moe0.pool(po)
            norm1.pool(po)
            attn1.pool(po)
            mlp1.pool(po)
            moe1.pool(po)

        @block.tensor
        def _(te):
            norm0.pe(te)
            attn0.pe(te)
            moe0.pe(te)
            norm1.pe(te)
            attn1.pe(te)
            mlp1.pe(te)
            moe1.pe(te)


def bf16_bits(m):
    return (m.astype(np.float32).view(np.uint32) >> 16).astype(np.uint16)


def shape_constants():
    pos = np.arange(T)
    tok = (pos - ROT) % T
    c = {}
    c["ident"] = np.eye(P, dtype=np.float32)
    c["identb"] = bf16_bits(np.eye(P))
    c["iota8"] = np.broadcast_to(np.arange(NE, dtype=np.float32), (P, NTT, NE)).copy()

    def causal(u):
        q, k = 64 * u + np.arange(64), (64 * u - 64 + np.arange(P)) % T
        tq, tk = tok[q][:, None], tok[k][None, :]
        return (tk <= tq) & (tk >= tq - WIN)

    def sided(u):
        q, k = 64 * u + np.arange(64), (64 * u - 32 + np.arange(P)) % T
        end_q = (q < ROT) | (q >= T - 32)
        bad = (k[None, :] < 32) & ((k[None, :] < ROT) != end_q[:, None])
        near = (q < 64) | (q >= T - 32)
        return ~(bad & near[:, None])

    def pair(f, t):
        return np.concatenate([f(2 * t), f(2 * t + 1)])

    def penal(m, n):
        return bf16_bits(np.tile(np.where(m, 0.0, -BIG), (1, n)))

    c["maskq"] = np.stack([penal(pair(causal, 0), 4), penal(pair(causal, 1), 4),
                           penal(pair(sided, 0), 4), penal(pair(sided, 3), 4)], 1)
    c["maskk"] = np.stack([penal(causal(0).T, 8), penal(causal(1).T, 8), penal(causal(2).T, 8),
                           penal(sided(0).T, 8), penal(sided(NU - 1).T, 8)], 1)
    tab = np.zeros((P, 64), np.float32)
    al = np.linspace(0.0, 1.0, 32, dtype=np.float32)
    p = np.arange(P)
    for t in range(NT):
        tab[:, t] = (~pair(causal, t)).sum(1)
        alpha = al[p % 32].copy()
        if t == 0:
            alpha[:ROT], alpha[ROT:32] = 0.0, 1.0
        tab[:, 4 + t] = alpha
        tab[:, 8 + t] = 1 - alpha
    odd = (p // 32) % 2
    for g in range(4):
        tab[:, 12 + g] = np.where((g == odd) | (g == odd + 1), 0, -1e30)
        tab[:, 16 + g] = np.where((g == odd + 1) | (g == odd + 2), 0, -1e30)
        tab[:, 20 + g] = p // 32 == g
        tab[:, 24 + g] = p // 32 == g
    c["tab"] = tab
    return c


def laid_out(inp):
    g = {k: np.ascontiguousarray(np.asarray(v)) for k, v in inp.items()}
    stored = [8 * hf + 4 * par + j for hf in range(2) for j in range(4) for par in range(2)]
    cols = np.array([h * HD + e for h in stored for e in range(HD)])
    a = {}
    a["x"] = np.roll(g["L0_attn_x"], ROT, axis=1)
    for L, q, k, v, o in ((0, "w_q", "w_k", "w_v", "w_o"), (1, "wq", "wk", "wv", "wproj")):
        n = f"L{L}_attn_"
        a[f"L{L}_wqk"] = np.concatenate([g[n + q][:, cols], g[n + k][:, cols]], 1)
        bq, bk, bv, bo = ("b_q", "b_k", "b_v", "b_o") if L == 0 else ("bq", "bk", "bv", "bproj")
        a[f"L{L}_bqk"] = np.concatenate([g[n + bq][cols], g[n + bk][cols]])
        a[f"L{L}_wv"], a[f"L{L}_bv"] = g[n + v], g[n + bv]
        a[f"L{L}_wo"], a[f"L{L}_bo"] = g[n + o], g[n + bo]
        f = f"L{L}_ffn_"
        a[f"L{L}_gw"] = g[f + "gate_w"] if L == 0 else g[f + "gate_w"].T
        a[f"L{L}_gb"] = g[f + "gate_b"]
        a[f"L{L}_w1e"] = g[f + "w1"].reshape(NE * P, DF)
        a[f"L{L}_w2e"] = g[f + "w2"].reshape(NE * DF, D)
        a[f"L{L}_b1e"], a[f"L{L}_b2e"] = g[f + "b1"].reshape(NE * FC, P).T, g[f + "b2"]
    a["L1_eb"] = g["L1_ffn_expert_bias"]
    a["L0_rms"] = np.concatenate([g["L0_attn_rms_q_w"], g["L0_attn_rms_k_w"]])
    for s, n in (("ln1g", "ln1_g"), ("ln1b", "ln1_b"), ("ln2g", "ln2_g"), ("ln2b", "ln2_b"),
                 ("mw1", "w1"), ("mb1", "b1"), ("mw2", "w2"), ("mb2", "b2")):
        a["L1_" + s] = g["L1_attn_" + n]
    a["L1_mb1"] = a["L1_mb1"].reshape(FC, P).T
    a.update(shape_constants())
    return {k: np.ascontiguousarray(v) for k, v in a.items()}


def kernel(**inputs):
    import concourse.bacc as bacc
    from concourse.bass_utils import run_bass_kernel_spmd

    arrays = laid_out(inputs)
    nc = bacc.Bacc("TRN2", target_bir_lowering=False, num_devices=1)
    aps = {n: nc.dram_tensor(f"in_{n}", v.shape, mybir.dt.from_np(v.dtype), kind="ExternalInput").ap()
           for n, v in arrays.items()}
    out = nc.dram_tensor("out", (B, T, D), F32, kind="ExternalOutput").ap()
    block_kernel(nc, aps, out, None)
    r = run_bass_kernel_spmd(nc, [{f"in_{n}": v for n, v in arrays.items()}], core_ids=[0])
    return np.roll(r.results[0]["out"], -ROT, axis=1)
```

```python
from contextlib import ExitStack

import concourse.bass as bass
import numpy as np
from concourse import mybir

F32 = mybir.dt.float32
BF16 = mybir.dt.bfloat16
ALU = mybir.AluOpType
ACT = mybir.ActivationFunctionType
AX = mybir.AxisListType

P = 128
D = 128
B, T = 4, 512
NT = T // P
NTT = B * NT
H, HD = 16, 8
NU = T // 64
NE, DF = 8, 512
FC = DF // P
NXT = NTT + NE
XPT = NXT // B
WIN = 64
WS = 3
EARLY = 4
ROT = 16
SPLIT = 6 * HD
BIG = 1e10
LN_EPS = 1e-5
RMS_EPS = 1.1920929e-07


class Steps:

    def __init__(self, eng, sem):
        self.eng, self.sem, self.n = eng, sem, 0

    def __call__(self, ins):
        self.n += 1
        ins.then_inc(self.sem, 1)
        self.eng.wait_ge(self.sem, self.n)

    def restart(self):
        self.eng.sem_clear(self.sem)
        self.n = 0


def block_kernel(nc, a, out, dbg):
    with ExitStack() as ctx:
        def sb(name, shape, dt=F32):
            return ctx.enter_context(nc.sbuf_tensor(name, shape, dt))

        def sem(name):
            return ctx.enter_context(nc.semaphore(name))

        arrived = sem("arrived")
        go = {e: sem(f"go_{e}") for e in ("vector", "scalar", "gpsimd", "tensor")}

        class Phase:

            def __init__(self, vec, act, pool, pe, first, last, n, sync=None):
                self.vec, self.act, self.pool, self.pe = vec, act, pool, pe
                self.first, self.last, self.n, self.sync = first, last, n, sync

        def turns(eng, name, n):
            with eng.Fori(0, n) as i:
                yield i
                eng.drain().then_inc(arrived, 1)
                eng.wait_ge(go[name], 1)
                eng.sem_clear(go[name])

        def clear_when_met(sp, first, last):
            sp.wait_ge(arrived, 4)
            sp.sem_clear(range(first.num, last.num + 1))
            sp.sem_clear(arrived)
            for e in go.values():
                sp.sem_inc(e, 1)

        ps_score = ctx.enter_context(nc.psum_tensor("ps_score", [P, 2, 1024], F32))
        ps_turn = ctx.enter_context(nc.psum_tensor("ps_turn", [P, 2, 512], F32))
        ps_proj = ctx.enter_context(nc.psum_tensor("ps_proj", [P, 2, 512], F32))

        x = sb("x", [P, NTT * D])
        xn = sb("xn", [P, NTT * D])
        xnT = sb("xnT", [P, B * T])
        xlT = sb("xlT", [P, B * T])
        s_out = sb("s_out", [P, NTT * D])
        moe = sb("moe", [P, NTT * D])
        gate = sb("gate", [P, NTT, NE])
        ident = sb("ident", [P, P])
        identb = sb("identb", [P, P], BF16)
        ones = sb("ones", [P, P])
        neghalf = sb("neghalf", [P, 256])
        maskq = sb("maskq", [P, 4, 512], BF16)
        maskk = sb("maskk", [P, 5, 512], BF16)
        tab = sb("tab", [P, 64])
        iota8 = sb("iota8", [P, NTT, NE])
        pick8 = sb("pick8", [P, NTT, NE])
        pick8b = sb("pick8b", [P, NTT, NE])
        best = sb("best", [P, NTT])
        pickA = sb("pickA", [P, NTT])
        pickB = sb("pickB", [P, NTT])

        stats = sb("stats", [P, NT, 6])
        mv = sb("mv", [P, NT, 2])
        var = sb("var", [P, NT])
        rstd = sb("rstd", [P, NT])
        xs = sb("xs", [P, NT * D])
        xsT = sb("xsT", [P, T])
        xT = sb("xT", [P, 64 + T + 64])
        q4 = sb("q4", [P, NT * H, HD])
        k4 = sb("k4", [P, NT * H, HD])
        sq = sb("sq", [P, NT * H, HD])
        rest = sb("rest", [P, NT * H, HD])
        ss = sb("ss", [P, 2, NT * H])
        rr = sb("rr", [P, 2, NT * H])
        rt = sb("rt", [P, 2, NT * H])
        eq = sb("eq", [P, NT, H, 64], BF16)
        ek = sb("ek", [P, NT, H, 64], BF16)
        qT = sb("qT", [P, 8, T], BF16)
        kT = sb("kT", [P, 8, 64 + T + 64], BF16)
        v = sb("v", [P, NU, H * 36])
        th = sb("th", [P, 2, 1024])
        pT = sb("pT", [P, 2, 1024])
        gm = sb("gm", [P, NT, H * 4])
        tsum = sb("tsum", [P, NT, H])
        inv = sb("inv", [P, NT, H])
        fit = sb("fit", [P, NT, H])
        fits = sb("fits", [P, NT, H])
        sinv = sb("sinv", [P, H])
        shift = sb("shift", [P, NT, H * 4])
        shifts = sb("shifts", [P, NT, H * 4])
        shr = sb("shr", [P, NT, H * 4])
        eA = sb("eA", [P, NT, H, 4])
        eB = sb("eB", [P, NT, H, 4])
        mA = sb("mA", [P, NT * H])
        osb = sb("osb", [P, H * 36])
        cs = sb("cs", [P, H, 4])
        cs2 = sb("cs2", [P, H, 4])
        wtot = sb("wtot", [P, H])
        wtot2 = sb("wtot2", [P, H])
        wpv = sb("wpv", [P, H, 8, 4])
        head = sb("head", [P, D])
        headT = sb("headT", [P, P])
        o1 = sb("o1", [P, D])

        w1 = sb("w1", [P, WS, DF])
        w2 = sb("w2", [P, WS, FC * D])
        b2r = sb("b2r", [P, WS, D])
        b1s = sb("b1s", [P, WS, FC])
        hT = sb("hT", [P, 2, FC * P])
        xg = sb("xg", [P, WS, D])
        xgT = sb("xgT", [P, 2, P])
        ys = sb("ys", [P, 2, D])
        tiles16 = sb("tiles16", [P, NE, NTT])
        before_tile = sb("before_tile", [P, NTT, NE])
        count8 = sb("count8", [P, NE])
        tiles8 = sb("tiles8", [P, NE])
        first8 = sb("first8", [P, NE])
        last8 = sb("last8", [P, NE])
        posf = sb("posf", [P, NTT])
        pos = sb("pos", [P, NTT], mybir.dt.int32)
        reached = sb("reached", [P, NXT, NE])
        expertf = sb("expertf", [P, NXT])
        expert = sb("expert", [P, NXT], mybir.dt.int32)
        cnst = sb("cnst", [P, P + NTT + NXT])
        sorted_x = nc.dram_tensor("sorted_x", (NXT * P, D), F32, kind="Internal").ap()
        sorted_y = nc.dram_tensor("sorted_y", (NXT * P, D), F32, kind="Internal").ap()
        earlier = cnst[:, 0:P]
        step128 = cnst[:, P:P + NTT]
        tile_no = cnst[:, P + NTT:P + NTT + NXT]

        load = sem("load")


        LOADS = [0]

        def fetch(eng, dst, src):
            LOADS[0] += 16
            eng.dma_start(dst, src).then_inc(load, 16)

        W = {}
        for n, shape in (("L0_wqk", [P, 256]), ("L1_wqk", [P, 256]), ("L0_wv", [P, 32]), ("L1_wv", [P, 128]),
                         ("L0_wo", [P, D]), ("L1_wo", [P, D]), ("L0_gw", [P, NE]), ("L1_gw", [P, NE]),
                         ("L1_mw1", [P, DF]), ("L1_mb1", [P, FC])):
            W[n] = sb(n, shape)
        W["L1_mw2"] = sb("L1_mw2", [P, FC, D])
        ROWS = {"L0_bo": D, "L1_bo": D,
                "L0_gb": NE, "L1_gb": NE, "L1_eb": NE, "L1_mb2": D}
        for n, k in ROWS.items():
            W[n] = sb(n, [1, k])
        WIDE = {"L0_bqk": 256, "L1_bqk": 256, "L0_bv": 32, "L1_bv": 128, "L0_rms": 16, "L1_ln1g": D, "L1_ln1b": D, "L1_ln2g": D, "L1_ln2b": D}
        for n, k in WIDE.items():
            W[n] = sb(n, [P, k])
        rmsw = sb("rmsw", [P, 2, HD])
        vbias = sb("vbias", [P, 4, D])

        x3 = a["x"].rearrange("b (t p) d -> p (b t) d", p=P)
        out3 = out.rearrange("b (t p) d -> p (b t) d", p=P)

        block = ctx.enter_context(nc.Block())

        tab_nm = tab[:, 0:4]
        tab_al = tab[:, 4:8]
        tab_al1 = tab[:, 8:12]
        tab_nA = tab[:, 12:16]
        tab_nB = tab[:, 16:20]
        tab_bd = tab[:, 20:24]
        tab_mod = tab[:, 24:28]

        dve_chain = sem("dve_chain")
        act_chain = sem("act_chain")
        pool_chain = sem("pool_chain")

        def sync_load(sp):
            fetch(sp, x[:, :].rearrange("p (n d) -> p n d", d=D), x3)
            for n in ("ident", "identb", "maskq", "maskk", "tab", "iota8", "cnst"):
                t = {"ident": ident, "identb": identb, "maskq": maskq, "maskk": maskk, "tab": tab, "iota8": iota8, "cnst": cnst}[n]
                src = a[n].bitcast(BF16) if n in ("identb", "maskq", "maskk") else a[n]
                fetch(sp, t[tuple(slice(None) for _ in t.shape)], src)
            for n, t in W.items():
                src = a[n]
                if n in ROWS or n in WIDE:
                    src = src.rearrange("(o n) -> o n", o=1)
                if n in WIDE:
                    src = src.broadcast_to([P, WIDE[n]])
                if n == "L1_mw2":
                    src = src.rearrange("(c p) n -> p c n", p=P)
                fetch(sp, t[tuple(slice(None) for _ in t.shape)], src)

        def loaded(eng):
            eng.wait_ge(load, LOADS_ALL)

        LOADS_ALL = 16 * (8 + len(W))

        made = sem("constants_made")
        filled = sem("filled")

        def pool_const(po):
            po.memset(ones[:, :], 1.0).then_inc(made, 1)
            po.memset(neghalf[:, :], -0.5).then_inc(made, 1)
            po.memset(eq[:, :, :, :], 0.0).then_inc(made, 1)
            po.memset(ek[:, :, :, :], 0.0).then_inc(made, 1)
            po.memset(moe[:, :], 0.0).then_inc(made, 1)
            po.wait_ge(made, 5)
            for h in range(2):
                po.dma_start(sorted_x[h * (NXT // 2) * P:(h + 1) * (NXT // 2) * P, :].rearrange("(n p) d -> p n d", p=P),
                             moe[:, 0:NXT // 2 * D].rearrange("p (n d) -> p n d", d=D)).then_inc(filled, 16)
            po.wait_ge(filled, 32)

        def consts(eng):
            eng.wait_ge(made, 5)

        def norm_phase(L, joined):
            s_var = sem(f"{L}_var")
            s_rstd = sem(f"{L}_rstd")
            s_xs = sem(f"{L}_xs")
            s_tr = sem(f"{L}_tr")
            s_xsT = sem(f"{L}_xsT")
            s_xnc = sem(f"{L}_xn_kept")
            s_gp = sem(f"{L}_gp")
            s_gate = sem(f"{L}_gate")
            xl = sb(f"xl{L}", [P, NT * D])
            s_xl = sem(f"{L}_xl")

            def vec(dv):
                st = Steps(dv, dve_chain)
                loaded(dv)
                if joined is not None:
                    dv.wait_ge(joined, 1)
                for i in turns(dv, "vector", B):
                    for r in range(1 + (L == 1)):
                        for t in range(NT):
                            src = x[:, bass.ds((i * NT + t) * D, D)] if r == 0 else xs[:, t * D:(t + 1) * D]
                            st(nc.vector.bn_stats(stats[:, t, :], src))
                            st(nc.vector.bn_aggr(mv[:, t, :], stats[:, t, :]))
                        nc.vector.tensor_scalar(var[:, :], mv[:, :, 1], LN_EPS, None, ALU.add).then_inc(s_var, 1)
                        if r > 0:
                            dv.wait_ge(s_tr, r)
                        dv.wait_ge(s_rstd, r + 1)
                        dst = xs if r == 0 else xl
                        for t in range(NT):
                            src = x[:, bass.ds((i * NT + t) * D, D)] if r == 0 else xs[:, t * D:(t + 1) * D]
                            ins = nc.vector.tensor_scalar(dst[:, t * D:(t + 1) * D], src, mv[:, t, 0:1],
                                                          rstd[:, t:t + 1], ALU.subtract, ALU.mult)
                            if r == 0 and t == NT - 1:
                                ins.then_inc(s_xs, 1)
                                dv.wait_ge(s_xs, 1)
                            else:
                                st(ins)
                        if r == 1:
                            x4 = xl[:, :].rearrange("p (t d) -> p t d", d=D)
                            st(nc.vector.tensor_tensor(x4, x4, W["L1_ln1g"][:, None, :].broadcast_to([P, NT, D]), ALU.mult))
                            nc.vector.tensor_tensor(x4, x4, W["L1_ln1b"][:, None, :].broadcast_to([P, NT, D]), ALU.add).then_inc(s_xl, 1)
                            dv.wait_ge(s_xl, 1)
                    st.restart()

            def pool(po):
                consts(po)
                for i in turns(po, "gpsimd", B):
                    for r in range(1 + (L == 1)):
                        po.wait_ge(s_var, r + 1)
                        nc.gpsimd.tensor_tensor(rstd[:, :], var[:, :], neghalf[:, 0:NT], ALU.pow).then_inc(s_rstd, 1)
                        if r == 0:
                            po.wait_ge(s_xs, 1)
                            nc.gpsimd.tensor_copy(xn[:, bass.ds(i * (NT * D), NT * D)], xs[:, :]).then_inc(s_xnc, 1)

            def pe(te):
                loaded(te)
                consts(te)
                for i in turns(te, "tensor", B):
                    te.wait_ge(s_xs, 1)
                    for t in range(NT):
                        ins = te.transpose(ps_turn[:, 0, t * P:(t + 1) * P], xs[:, t * D:(t + 1) * D], ident[:, :])
                    ins.then_inc(s_tr, 1)
                    te.wait_ge(s_xsT, 1)
                    for t in range(NT):
                        o = ps_proj[:, 0, t * NE:(t + 1) * NE]
                        te.matmul(o, xsT[:, t * P:(t + 1) * P], W[f"L{L}_gw"][:, :], start=True, stop=False)
                        if L == 1:
                            te.matmul(o, ones[0:1, :], W["L1_eb"][:, :], start=False, stop=False)
                        ins = te.matmul(o, ones[0:1, :], W[f"L{L}_gb"][:, :], start=False, stop=True)
                    ins.then_inc(s_gp, 1)
                    if L == 1:
                        te.wait_ge(s_xl, 1)
                        for t in range(NT):
                            ins = te.transpose(ps_turn[:, 1, t * P:(t + 1) * P], xl[:, t * D:(t + 1) * D], ident[:, :])
                        ins.then_inc(s_tr, 1)

            def act(ac):
                for i in turns(ac, "scalar", B):
                    ac.wait_ge(s_tr, 1)
                    nc.scalar.activation(xsT[:, :], ps_turn[:, 0, :], ACT.Copy).then_inc(s_xsT, 1)
                    nc.scalar.activation(xnT[:, bass.ds(i * T, T)], ps_turn[:, 0, :], ACT.Copy).then_inc(s_xsT, 1)
                    ac.wait_ge(s_gp, 1)
                    nc.scalar.activation(
                        gate[:, :, :].rearrange("p n e -> p (n e)")[:, bass.ds(i * (NT * NE), NT * NE)],
                        ps_proj[:, 0, 0:NT * NE], ACT.Copy).then_inc(s_gate, 1)
                    if L == 1:
                        ac.wait_ge(s_tr, 2)
                        nc.scalar.activation(xlT[:, bass.ds(i * T, T)], ps_turn[:, 1, :], ACT.Copy).then_inc(s_xsT, 1)
            return Phase(vec, act, pool, pe, s_var, s_xl, B)

        def attention_phase(L):
            NG = 1 if L == 0 else 4
            NK = SPLIT + 3 * NG
            KOFF = 64 if L == 0 else 32
            NV = 32 if L == 0 else 128
            srcT = xnT if L == 0 else xlT
            ev = 2 if L == 0 else 2
            s_xT = sem(f"{L}_xT")
            s_qkp = sem(f"{L}_qk_proj")
            s_qk = sem(f"{L}_qk")
            s_vp = sem(f"{L}_v_proj")
            s_v = sem(f"{L}_v")
            s_ms = sem(f"{L}_ms")
            s_rms = sem(f"{L}_rms")
            s_ek = sem(f"{L}_ek")
            s_dup = sem(f"{L}_dup")
            s_eq = sem(f"{L}_eq")
            s_turn = sem(f"{L}_turned")
            s_T = sem(f"{L}_T")
            s_pad = sem(f"{L}_pad")
            s_sc = sem(f"{L}_scores")
            s_th = sem(f"{L}_tanh")
            s_mx = sem(f"{L}_max")
            s_inv = sem(f"{L}_inv")
            s_sin = sem(f"{L}_suminv")
            s_dif = sem(f"{L}_dif")
            s_cof = sem(f"{L}_cof")
            s_st = sem(f"{L}_shifted")
            s_p = sem(f"{L}_probs")
            s_pv = sem(f"{L}_pv")
            s_hd = sem(f"{L}_head")
            s_osb = sem(f"{L}_osb")
            s_hT = sem(f"{L}_headT")
            s_hTs = sem(f"{L}_headTs")
            s_ew = [sem(f"{L}_expert_in{k}") for k in range(WS)]
            s_ex = sem(f"{L}_expert_xT")
            s_exs = sem(f"{L}_expert_xT_kept")
            s_eu = sem(f"{L}_expert_up")
            s_eh = sem(f"{L}_expert_hidden")
            s_ed = sem(f"{L}_expert_down")
            s_ec = sem(f"{L}_expert_copied")
            s_ey = sem(f"{L}_expert_y")
            s_es = [sem(f"{L}_expert_out{k}") for k in range(2)]
            s_op = sem(f"{L}_oproj")
            s_o = sem(f"{L}_o")

            def slot(n):
                return ps_turn[:, :, :].rearrange("p a b -> p (a b)") if n % 3 == 2 else ps_score[:, n % 3, :]

            e_w1, e_w2, e_b1, e_b2 = a[f"L{L}_w1e"], a[f"L{L}_w2e"], a[f"L{L}_b1e"], a[f"L{L}_b2e"]

            def sync(sp, i):
                for j in range(XPT + WS):
                    if j >= WS:
                        t = j - WS
                        sp.wait_ge(s_ey, t + 1)
                        sp.dma_start(sorted_y[bass.ds((i * XPT + t) * P, P), :], ys[:, t % 2, :]).then_inc(s_es[t % 2], 16)
                    if j < XPT:
                        k = j % WS
                        ex = sp.value_load(expert[0:1, bass.ds(i * XPT + j, 1)], min_val=0, max_val=NE - 1)
                        sp.dma_start(xg[:, k, :], sorted_x[bass.ds((i * XPT + j) * P, P), :]).then_inc(s_ew[k], 16)
                        sp.dma_start(w1[:, k, :], e_w1[bass.ds(ex * P, P), :]).then_inc(s_ew[k], 16)
                        sp.dma_start(w2[:, k, :].rearrange("p (c n) -> p c n", c=FC),
                                     e_w2[bass.ds(ex * DF, DF), :].rearrange("(c p) n -> p c n", p=P)).then_inc(s_ew[k], 16)
                        sp.dma_start(b1s[:, k, :], e_b1[bass.ds(ex * P, P), :]).then_inc(s_ew[k], 16)
                        sp.dma_start(b2r[:, k, :], e_b2[bass.ds(ex, 1), :].broadcast_to([P, D])).then_inc(s_ew[k], 16)
                for k in range(2):
                    sp.wait_ge(s_es[k], 16 * (XPT // 2))

            def pool(po):
                for i in turns(po, "gpsimd", B):
                    for j in range(XPT):
                        po.wait_ge(s_ec, j + 1)
                        nc.gpsimd.tensor_tensor(ys[:, j % 2, :], ys[:, j % 2, :], b2r[:, j % WS, :], ALU.add).then_inc(s_ey, 1)

            def vec(dv):
                st = Steps(dv, dve_chain)
                ekv = ek[:, :, :, :].rearrange("p t h r -> p (t h) r")
                eqv = eq[:, :, :, :].rearrange("p t h r -> p (t h) r")
                vv = v[:, :, 0:H * 36].rearrange("p u (h g e) -> p u h g e", g=4, e=9)
                if L == 0:
                    consts(dv)
                    st(nc.vector.memset(ekv[:, :, SPLIT:SPLIT + 3], 1.0))
                    st(nc.vector.memset(v[:, :, 0:36].rearrange("p u (h e) -> p u h e", e=9)[:, :, :, 8], 1.0))
                    st(nc.vector.tensor_scalar(rmsw[:, 0, :], W["L0_rms"][:, 0:8], float(1 / np.sqrt(np.float32(HD))), None, ALU.mult))
                    st(nc.vector.tensor_copy(rmsw[:, 1, :], W["L0_rms"][:, 8:16]))
                else:
                    for s in range(3):
                        st(nc.vector.tensor_copy(ekv[:, :, SPLIT + 4 * s:SPLIT + 4 * s + 4],
                                                 tab_mod[:, None, :].broadcast_to([P, NT * H, 4])))
                    for g in range(4):
                        st(nc.vector.tensor_scalar(vbias[:, g, :], W["L1_bv"][:, :], tab_bd[:, g:g + 1], None, ALU.mult))
                    for u in range(NU):
                        st(nc.vector.tensor_copy(vv[:, u, :, :, 8], tab_bd[:, None, :].broadcast_to([P, H, 4])))
                st.restart()

                def split_q(st, i, n):
                    st(nc.vector.tensor_copy(eqv[:, :, 0:24].rearrange("p h (c e) -> p h c e", c=3),
                                             q4[:, :, None, :].broadcast_to([P, NT * H, 3, HD])))
                    st(nc.vector.tensor_tensor(rest[:, :, :], q4[:, :, :], eqv[:, :, 0:8], ALU.subtract))
                    st(nc.vector.tensor_copy(eqv[:, :, 24:40].rearrange("p h (c e) -> p h c e", c=2),
                                             rest[:, :, None, :].broadcast_to([P, NT * H, 2, HD])))
                    nc.vector.tensor_tensor(eqv[:, :, 40:48], rest[:, :, :], eqv[:, :, 24:32], ALU.subtract).then_inc(s_eq, 1)
                    dv.wait_ge(s_eq, n)

                for i in turns(dv, "vector", B):
                    nc.vector.tensor_copy(xT[:, 64:64 + T], srcT[:, bass.ds(i * T, T)]).then_inc(s_xT, 1)
                    nc.vector.tensor_copy(xT[:, 0:64], srcT[:, bass.ds(i * T + T - 64, 64)]).then_inc(s_xT, 1)
                    nc.vector.tensor_copy(xT[:, 64 + T:128 + T], srcT[:, bass.ds(i * T, 64)]).then_inc(s_xT, 1)
                    for c in range(2):
                        dv.wait_ge(s_vp, c + 1)
                        if L == 0:
                            for u in range(4):
                                ins = nc.vector.tensor_tensor(
                                    v[:, 4 * c + u, 0:36].rearrange("p (h e) -> p h e", e=9)[:, :, 0:8],
                                    ps_proj[:, c, 32 * u:32 * u + 32].rearrange("p (h e) -> p h e", e=8),
                                    W["L0_bv"][:, :].rearrange("p (h e) -> p h e", e=8), ALU.add)
                            ins.then_inc(s_v, 1)
                        else:
                            for u in range(4):
                                o = ps_proj[:, c, u * 128:(u + 1) * 128].rearrange("p (h e) -> p h e", e=8)
                                for g in range(4):
                                    ins = nc.vector.scalar_tensor_tensor(
                                        out=vv[:, 4 * c + u, :, g, 0:8], in0=o, scalar=tab_bd[:, g:g + 1],
                                        in1=vbias[:, g, :].rearrange("p (h e) -> p h e", e=8), op0=ALU.mult, op1=ALU.add)
                            ins.then_inc(s_v, 1)
                    for t in range(NT):
                        dv.wait_ge(s_qkp, t + 1)
                        for z, m in ((q4, 0), (k4, 128)):
                            nc.vector.tensor_tensor(z[:, t * H:(t + 1) * H, :].rearrange("p h e -> p (h e)"),
                                                    ps_proj[:, t % 2, m:m + 128], W[f"L{L}_bqk"][:, m:m + 128],
                                                    ALU.add).then_inc(s_qk, 1)
                    dv.wait_ge(s_qk, 2 * NT)
                    if L == 0:
                        for z, m in ((q4, 0), (k4, 1)):
                            st(nc.vector.tensor_tensor(sq[:, :, :], z[:, :, :], z[:, :, :], ALU.mult))
                            st(nc.vector.tensor_reduce(ss[:, m, :], sq[:, :, :], AX.X, ALU.add))
                        nc.vector.tensor_scalar(ss[:, :, :], ss[:, :, :], 1.0 / HD, RMS_EPS, ALU.mult, ALU.add).then_inc(s_ms, 1)
                        dv.wait_ge(s_rms, 1)
                        st(nc.vector.reciprocal(rr[:, :, :], rr[:, :, :]))
                        st(nc.vector.tensor_tensor(rt[:, :, :], rr[:, :, :], rr[:, :, :], ALU.mult))
                        st(nc.vector.tensor_tensor(rt[:, :, :], rt[:, :, :], ss[:, :, :], ALU.mult))
                        st(nc.vector.tensor_scalar(rt[:, :, :], rt[:, :, :], -0.5, 1.5, ALU.mult, ALU.add))
                        st(nc.vector.tensor_tensor(rr[:, :, :], rr[:, :, :], rt[:, :, :], ALU.mult))
                        for z, m in ((q4, 0), (k4, 1)):
                            st(nc.vector.tensor_tensor(z[:, :, :], z[:, :, :], rr[:, m, :, None].broadcast_to([P, NT * H, HD]), ALU.mult))
                            st(nc.vector.tensor_tensor(z[:, :, :], z[:, :, :], rmsw[:, m:m + 1, :].broadcast_to([P, NT * H, HD]), ALU.mult))
                    else:
                        st(nc.vector.tensor_scalar(q4[:, :, :], q4[:, :, :], float(HD) ** -0.5, None, ALU.mult))
                    st(nc.vector.tensor_copy(ekv[:, :, 0:8], k4[:, :, :]))
                    st(nc.vector.tensor_tensor(rest[:, :, :], k4[:, :, :], ekv[:, :, 0:8], ALU.subtract))
                    st(nc.vector.tensor_copy(ekv[:, :, 8:16], rest[:, :, :]))
                    nc.vector.tensor_tensor(ekv[:, :, 16:24], rest[:, :, :], ekv[:, :, 8:16], ALU.subtract).then_inc(s_ek, 1)
                    nc.vector.tensor_copy(ekv[:, :, 24:40], ekv[:, :, 0:16]).then_inc(s_dup, 1)
                    nc.vector.tensor_copy(ekv[:, :, 40:48], ekv[:, :, 0:8]).then_inc(s_dup, 1)
                    split_q(st, i, 1)
                    dv.wait_ge(s_T, NT)
                    nc.vector.tensor_copy(kT[:, :, 0:64], kT[:, :, T:T + 64]).then_inc(s_pad, 1)
                    nc.vector.tensor_copy(kT[:, :, 64 + T:128 + T], kT[:, :, 64:128]).then_inc(s_pad, 1)
                    for t in range(NT):
                        for hf in range(2):
                            n = 2 * t + hf
                            src = slot(n)
                            if L == 0:
                                dv.wait_ge(s_th, n + 1)
                                st(nc.vector.tensor_reduce(tsum[:, t, 8 * hf:8 * hf + 8],
                                                           th[:, n % 2, :].rearrange("p (h k) -> p h k", k=128), AX.X, ALU.add))
                                nc.vector.tensor_reduce(gm[:, t, 8 * hf:8 * hf + 8],
                                                                src.rearrange("p (h k) -> p h k", k=128), AX.X, ALU.max).then_inc(s_mx, 1)
                            else:
                                dv.wait_ge(s_sc, n + 1)
                                nc.vector.tensor_reduce(gm[:, t, 32 * hf:32 * hf + 32],
                                                                src.rearrange("p (h k) -> p h k", k=32), AX.X, ALU.max).then_inc(s_mx, 1)
                    dv.wait_ge(s_mx, 2 * NT)
                    if L == 0:
                        for t in range(NT):
                            st(nc.vector.tensor_scalar(inv[:, t, :], tsum[:, t, :], tab_nm[:, t:t + 1], 1.0 / (2 * T), ALU.add, ALU.mult))
                        st(nc.vector.tensor_scalar(inv[:, :, :], inv[:, :, :], 1.0, None, ALU.add))
                        nc.vector.reciprocal(inv[:, :, :], inv[:, :, :]).then_inc(s_inv, 1)
                        dv.wait_ge(s_sin, 1)
                        st(nc.vector.tensor_reduce(sinv[:, :], ps_proj[:, 0, 0:NT * H].rearrange("p (t h) -> p h t", h=H), AX.X, ALU.add))
                        st(nc.vector.reciprocal(sinv[:, :], sinv[:, :]))
                        st(nc.vector.tensor_tensor(fit[:, :, :], inv[:, :, :], sinv[:, None, :].broadcast_to([P, NT, H]), ALU.mult))
                        st(nc.vector.scalar_tensor_tensor(out=shift[:, :, 0:H], in0=gm[:, :, 0:H], scalar=-1.0, in1=fit[:, :, :],
                                                          op0=ALU.mult, op1=ALU.mult))
                        for par in range(2):
                            st(nc.vector.tensor_copy(
                                fits[:, :, :].rearrange("p t (f j a) -> p (t f) j a", f=2, a=2)[:, :, :, par],
                                fit[:, :, :].rearrange("p t (f a j) -> p (t f) a j", f=2, a=2)[:, :, par, :]))
                            st(nc.vector.tensor_copy(
                                shifts[:, :, 0:H].rearrange("p t (f j a) -> p t f j a", f=2, a=2)[:, :, :, :, par],
                                shift[:, :, 0:H].rearrange("p t (f a j) -> p t f a j", f=2, a=2)[:, :, :, par, :]))
                        st(nc.vector.tensor_tensor(q4[:, :, :], q4[:, :, :], fits[:, :, :].rearrange("p t h -> p (t h)")[:, :, None].broadcast_to([P, NT * H, HD]), ALU.mult))
                        rows = [shifts[:, :, 0:H]]
                    else:
                        g3 = gm[:, :, :].rearrange("p t (h g) -> p (t h) g", g=4)
                        for n, (e_, nm) in enumerate(((eA, tab_nA), (eB, tab_nB))):
                            e3 = e_[:, :, :, :].rearrange("p t h g -> p (t h) g")
                            st(nc.vector.tensor_tensor(e3, g3, nm[:, None, :].broadcast_to([P, NT * H, 4]), ALU.add))
                            st(nc.vector.tensor_reduce(mA[:, :], e3, AX.X, ALU.max))
                            nc.vector.tensor_tensor(e3, e3, mA[:, :, None].broadcast_to([P, NT * H, 4]), ALU.subtract).then_inc(s_dif, 1)
                            dv.wait_ge(s_dif, n + 1)
                        for par in range(2):
                            for f in range(2):
                                for blk, base in ((0, 3), (1, 1)):
                                    sp_ = slice(64 * blk, 64 * blk + 64)
                                    dst = shifts[sp_, :, :].rearrange("p t (f j a g) -> p t f j a g", f=2, a=2, g=4)[:, :, f, :, par, :]
                                    src = gm[sp_, :, :].rearrange("p t (f a j g) -> p t f a j g", f=2, a=2, g=4)[:, :, f, par, :, :]
                                    k = 4 - base
                                    st(nc.vector.tensor_scalar(dst[:, :, :, base:4], src[:, :, :, 0:k], -1.0, None, ALU.mult))
                                    st(nc.vector.tensor_scalar(dst[:, :, :, 0:base], src[:, :, :, k:4], -1.0, None, ALU.mult))
                    sh = shifts[:, :, 0:H * NG].rearrange("p t (h g) -> p t h g", g=NG)
                    r3 = shr[:, :, 0:H * NG].rearrange("p t (h g) -> p t h g", g=NG)
                    part = [eq[:, :, :, SPLIT + NG * s:SPLIT + NG * (s + 1)] for s in range(3)]
                    dv.wait_ge(s_turn, 2 * NT)
                    st(nc.vector.tensor_copy(part[0], sh))
                    st(nc.vector.tensor_tensor(r3, sh, part[0], ALU.subtract))
                    st(nc.vector.tensor_copy(part[1], r3))
                    st(nc.vector.tensor_tensor(part[2], r3, part[1], ALU.subtract))
                    split_q(st, i, 2)
                    for t in range(NT):
                        dv.wait_ge(s_pv, 2 * t + 2)
                        if L == 0:
                            o = ps_turn[:, 0, 0:H * 9].rearrange("p (h e) -> p h e", e=9)
                            st(nc.vector.reciprocal(wtot[:, :], o[:, :, 8]))
                            if t > 0:
                                dv.wait_ge(s_hT, t)
                            nc.vector.tensor_tensor(head[:, :].rearrange("p (h e) -> p h e", e=8), o[:, :, 0:8],
                                                            wtot[:, :, None].broadcast_to([P, H, 8]), ALU.mult).then_inc(s_hd, 1)
                        else:
                            if t == 0:
                                dv.wait_ge(s_cof, 2)
                            st(nc.vector.tensor_copy(osb[:, 0:288], ps_turn[:, 0, 0:288]))
                            nc.vector.tensor_copy(osb[:, 288:576], ps_turn[:, 1, 0:288]).then_inc(s_osb, 1)
                            dv.wait_ge(s_osb, t + 1)
                            o = osb[:, :].rearrange("p (h g e) -> p h g e", g=4, e=9)
                            for n, (e_, al, c_, w_) in enumerate(((eA, tab_al1, cs, wtot), (eB, tab_al, cs2, wtot2))):
                                st(nc.vector.tensor_tensor(c_[:, :, :], e_[:, t, :, :], o[:, :, :, 8], ALU.mult))
                                st(nc.vector.tensor_reduce(w_[:, :], c_[:, :, :], AX.X, ALU.add))
                                st(nc.vector.reciprocal(w_[:, :], w_[:, :]))
                                st(nc.vector.tensor_scalar(w_[:, :], w_[:, :], al[:, t:t + 1], None, ALU.mult))
                                st(nc.vector.tensor_tensor(c_[:, :, :], e_[:, t, :, :], w_[:, :, None].broadcast_to([P, H, 4]), ALU.mult))
                            st(nc.vector.tensor_tensor(cs[:, :, :], cs[:, :, :], cs2[:, :, :], ALU.add))
                            st(nc.vector.tensor_tensor(wpv[:, :, :, :].rearrange("p h e g -> p h g e"), o[:, :, :, 0:8],
                                                       cs[:, :, :, None].broadcast_to([P, H, 4, 8]), ALU.mult))
                            if t > 0:
                                dv.wait_ge(s_hT, t)
                            nc.vector.tensor_reduce(head[:, :], wpv[:, :, :, :].rearrange("p h e g -> p (h e) g"), AX.X, ALU.add).then_inc(s_hd, 1)
                        dv.wait_ge(s_hd, t + 1)
                    st.restart()

            def pe(te):
                for i in turns(te, "tensor", B):
                    te.wait_ge(s_xT, 3)
                    for c in range(2):
                        for u in range(4):
                            p0 = 64 + 64 * (4 * c + u) - KOFF
                            o = ps_proj[:, c, u * NV:(u + 1) * NV]
                            ins = te.matmul(o, xT[:, p0:p0 + P], W[f"L{L}_wv"][:, :], start=True, stop=True)
                        ins.then_inc(s_vp, 1)
                    for t in range(NT):
                        if t < 2:
                            te.wait_ge(s_v, t + 1)
                        else:
                            te.wait_ge(s_qk, 2 * (t - 1))
                        o = ps_proj[:, t % 2, 0:256]
                        te.matmul(o, xT[:, 64 + t * P:64 + (t + 1) * P], W[f"L{L}_wqk"][:, :],
                                  start=True, stop=True).then_inc(s_qkp, 1)

                    def turn(src, n, t):
                        if n >= 2:
                            te.wait_ge(s_T, n - 1)
                        dst = ps_turn[:, n % 2, :].bitcast(BF16)
                        for pr in range(8):
                            ins = te.transpose(dst[:, pr * P:(pr + 1) * P],
                                               src[:, t, 2 * pr:2 * pr + 2, :].rearrange("p h r -> p (h r)"), identb[:, :])
                        ins.then_inc(s_turn, 1)

                    def expert_up(j):
                        k = j % 2
                        te.wait_ge(s_ew[j % WS], 80 * (j // WS + 1))
                        if j >= 2:
                            te.wait_ge(s_ec, j - 1)
                        te.transpose(ps_score[:, k, 512:640], xg[:, j % WS, :], ident[:, :]).then_inc(s_ex, 1)
                        te.wait_ge(s_exs, j + 1)
                        for c in range(FC):
                            ins = te.matmul(ps_score[:, k, c * P:(c + 1) * P], w1[:, j % WS, c * P:(c + 1) * P], xgT[:, k, :],
                                            start=True, stop=True)
                        ins.then_inc(s_eu, 1)

                    def expert_down(j):
                        k = j % 2
                        te.wait_ge(s_eh, j + 1)
                        for c in range(FC):
                            ins = te.matmul(ps_score[:, k, 512:640], hT[:, k, c * P:(c + 1) * P], w2[:, j % WS, c * D:(c + 1) * D],
                                            start=(c == 0), stop=(c == FC - 1))
                        ins.then_inc(s_ed, 1)

                    for j in range(EARLY):
                        expert_up(j)
                        if j >= 1:
                            expert_down(j - 1)
                    expert_down(EARLY - 1)
                    te.wait_ge(s_ek, 1)
                    te.wait_ge(s_dup, 2)
                    for t in range(NT):
                        turn(ek, t, t)
                    te.wait_ge(s_eq, 1)
                    for t in range(NT):
                        turn(eq, NT + t, t)
                    te.wait_ge(s_pad, 2)
                    te.wait_ge(s_T, 2 * NT)
                    for t in range(NT):
                        for hf in range(2):
                            n = 2 * t + hf
                            if n == 0:
                                te.wait_ge(s_ec, EARLY)
                            if n >= 3:
                                te.wait_ge(s_mx, n - 2)
                            bank = [slot(n)[:, 512 * par:512 * par + 512] for par in range(2)]
                            m = {0: {0: 0, 1: 1, 2: 1, 3: 1}, 1: {0: 2, 3: 3}}[L].get(t)
                            if m is not None:
                                for par in range(2):
                                    te.matmul(bank[par], identb[:, :], maskq[:, m, :], start=True, stop=False, skip_group_check=True)
                            for blk in range(2):
                                for j in range(4):
                                    for par in range(2):
                                        q0 = t * P + 64 * blk
                                        ins = te.matmul(bank[par][64 * blk:64 * blk + 64, j * P:(j + 1) * P],
                                                        qT[64 * par:64 * par + SPLIT, 4 * hf + j, q0:q0 + 64],
                                                        kT[64 * par:64 * par + SPLIT, 4 * hf + j, 64 + q0 - KOFF:64 + q0 - KOFF + P],
                                                        start=m is None, stop=True, skip_group_check=True)
                            ins.then_inc(s_sc, 1)
                    te.wait_ge(s_mx, 2 * NT)
                    expert_up(EARLY)
                    if L == 0:
                        te.wait_ge(s_inv, 1)
                        te.matmul(ps_proj[:, 0, 0:NT * H], ones[:, :], inv[:, :, :].rearrange("p t h -> p (t h)"), start=True, stop=True).then_inc(s_sin, 1)
                    for j in range(EARLY + 1, XPT):
                        expert_up(j)
                        expert_down(j - 1)
                    expert_down(XPT - 1)
                    te.wait_ge(s_eq, 2)
                    for t in range(NT):
                        turn(eq, 2 * NT + t, t)
                    te.wait_ge(s_T, 3 * NT)
                    te.wait_ge(s_ec, XPT)

                    def probs(u):
                        if u >= 2:
                            te.wait_ge(s_p, u - 1)
                        bank = [ps_score[:, u % 2, 512 * par:512 * par + 512] for par in range(2)]
                        m = ({0: 0, 1: 1} if L == 0 else {0: 3, NU - 1: 4}).get(u, 2 if L == 0 else None)
                        if m is not None:
                            for par in range(2):
                                te.matmul(bank[par], identb[:, :], maskk[:, m, :], start=True, stop=False, skip_group_check=True)
                        for pr in range(8):
                            for par in range(2):
                                k0 = 64 + 64 * u - KOFF
                                ins = te.matmul(bank[par][:, pr * 64:pr * 64 + 64],
                                                kT[64 * par:64 * par + NK, pr, k0:k0 + P],
                                                qT[64 * par:64 * par + NK, pr, 64 * u:64 * u + 64],
                                                start=m is None, stop=True, skip_group_check=True)
                        ins.then_inc(s_st, 1)

                    def weigh(u):
                        te.wait_ge(s_p, u + 1)
                        t, blk = u // 2, u % 2
                        if blk == 0 and t >= 1:
                            if t > 0:
                                te.wait_ge((s_hd if L == 0 else s_osb), t)
                        for h in range(H):
                            hf, par, j = h // 8, h // 4 % 2, h % 4
                            w_ = pT[:, u % 2, par * 512 + (4 * hf + j) * 64:par * 512 + (4 * hf + j) * 64 + 64]
                            if L == 0:
                                o = ps_turn[64 * blk:64 * blk + 64, 0, 9 * h:9 * h + 9]
                                r = v[:, u, 9 * (h // 4):9 * (h // 4) + 9]
                            else:
                                o = ps_turn[64 * blk:64 * blk + 64, hf, 36 * (h % 8):36 * (h % 8) + 36]
                                r = v[:, u, 36 * h:36 * h + 36]
                            ins = te.matmul(o, w_, r, start=True, stop=True)
                        ins.then_inc(s_pv, 1)

                    def project(t):
                        te.wait_ge(s_hd, t + 1)
                        if t >= 1:
                            if t > 0:
                                te.wait_ge(s_o, t)
                        te_ins = te.transpose(ps_proj[:, 0, 0:P], head[:, :], ident[:, :])
                        te_ins.then_inc(s_hT, 1)
                        te.wait_ge(s_hTs, t + 1)
                        te.matmul(ps_proj[:, 1, 0:D], headT[:, :], W[f"L{L}_wo"][:, :], start=True, stop=False)
                        te.matmul(ps_proj[:, 1, 0:D], ones[0:1, :], W[f"L{L}_bo"][:, :], start=False, stop=True).then_inc(s_op, 1)

                    probs(0)
                    for u in range(NU):
                        if u + 1 < NU:
                            probs(u + 1)
                        if u == 0:
                            te.wait_ge(s_v, 2)
                        weigh(u)
                        if u % 2 == 1 and u >= 3:
                            project(u // 2 - 1)
                    project(NT - 1)

            def act(ac):
                for i in turns(ac, "scalar", B):
                    if L == 0:
                        ac.wait_ge(s_ms, 1)
                        nc.scalar.activation(rr[:, :, :], ss[:, :, :], ACT.Sqrt).then_inc(s_rms, 1)

                    def expert_hidden(j):
                        k = j % 2
                        ac.wait_ge(s_ex, j + 1)
                        nc.scalar.activation(xgT[:, k, :], ps_score[:, k, 512:640], ACT.Copy).then_inc(s_exs, 1)
                        ac.wait_ge(s_eu, j + 1)
                        for c in range(FC):
                            ins = nc.scalar.activation(hT[:, k, c * P:(c + 1) * P], ps_score[:, k, c * P:(c + 1) * P],
                                                       ACT.Gelu if L == 0 else ACT.Relu, bias=b1s[:, j % WS, c:c + 1])
                        ins.then_inc(s_eh, 1)

                    def expert_result(j):
                        ac.wait_ge(s_ed, j + 1)
                        if j >= 2:
                            ac.wait_ge(s_es[j % 2], 16 * (j // 2))
                        nc.scalar.activation(ys[:, j % 2, :], ps_score[:, j % 2, 512:640], ACT.Copy).then_inc(s_ec, 1)

                    for j in range(EARLY):
                        expert_hidden(j)
                        if j >= 1:
                            expert_result(j - 1)
                    expert_result(EARLY - 1)

                    def keep(n, dst):
                        ac.wait_ge(s_turn, n + 1)
                        nc.scalar.activation(dst, ps_turn[:, n % 2, :].bitcast(BF16).rearrange("p (r k) -> p r k", k=P), ACT.Copy).then_inc(s_T, 1)

                    for t in range(NT):
                        keep(t, kT[:, :, 64 + t * P:64 + (t + 1) * P])
                    for t in range(NT):
                        keep(NT + t, qT[:, :, t * P:(t + 1) * P])
                    if L == 0:
                        for n in range(2 * NT):
                            ac.wait_ge(s_sc, n + 1)
                            if n - 1 > 0:
                                ac.wait_ge(s_mx, n - 1)
                            nc.scalar.activation(th[:, n % 2, :], slot(n), ACT.Tanh, scale=0.5).then_inc(s_th, 1)
                    for j in range(EARLY, XPT):
                        expert_hidden(j)
                        if j > EARLY:
                            expert_result(j - 1)
                    expert_result(XPT - 1)
                    if L == 1:
                        for n, e_ in enumerate((eA, eB)):
                            ac.wait_ge(s_dif, n + 1)
                            nc.scalar.activation(e_[:, :, :, :], e_[:, :, :, :], ACT.Exp).then_inc(s_cof, 1)
                    for t in range(NT):
                        keep(2 * NT + t, qT[:, :, t * P:(t + 1) * P])

                    def finish(t):
                        ac.wait_ge(s_hT, t + 1)
                        if t > 0:
                            ac.wait_ge(s_op, t)
                        nc.scalar.activation(headT[:, :], ps_proj[:, 0, 0:P], ACT.Copy).then_inc(s_hTs, 1)
                        ac.wait_ge(s_op, t + 1)
                        nc.scalar.activation(s_out[:, bass.ds((i * NT + t) * D, D)], ps_proj[:, 1, 0:D], ACT.Copy).then_inc(s_o, 1)

                    for u in range(NU):
                        ac.wait_ge(s_st, u + 1)
                        if u - 1 > 0:
                            ac.wait_ge(s_pv, u - 1)
                        nc.scalar.activation(pT[:, u % 2, :], ps_score[:, u % 2, :], ACT.Exp).then_inc(s_p, 1)
                        if u % 2 == 0 and u >= 4:
                            finish(u // 2 - 2)
                    finish(NT - 2)
                    finish(NT - 1)
            return Phase(vec, act, pool, pe, s_xT, s_o, B, sync)

        def mlp_phase():
            s_var = sem("m_var")
            s_rstd = sem("m_rstd")
            s_h = sem("m_h")
            s_tr = sem("m_tr")
            s_hT = sem("m_hT")
            s_up = sem("m_up")
            s_act = sem("m_act")
            s_dn = sem("m_dn")
            s_out_ = sem("m_out")
            hx = sb("hx", [P, D])
            hxT = sb("hxT", [P, P])

            def vec(dv):
                st = Steps(dv, dve_chain)
                for i in turns(dv, "vector", B):
                    for t in range(NT):
                        at = bass.ds((i * NT + t) * D, D)
                        st(nc.vector.tensor_tensor(s_out[:, at], s_out[:, at], xn[:, at], ALU.add))
                        st(nc.vector.bn_stats(stats[:, 0, :], s_out[:, at]))
                        st(nc.vector.bn_aggr(mv[:, 0, :], stats[:, 0, :]))
                        nc.vector.tensor_scalar(var[:, 0:1], mv[:, 0, 1:2], LN_EPS, None, ALU.add).then_inc(s_var, 1)
                        dv.wait_ge(s_rstd, t + 1)
                        if t > 0:
                            dv.wait_ge(s_tr, t)
                        st(nc.vector.tensor_scalar(hx[:, :], s_out[:, at], mv[:, 0, 0:1], rstd[:, 0:1], ALU.subtract, ALU.mult))
                        st(nc.vector.tensor_tensor(hx[:, :], hx[:, :], W["L1_ln2g"][:, :], ALU.mult))
                        nc.vector.tensor_tensor(hx[:, :], hx[:, :], W["L1_ln2b"][:, :], ALU.add).then_inc(s_h, 1)
                        dv.wait_ge(s_h, t + 1)
                        dv.wait_ge(s_dn, t + 1)
                        nc.vector.tensor_tensor(s_out[:, at], s_out[:, at], ps_proj[:, 1, 0:D], ALU.add).then_inc(s_out_, 1)
                        dv.wait_ge(s_out_, t + 1)
                    st.restart()

            def pool(po):
                for i in turns(po, "gpsimd", B):
                    for t in range(NT):
                        po.wait_ge(s_var, t + 1)
                        nc.gpsimd.tensor_tensor(rstd[:, 0:1], var[:, 0:1], neghalf[:, 0:1], ALU.pow).then_inc(s_rstd, 1)

            def pe(te):
                for i in turns(te, "tensor", B):
                    for t in range(NT):
                        te.wait_ge(s_h, t + 1)
                        te.transpose(ps_proj[:, 0, 0:P], hx[:, :], ident[:, :]).then_inc(s_tr, 1)
                        te.wait_ge(s_hT, t + 1)
                        for c in range(FC):
                            o = ps_turn[:, 0, c * P:(c + 1) * P]
                            ins = te.matmul(o, W["L1_mw1"][:, c * P:(c + 1) * P], hxT[:, :], start=True, stop=True)
                        ins.then_inc(s_up, 1)
                        te.wait_ge(s_act, t + 1)
                        for c in range(FC):
                            te.matmul(ps_proj[:, 1, 0:D], hT[:, 0, c * P:(c + 1) * P], W["L1_mw2"][:, c, :], start=(c == 0), stop=False)
                        te.matmul(ps_proj[:, 1, 0:D], ones[0:1, :], W["L1_mb2"][:, :], start=False, stop=True).then_inc(s_dn, 1)

            def act(ac):
                st = Steps(ac, act_chain)
                for i in turns(ac, "scalar", B):
                    for t in range(NT):
                        ac.wait_ge(s_tr, t + 1)
                        nc.scalar.activation(hxT[:, :], ps_proj[:, 0, 0:P], ACT.Copy).then_inc(s_hT, 1)
                        ac.wait_ge(s_up, t + 1)
                        for c in range(FC):
                            ins = nc.scalar.activation(hT[:, 0, c * P:(c + 1) * P], ps_turn[:, 0, c * P:(c + 1) * P], ACT.Gelu,
                                                       bias=W["L1_mb1"][:, c:c + 1])
                        ins.then_inc(s_act, 1)
            return Phase(vec, act, pool, pe, s_var, s_out_, B)

        def route_phase(L):
            s_pick = sem(f"{L}_picked")
            s_cnt = sem(f"{L}_counted")
            s_pos = sem(f"{L}_positions")
            s_exp = sem(f"{L}_tile_experts")
            s_sorted = sem(f"{L}_sorted")

            def vec(dv):
                st = Steps(dv, dve_chain)

                def first_best(dst, src):
                    st(nc.vector.tensor_reduce(best[:, :], src, AX.X, ALU.max))
                    st(nc.vector.tensor_tensor(pick8[:, :, :], src, best[:, :, None].broadcast_to([P, NTT, NE]), ALU.is_equal))
                    st(nc.vector.tensor_scalar(pick8[:, :, :], pick8[:, :, :], -100.0, 100.0, ALU.mult, ALU.add))
                    st(nc.vector.tensor_tensor(pick8[:, :, :], pick8[:, :, :], iota8[:, :, :], ALU.add))
                    st(nc.vector.tensor_reduce(dst[:, :], pick8[:, :, :], AX.X, ALU.min))

                def onehot(src):
                    return nc.vector.tensor_tensor(pick8b[:, :, :], iota8[:, :, :], src[:, :, None].broadcast_to([P, NTT, NE]), ALU.is_equal)

                first_best(pickA, gate[:, :, :])
                if L == 0:
                    st(onehot(pickA))
                    st(nc.vector.tensor_scalar(pick8b[:, :, :], pick8b[:, :, :], -3e38, None, ALU.mult))
                    st(nc.vector.tensor_tensor(pick8b[:, :, :], pick8b[:, :, :], gate[:, :, :], ALU.add))
                    first_best(pickB, pick8b[:, :, :])
                    st(nc.vector.tensor_tensor(pickA[:, :], pickA[:, :], pickB[:, :], ALU.max))
                onehot(pickA).then_inc(s_pick, 1)
                dv.wait_ge(s_cnt, 1)
                total = ps_proj[:, 1, 0:NTT * NE].rearrange("p (t e) -> p t e", e=NE)
                st(nc.vector.memset(before_tile[:, 0, :], 0.0))
                for t in range(1, NTT):
                    st(nc.vector.tensor_tensor(before_tile[:, t, :], before_tile[:, t - 1, :], total[:, t - 1, :], ALU.add))
                st(nc.vector.tensor_tensor(count8[:, :], before_tile[:, NTT - 1, :], total[:, NTT - 1, :], ALU.add))
                st(nc.vector.tensor_tensor(tiles16[:, :, :], count8[:, :, None].broadcast_to([P, NE, NTT]),
                                           step128[:, None, :].broadcast_to([P, NE, NTT]), ALU.is_gt))
                st(nc.vector.tensor_reduce(tiles8[:, :], tiles16[:, :, :], AX.X, ALU.add))
                st(nc.vector.memset(first8[:, 0:1], 0.0))
                for e in range(1, NE):
                    st(nc.vector.tensor_tensor(first8[:, e:e + 1], first8[:, e - 1:e], tiles8[:, e - 1:e], ALU.add))
                st(nc.vector.tensor_tensor(last8[:, :], first8[:, :], tiles8[:, :], ALU.add))
                st(nc.vector.tensor_tensor(reached[:, :, :], tile_no[:, :, None].broadcast_to([P, NXT, NE]),
                                           last8[:, None, :].broadcast_to([P, NXT, NE]), ALU.is_ge))
                st(nc.vector.tensor_reduce(expertf[:, :], reached[:, :, :], AX.X, ALU.add))
                nc.vector.tensor_scalar(expert[:, :], expertf[:, :], float(NE - 1), None, ALU.min).then_inc(s_exp, 1)
                st(nc.vector.tensor_scalar(first8[:, :], first8[:, :], float(P), None, ALU.mult))
                st(nc.vector.tensor_tensor(before_tile[:, :, :], before_tile[:, :, :], first8[:, None, :].broadcast_to([P, NTT, NE]), ALU.add))
                st(nc.vector.tensor_tensor(before_tile[:, :, :], before_tile[:, :, :],
                                           ps_proj[:, 0, 0:NTT * NE].rearrange("p (t e) -> p t e", e=NE), ALU.add))
                st(nc.vector.tensor_tensor(before_tile[:, :, :], before_tile[:, :, :], pick8b[:, :, :], ALU.mult))
                st(nc.vector.tensor_reduce(posf[:, :], before_tile[:, :, :], AX.X, ALU.add))
                nc.vector.tensor_copy(pos[:, :], posf[:, :]).then_inc(s_pos, 1)
                st.restart()

            def pe(te):
                te.wait_ge(s_pick, 1)
                one = pick8b[:, :, :].rearrange("p t e -> p (t e)")
                te.matmul(ps_proj[:, 0, 0:NTT * NE], earlier, one, start=True, stop=True)
                te.matmul(ps_proj[:, 1, 0:NTT * NE], ones[:, :], one, start=True, stop=True).then_inc(s_cnt, 1)

            def scatter(po):
                po.wait_ge(s_pos, 1)
                for t in range(NTT):
                    po.indirect_dma_start(out=sorted_x, out_offset=bass.IndirectOffsetOnAxis(ap=pos[:, t:t + 1], axis=0),
                                          in_=xn[:, t * D:(t + 1) * D], in_offset=None).then_inc(s_sorted, 16)
            return vec, pe, scatter, s_exp, s_sorted, s_pos

        def gather_phase(L):
            s_back = sem(f"{L}_back")

            def gather(po):
                for t in range(NTT):
                    po.indirect_dma_start(out=moe[:, t * D:(t + 1) * D], out_offset=None, in_=sorted_y,
                                          in_offset=bass.IndirectOffsetOnAxis(ap=pos[:, t:t + 1], axis=0)).then_inc(s_back, 16)
            return gather, s_back

        def join_phase(L, s_back):
            s_e = sem(f"j{L}_e")
            s_x = sem(f"j{L}_x")
            k = 2.0 if L == 0 else 1.0

            def act(ac):
                ac.wait_ge(s_back, 16 * NTT)
                nc.scalar.activation(xnT[:, :], moe[:, :], ACT.Exp, scale=-k).then_inc(s_e, 1)

            def vec(dv):
                st = Steps(dv, dve_chain)
                dv.wait_ge(s_back, 16 * NTT)
                dv.wait_ge(s_e, 1)
                st(nc.vector.tensor_scalar(xnT[:, :], xnT[:, :], 1.0, None, ALU.add))
                st(nc.vector.reciprocal(xnT[:, :], xnT[:, :]))
                st(nc.vector.scalar_tensor_tensor(out=moe[:, :], in0=moe[:, :], scalar=k, in1=xnT[:, :], op0=ALU.mult, op1=ALU.mult))
                st(nc.vector.tensor_tensor(moe[:, :], moe[:, :], s_out[:, :], ALU.mult))
                nc.vector.tensor_tensor(x[:, :], x[:, :], moe[:, :], ALU.add).then_inc(s_x, 1)
                dv.wait_ge(s_x, 1)
                st.restart()
            return act, vec, s_x

        norm0 = norm_phase(0, None)
        route0_vec, route0_pe, scatter0, experts0, sorted0, _ = route_phase(0)
        attn0 = attention_phase(0)
        gather0, back0 = gather_phase(0)
        join0_act, join0_vec, joined0 = join_phase(0, back0)
        norm1 = norm_phase(1, joined0)
        route1_vec, route1_pe, scatter1, experts1, sorted1, _ = route_phase(1)
        attn1, mlp1 = attention_phase(1), mlp_phase()
        gather1, back1 = gather_phase(1)
        join1_act, join1_vec, joined1 = join_phase(1, back1)
        stored = sem("stored")

        @block.sync
        def _(sp):
            sync_load(sp)
            for ph, experts_known, all_sorted in ((norm0, None, None), (attn0, experts0, sorted0), (norm1, None, None),
                                                  (attn1, experts1, sorted1), (mlp1, None, None)):
                if experts_known is not None:
                    sp.wait_ge(experts_known, 1)
                    sp.wait_ge(all_sorted, 16 * NTT)
                with sp.Fori(0, ph.n) as i:
                    if ph.sync is not None:
                        ph.sync(sp, i)
                    clear_when_met(sp, ph.first, ph.last)
            sp.wait_ge(joined1, 1)
            sp.dma_start(out3, x[:, :].rearrange("p (n d) -> p n d", d=D)).then_inc(stored, 16)
            sp.wait_ge(stored, 16)

        @block.vector
        def _(dv):
            norm0.vec(dv)
            route0_vec(dv)
            attn0.vec(dv)
            join0_vec(dv)
            norm1.vec(dv)
            route1_vec(dv)
            attn1.vec(dv)
            mlp1.vec(dv)
            join1_vec(dv)

        @block.scalar
        def _(ac):
            norm0.act(ac)
            attn0.act(ac)
            join0_act(ac)
            norm1.act(ac)
            attn1.act(ac)
            mlp1.act(ac)
            join1_act(ac)

        @block.gpsimd
        def _(po):
            pool_const(po)
            norm0.pool(po)
            scatter0(po)
            attn0.pool(po)
            gather0(po)
            norm1.pool(po)
            scatter1(po)
            attn1.pool(po)
            gather1(po)
            mlp1.pool(po)

        @block.tensor
        def _(te):
            norm0.pe(te)
            route0_pe(te)
            attn0.pe(te)
            norm1.pe(te)
            route1_pe(te)
            attn1.pe(te)
            mlp1.pe(te)


def bf16_bits(m):
    return (m.astype(np.float32).view(np.uint32) >> 16).astype(np.uint16)


def shape_constants():
    pos = np.arange(T)
    tok = (pos - ROT) % T
    c = {}
    c["ident"] = np.eye(P, dtype=np.float32)
    c["identb"] = bf16_bits(np.eye(P))
    c["iota8"] = np.broadcast_to(np.arange(NE, dtype=np.float32), (P, NTT, NE)).copy()

    def causal(u):
        q, k = 64 * u + np.arange(64), (64 * u - 64 + np.arange(P)) % T
        tq, tk = tok[q][:, None], tok[k][None, :]
        return (tk <= tq) & (tk >= tq - WIN)

    def sided(u):
        q, k = 64 * u + np.arange(64), (64 * u - 32 + np.arange(P)) % T
        end_q = (q < ROT) | (q >= T - 32)
        bad = (k[None, :] < 32) & ((k[None, :] < ROT) != end_q[:, None])
        near = (q < 64) | (q >= T - 32)
        return ~(bad & near[:, None])

    def pair(f, t):
        return np.concatenate([f(2 * t), f(2 * t + 1)])

    def penal(m, n):
        return bf16_bits(np.tile(np.where(m, 0.0, -BIG), (1, n)))

    c["maskq"] = np.stack([penal(pair(causal, 0), 4), penal(pair(causal, 1), 4),
                           penal(pair(sided, 0), 4), penal(pair(sided, 3), 4)], 1)
    c["maskk"] = np.stack([penal(causal(0).T, 8), penal(causal(1).T, 8), penal(causal(2).T, 8),
                           penal(sided(0).T, 8), penal(sided(NU - 1).T, 8)], 1)
    tab = np.zeros((P, 64), np.float32)
    al = np.linspace(0.0, 1.0, 32, dtype=np.float32)
    p = np.arange(P)
    for t in range(NT):
        tab[:, t] = (~pair(causal, t)).sum(1)
        alpha = al[p % 32].copy()
        if t == 0:
            alpha[:ROT], alpha[ROT:32] = 0.0, 1.0
        tab[:, 4 + t] = alpha
        tab[:, 8 + t] = 1 - alpha
    odd = (p // 32) % 2
    for g in range(4):
        tab[:, 12 + g] = np.where((g == odd) | (g == odd + 1), 0, -1e30)
        tab[:, 16 + g] = np.where((g == odd + 1) | (g == odd + 2), 0, -1e30)
        tab[:, 20 + g] = p // 32 == g
        tab[:, 24 + g] = p // 32 == g
    c["tab"] = tab
    c["cnst"] = np.concatenate([np.triu(np.ones((P, P)), 1), np.tile(128.0 * np.arange(NTT), (P, 1)),
                                np.tile(1.0 * np.arange(NXT), (P, 1))], 1).astype(np.float32)
    return c


def laid_out(inp):
    g = {k: np.ascontiguousarray(np.asarray(v)) for k, v in inp.items()}
    stored = [8 * hf + 4 * par + j for hf in range(2) for j in range(4) for par in range(2)]
    cols = np.array([h * HD + e for h in stored for e in range(HD)])
    a = {}
    a["x"] = np.roll(g["L0_attn_x"], ROT, axis=1)
    for L, q, k, v, o in ((0, "w_q", "w_k", "w_v", "w_o"), (1, "wq", "wk", "wv", "wproj")):
        n = f"L{L}_attn_"
        a[f"L{L}_wqk"] = np.concatenate([g[n + q][:, cols], g[n + k][:, cols]], 1)
        bq, bk, bv, bo = ("b_q", "b_k", "b_v", "b_o") if L == 0 else ("bq", "bk", "bv", "bproj")
        a[f"L{L}_bqk"] = np.concatenate([g[n + bq][cols], g[n + bk][cols]])
        a[f"L{L}_wv"], a[f"L{L}_bv"] = g[n + v], g[n + bv]
        a[f"L{L}_wo"], a[f"L{L}_bo"] = g[n + o], g[n + bo]
        f = f"L{L}_ffn_"
        a[f"L{L}_gw"] = g[f + "gate_w"] if L == 0 else g[f + "gate_w"].T
        a[f"L{L}_gb"] = g[f + "gate_b"]
        a[f"L{L}_w1e"] = g[f + "w1"].reshape(NE * P, DF)
        a[f"L{L}_w2e"] = g[f + "w2"].reshape(NE * DF, D)
        a[f"L{L}_b1e"], a[f"L{L}_b2e"] = g[f + "b1"].reshape(NE, FC, P).transpose(0, 2, 1).reshape(NE * P, FC), g[f + "b2"]
    a["L1_eb"] = g["L1_ffn_expert_bias"]
    a["L0_rms"] = np.concatenate([g["L0_attn_rms_q_w"], g["L0_attn_rms_k_w"]])
    for s, n in (("ln1g", "ln1_g"), ("ln1b", "ln1_b"), ("ln2g", "ln2_g"), ("ln2b", "ln2_b"),
                 ("mw1", "w1"), ("mb1", "b1"), ("mw2", "w2"), ("mb2", "b2")):
        a["L1_" + s] = g["L1_attn_" + n]
    a["L1_mb1"] = a["L1_mb1"].reshape(FC, P).T
    a.update(shape_constants())
    return {k: np.ascontiguousarray(v) for k, v in a.items()}


def kernel(**inputs):
    import concourse.bacc as bacc
    from concourse.bass_utils import run_bass_kernel_spmd

    arrays = laid_out(inputs)
    nc = bacc.Bacc("TRN2", target_bir_lowering=False, num_devices=1)
    aps = {n: nc.dram_tensor(f"in_{n}", v.shape, mybir.dt.from_np(v.dtype), kind="ExternalInput").ap()
           for n, v in arrays.items()}
    out = nc.dram_tensor("out", (B, T, D), F32, kind="ExternalOutput").ap()
    block_kernel(nc, aps, out, None)
    r = run_bass_kernel_spmd(nc, [{f"in_{n}": v for n, v in arrays.items()}], core_ids=[0])
    return np.roll(r.results[0]["out"], -ROT, axis=1)
```

```python
from contextlib import ExitStack

import concourse.bass as bass
import numpy as np
from concourse import mybir

F32 = mybir.dt.float32
BF16 = mybir.dt.bfloat16
ALU = mybir.AluOpType
ACT = mybir.ActivationFunctionType
AX = mybir.AxisListType

P = 128
D = 128
B, T = 4, 512
NT = T // P
NTT = B * NT
H, HD = 16, 8
NU = T // 64
NE, DF = 8, 512
FC = DF // P
NXT = NTT + NE
XPT = NXT // B
WIN = 64
WS = 3
EARLY = 4
ROT = 16
SPLIT = 6 * HD
BIG = 1e10
LN_EPS = 1e-5
RMS_EPS = 1.1920929e-07


class Steps:

    def __init__(self, eng, sem):
        self.eng, self.sem, self.n = eng, sem, 0

    def __call__(self, ins):
        self.n += 1
        ins.then_inc(self.sem, 1)
        self.eng.wait_ge(self.sem, self.n)

    def beside(self, ins):
        self.n += 1
        ins.then_inc(self.sem, 1)

    def meet(self):
        self.eng.wait_ge(self.sem, self.n)

    def restart(self):
        self.eng.sem_clear(self.sem)
        self.n = 0


def block_kernel(nc, a, out, dbg):
    with ExitStack() as ctx:
        def sb(name, shape, dt=F32):
            return ctx.enter_context(nc.sbuf_tensor(name, shape, dt))

        def sem(name):
            return ctx.enter_context(nc.semaphore(name))

        arrived = sem("arrived")
        go = {e: sem(f"go_{e}") for e in ("vector", "scalar", "gpsimd", "tensor")}

        class Phase:

            def __init__(self, vec, act, pool, pe, first, last, n, sync=None):
                self.vec, self.act, self.pool, self.pe = vec, act, pool, pe
                self.first, self.last, self.n, self.sync = first, last, n, sync

        def turns(eng, name, n):
            with eng.Fori(0, n) as i:
                yield i
                eng.drain().then_inc(arrived, 1)
                eng.wait_ge(go[name], 1)
                eng.sem_clear(go[name])

        def clear_when_met(sp, first, last):
            sp.wait_ge(arrived, 4)
            sp.sem_clear(range(first.num, last.num + 1))
            sp.sem_clear(arrived)
            for e in go.values():
                sp.sem_inc(e, 1)

        ps_score = ctx.enter_context(nc.psum_tensor("ps_score", [P, 2, 1024], F32))
        ps_turn = ctx.enter_context(nc.psum_tensor("ps_turn", [P, 2, 512], F32))
        ps_proj = ctx.enter_context(nc.psum_tensor("ps_proj", [P, 2, 512], F32))

        x = sb("x", [P, NTT * D])
        xn = sb("xn", [P, NTT * D])
        xnT = sb("xnT", [P, B * T])
        xlT = sb("xlT", [P, B * T])
        s_out = sb("s_out", [P, NTT * D])
        moe = sb("moe", [P, NTT * D])
        gate = sb("gate", [P, NTT, NE])
        ident = sb("ident", [P, P])
        identb = sb("identb", [P, P], BF16)
        ones = sb("ones", [P, P])
        neghalf = sb("neghalf", [P, 256])
        maskq = sb("maskq", [P, 4, 512], BF16)
        maskk = sb("maskk", [P, 5, 512], BF16)
        tab = sb("tab", [P, 64])
        iota8 = sb("iota8", [P, NTT, NE])
        pick8 = sb("pick8", [P, NTT, NE])
        pick8b = sb("pick8b", [P, NTT, NE])
        best = sb("best", [P, NTT])
        pickA = sb("pickA", [P, NTT])
        pickB = sb("pickB", [P, NTT])

        stats = sb("stats", [P, 2 * NT, 6])
        mv = sb("mv", [P, 2 * NT, 2])
        var = sb("var", [P, 2 * NT])
        rstd = sb("rstd", [P, 2 * NT])
        xs = sb("xs", [P, 2, NT * D])
        xl = sb("xl", [P, 2, NT * D])
        xsT = sb("xsT", [P, 2, T])
        xT = sb("xT", [P, 64 + T + 64])
        q4 = sb("q4", [P, NT * H, HD])
        k4 = sb("k4", [P, NT * H, HD])
        sq = sb("sq", [P, NT * H, HD])
        rest = sb("rest", [P, NT * H, HD])
        ss = sb("ss", [P, 2, NT * H])
        rr = sb("rr", [P, 2, NT * H])
        rt = sb("rt", [P, 2, NT * H])
        eq = sb("eq", [P, NT, H, 64], BF16)
        ek = sb("ek", [P, NT, H, 64], BF16)
        qT = sb("qT", [P, 8, T], BF16)
        kT = sb("kT", [P, 8, 64 + T + 64], BF16)
        v = sb("v", [P, NU, H * 36])
        th = sb("th", [P, 2, 1024])
        pT = sb("pT", [P, 2, 1024])
        gm = sb("gm", [P, NT, H * 4])
        tsum = sb("tsum", [P, NT, H])
        inv = sb("inv", [P, NT, H])
        fit = sb("fit", [P, NT, H])
        fits = sb("fits", [P, NT, H])
        sinv = sb("sinv", [P, H])
        shift = sb("shift", [P, NT, H * 4])
        shifts = sb("shifts", [P, NT, H * 4])
        shr = sb("shr", [P, NT, H * 4])
        eA = sb("eA", [P, NT, H, 4])
        eB = sb("eB", [P, NT, H, 4])
        mA = sb("mA", [P, NT * H])
        osb = sb("osb", [P, H * 36])
        cs = sb("cs", [P, H, 4])
        cs2 = sb("cs2", [P, H, 4])
        wtot = sb("wtot", [P, H])
        wtot2 = sb("wtot2", [P, H])
        wpv = sb("wpv", [P, H, 8, 4])
        head = sb("head", [P, D])
        headT = sb("headT", [P, P])
        o1 = sb("o1", [P, D])

        w1 = sb("w1", [P, WS, DF])
        w2 = sb("w2", [P, WS, FC * D])
        b2r = sb("b2r", [P, WS, D])
        b1s = sb("b1s", [P, WS, FC])
        hT = sb("hT", [P, 2, FC * P])
        xg = sb("xg", [P, WS, D])
        xgT = sb("xgT", [P, 2, P])
        ys = sb("ys", [P, 2, D])
        tiles16 = sb("tiles16", [P, NE, NTT])
        before_tile = sb("before_tile", [P, NTT, NE])
        count8 = sb("count8", [P, NE])
        tiles8 = sb("tiles8", [P, NE])
        first8 = sb("first8", [P, NE])
        last8 = sb("last8", [P, NE])
        posf = sb("posf", [P, NTT])
        pos = sb("pos", [P, NTT], mybir.dt.int32)
        reached = sb("reached", [P, NXT, NE])
        expertf = sb("expertf", [P, NXT])
        expert = sb("expert", [P, NXT], mybir.dt.int32)
        cnst = sb("cnst", [P, P + NTT + NXT])
        sorted_x = nc.dram_tensor("sorted_x", (NXT * P, D), F32, kind="Internal").ap()
        sorted_y = nc.dram_tensor("sorted_y", (NXT * P, D), F32, kind="Internal").ap()
        earlier = cnst[:, 0:P]
        step128 = cnst[:, P:P + NTT]
        tile_no = cnst[:, P + NTT:P + NTT + NXT]

        load = sem("load")
        LOADS = [0]

        def fetch(eng, dst, src):
            LOADS[0] += 16
            eng.dma_start(dst, src).then_inc(load, 16)

        W = {}
        for n, shape in (("L0_wqk", [P, 256]), ("L1_wqk", [P, 256]), ("L0_wv", [P, 32]), ("L1_wv", [P, 128]),
                         ("L0_wo", [P, D]), ("L1_wo", [P, D]), ("L0_gw", [P, NE]), ("L1_gw", [P, NE]),
                         ("L1_mw1", [P, DF]), ("L1_mb1", [P, FC])):
            W[n] = sb(n, shape)
        W["L1_mw2"] = sb("L1_mw2", [P, FC, D])
        ROWS = {"L0_bo": D, "L1_bo": D,
                "L0_gb": NE, "L1_gb": NE, "L1_eb": NE}
        for n, k in ROWS.items():
            W[n] = sb(n, [1, k])
        WIDE = {"L0_bqk": 256, "L1_bqk": 256, "L0_bv": 32, "L1_bv": 128, "L0_rms": 16, "L1_ln1g": D, "L1_ln1b": D, "L1_ln2g": D, "L1_ln2b": D, "L1_mb2": D}
        for n, k in WIDE.items():
            W[n] = sb(n, [P, k])
        rmsw = sb("rmsw", [P, 2, HD])
        vbias = sb("vbias", [P, 4, D])

        x3 = a["x"].rearrange("b (t p) d -> p (b t) d", p=P)
        out3 = out.rearrange("b (t p) d -> p (b t) d", p=P)

        block = ctx.enter_context(nc.Block())

        tab_nm = tab[:, 0:4]
        tab_al = tab[:, 4:8]
        tab_al1 = tab[:, 8:12]
        tab_nA = tab[:, 12:16]
        tab_nB = tab[:, 16:20]
        tab_bd = tab[:, 20:24]
        tab_mod = tab[:, 24:28]

        dve_chain = sem("dve_chain")
        act_chain = sem("act_chain")
        pool_chain = sem("pool_chain")

        def sync_load(sp):
            fetch(sp, x[:, :].rearrange("p (n d) -> p n d", d=D), x3)
            for n in ("ident", "identb", "maskq", "maskk", "tab", "iota8", "cnst"):
                t = {"ident": ident, "identb": identb, "maskq": maskq, "maskk": maskk, "tab": tab, "iota8": iota8, "cnst": cnst}[n]
                src = a[n].bitcast(BF16) if n in ("identb", "maskq", "maskk") else a[n]
                fetch(sp, t[tuple(slice(None) for _ in t.shape)], src)
            for n, t in W.items():
                src = a[n]
                if n in ROWS or n in WIDE:
                    src = src.rearrange("(o n) -> o n", o=1)
                if n in WIDE:
                    src = src.broadcast_to([P, WIDE[n]])
                if n == "L1_mw2":
                    src = src.rearrange("(c p) n -> p c n", p=P)
                fetch(sp, t[tuple(slice(None) for _ in t.shape)], src)

        def loaded(eng):
            eng.wait_ge(load, LOADS_ALL)

        LOADS_ALL = 16 * (8 + len(W))

        made = sem("constants_made")
        filled = sem("filled")

        def pool_const(po):
            po.memset(ones[:, :], 1.0).then_inc(made, 1)
            po.memset(neghalf[:, :], -0.5).then_inc(made, 1)
            po.memset(eq[:, :, :, :], 0.0).then_inc(made, 1)
            po.memset(ek[:, :, :, :], 0.0).then_inc(made, 1)
            po.memset(moe[:, :], 0.0).then_inc(made, 1)
            po.wait_ge(made, 5)
            for h in range(2):
                po.dma_start(sorted_x[h * (NXT // 2) * P:(h + 1) * (NXT // 2) * P, :].rearrange("(n p) d -> p n d", p=P),
                             moe[:, 0:NXT // 2 * D].rearrange("p (n d) -> p n d", d=D)).then_inc(filled, 16)
            po.wait_ge(filled, 32)

        def consts(eng):
            eng.wait_ge(made, 5)

        def norm_phase(L, joined):
            s_var = sem(f"{L}_var")
            s_rstd = sem(f"{L}_rstd")
            s_xs = sem(f"{L}_xs")
            s_tr = sem(f"{L}_tr")
            s_xsT = sem(f"{L}_xsT")
            s_xnc = sem(f"{L}_xn_kept")
            s_gp = sem(f"{L}_gp")
            s_gate = sem(f"{L}_gate")
            s_xl = sem(f"{L}_xl")

            def vec(dv):
                st = Steps(dv, dve_chain)
                loaded(dv)
                if joined is not None:
                    dv.wait_ge(joined, B)
                for i in turns(dv, "vector", B // 2):
                    for r in range(1 + (L == 1)):
                        src = [x[:, bass.ds((i * 2 * NT + t) * D, D)] if r == 0 else xs[:, t // NT, t % NT * D:(t % NT + 1) * D]
                               for t in range(2 * NT)]
                        dst = (xs, xl)[r]
                        for t in range(2 * NT):
                            st.beside(nc.vector.bn_stats(stats[:, t, :], src[t]))
                        st.meet()
                        for t in range(2 * NT):
                            st.beside(nc.vector.bn_aggr(mv[:, t, :], stats[:, t, :]))
                        st.meet()
                        nc.vector.tensor_scalar(var[:, :], mv[:, :, 1], LN_EPS, None, ALU.add).then_inc(s_var, 1)
                        dv.wait_ge(s_rstd, r + 1)
                        for h in range(2):
                            for t in range(h * NT, (h + 1) * NT):
                                ins = nc.vector.tensor_scalar(dst[:, h, t % NT * D:(t % NT + 1) * D], src[t], mv[:, t, 0:1],
                                                              rstd[:, t:t + 1], ALU.subtract, ALU.mult)
                                if r == 0 and t % NT == NT - 1:
                                    ins.then_inc(s_xs, 1)
                                else:
                                    st.beside(ins)
                        st.meet()
                        if r == 0:
                            dv.wait_ge(s_xs, 2)
                        else:
                            for h in range(2):
                                x4 = xl[:, h, :].rearrange("p (t d) -> p t d", d=D)
                                st(nc.vector.tensor_tensor(x4, x4, W["L1_ln1g"][:, None, :].broadcast_to([P, NT, D]), ALU.mult))
                                nc.vector.tensor_tensor(x4, x4, W["L1_ln1b"][:, None, :].broadcast_to([P, NT, D]), ALU.add).then_inc(s_xl, 1)
                            dv.wait_ge(s_xl, 2)
                    st.restart()

            def pool(po):
                consts(po)
                for i in turns(po, "gpsimd", B // 2):
                    for r in range(1 + (L == 1)):
                        po.wait_ge(s_var, r + 1)
                        nc.gpsimd.tensor_tensor(rstd[:, :], var[:, :], neghalf[:, 0:2 * NT], ALU.pow).then_inc(s_rstd, 1)
                    for h in range(2):
                        po.wait_ge(s_xs, h + 1)
                        nc.gpsimd.tensor_copy(xn[:, bass.ds((2 * i + h) * (NT * D), NT * D)], xs[:, h, :]).then_inc(s_xnc, 1)

            def pe(te):
                loaded(te)
                consts(te)
                for i in turns(te, "tensor", B // 2):
                    for h in range(2):
                        te.wait_ge(s_xs, h + 1)
                        for t in range(NT):
                            ins = te.transpose(ps_turn[:, h, t * P:(t + 1) * P], xs[:, h, t * D:(t + 1) * D], ident[:, :])
                        ins.then_inc(s_tr, 1)
                    for h in range(2):
                        te.wait_ge(s_xsT, h + 1)
                        for t in range(NT):
                            o = ps_proj[:, h, t * NE:(t + 1) * NE]
                            te.matmul(o, xsT[:, h, t * P:(t + 1) * P], W[f"L{L}_gw"][:, :], start=True, stop=False)
                            if L == 1:
                                te.matmul(o, ones[0:1, :], W["L1_eb"][:, :], start=False, stop=False)
                            ins = te.matmul(o, ones[0:1, :], W[f"L{L}_gb"][:, :], start=False, stop=True)
                        ins.then_inc(s_gp, 1)
                    if L == 1:
                        for h in range(2):
                            te.wait_ge(s_xl, h + 1)
                            for t in range(NT):
                                ins = te.transpose(ps_score[:, h, t * P:(t + 1) * P], xl[:, h, t * D:(t + 1) * D], ident[:, :])
                            ins.then_inc(s_tr, 1)

            def act(ac):
                for i in turns(ac, "scalar", B // 2):
                    for h in range(2):
                        ac.wait_ge(s_tr, h + 1)
                        nc.scalar.activation(xsT[:, h, :], ps_turn[:, h, :], ACT.Copy).then_inc(s_xsT, 1)
                    if L == 0:
                        for h in range(2):
                            nc.scalar.activation(xnT[:, bass.ds((2 * i + h) * T, T)], ps_turn[:, h, :], ACT.Copy).then_inc(s_xsT, 1)
                    for h in range(2):
                        ac.wait_ge(s_gp, h + 1)
                        nc.scalar.activation(
                            gate[:, :, :].rearrange("p n e -> p (n e)")[:, bass.ds((2 * i + h) * (NT * NE), NT * NE)],
                            ps_proj[:, h, 0:NT * NE], ACT.Copy).then_inc(s_gate, 1)
                    if L == 1:
                        for h in range(2):
                            ac.wait_ge(s_tr, h + 3)
                            nc.scalar.activation(xlT[:, bass.ds((2 * i + h) * T, T)], ps_score[:, h, 0:T], ACT.Copy).then_inc(s_xsT, 1)
            return Phase(vec, act, pool, pe, s_var, s_xl, B // 2)

        def attention_phase(L):
            NG = 1 if L == 0 else 4
            NK = SPLIT + 3 * NG
            KOFF = 64 if L == 0 else 32
            NV = 32 if L == 0 else 128
            srcT = xnT if L == 0 else xlT
            s_xT = sem(f"{L}_xT")
            s_qkp = sem(f"{L}_qk_proj")
            s_qk = sem(f"{L}_qk")
            s_vp = sem(f"{L}_v_proj")
            s_v = sem(f"{L}_v")
            s_ms = sem(f"{L}_ms")
            s_rms = sem(f"{L}_rms")
            s_ek = sem(f"{L}_ek")
            s_dup = sem(f"{L}_dup")
            s_eq = sem(f"{L}_eq")
            s_turn = sem(f"{L}_turned")
            s_T = sem(f"{L}_even_turned_kept")
            s_Td = sem(f"{L}_odd_turned_kept")
            s_pad = sem(f"{L}_pad")
            s_sc = sem(f"{L}_scores")
            s_th = sem(f"{L}_tanh")
            s_mx = sem(f"{L}_max")
            s_inv = sem(f"{L}_inv")
            s_sin = sem(f"{L}_suminv")
            s_dif = sem(f"{L}_dif")
            s_cof = sem(f"{L}_cof")
            s_st = sem(f"{L}_shifted")
            s_p = sem(f"{L}_probs")
            s_pv = sem(f"{L}_pv")
            s_hd = sem(f"{L}_head")
            s_osb = sem(f"{L}_osb")
            s_hT = sem(f"{L}_headT")
            s_hTs = sem(f"{L}_headTs")
            s_ew = [sem(f"{L}_expert_in{k}") for k in range(WS)]
            s_ex = sem(f"{L}_expert_xT")
            s_exs = sem(f"{L}_expert_xT_kept")
            s_eu = sem(f"{L}_expert_up")
            s_eh = sem(f"{L}_expert_hidden")
            s_ed = sem(f"{L}_expert_down")
            s_ec = sem(f"{L}_expert_copied")
            s_ey = sem(f"{L}_expert_y")
            s_es = [sem(f"{L}_expert_out{k}") for k in range(2)]
            s_op = sem(f"{L}_oproj")
            s_o = sem(f"{L}_o")

            def slot(n):
                return ps_turn[:, :, :].rearrange("p a b -> p (a b)") if n % 3 == 2 else ps_score[:, n % 3, :]

            e_w1, e_w2, e_b1, e_b2 = a[f"L{L}_w1e"], a[f"L{L}_w2e"], a[f"L{L}_b1e"], a[f"L{L}_b2e"]

            def sync(sp, i):
                for j in range(XPT + WS):
                    if j >= WS:
                        t = j - WS
                        sp.wait_ge(s_ey, t + 1)
                        sp.dma_start(sorted_y[bass.ds((i * XPT + t) * P, P), :], ys[:, t % 2, :]).then_inc(s_es[t % 2], 16)
                    if j < XPT:
                        k = j % WS
                        ex = sp.value_load(expert[0:1, bass.ds(i * XPT + j, 1)], min_val=0, max_val=NE - 1)
                        sp.dma_start(xg[:, k, :], sorted_x[bass.ds((i * XPT + j) * P, P), :]).then_inc(s_ew[k], 16)
                        sp.dma_start(w1[:, k, :], e_w1[bass.ds(ex * P, P), :]).then_inc(s_ew[k], 16)
                        sp.dma_start(w2[:, k, :].rearrange("p (c n) -> p c n", c=FC),
                                     e_w2[bass.ds(ex * DF, DF), :].rearrange("(c p) n -> p c n", p=P)).then_inc(s_ew[k], 16)
                        sp.dma_start(b1s[:, k, :], e_b1[bass.ds(ex * P, P), :]).then_inc(s_ew[k], 16)
                        sp.dma_start(b2r[:, k, :], e_b2[bass.ds(ex, 1), :].broadcast_to([P, D])).then_inc(s_ew[k], 16)
                for k in range(2):
                    sp.wait_ge(s_es[k], 16 * (XPT // 2))

            def pool(po):
                for i in turns(po, "gpsimd", B):
                    for j in range(XPT):
                        po.wait_ge(s_ec, j + 1)
                        nc.gpsimd.tensor_tensor(ys[:, j % 2, :], ys[:, j % 2, :], b2r[:, j % WS, :], ALU.add).then_inc(s_ey, 1)

            def vec(dv):
                st = Steps(dv, dve_chain)
                ekv = ek[:, :, :, :].rearrange("p t h r -> p (t h) r")
                eqv = eq[:, :, :, :].rearrange("p t h r -> p (t h) r")
                vv = v[:, :, 0:H * 36].rearrange("p u (h g e) -> p u h g e", g=4, e=9)
                if L == 0:
                    consts(dv)
                    st(nc.vector.memset(ekv[:, :, SPLIT:SPLIT + 3], 1.0))
                    st(nc.vector.memset(v[:, :, 0:36].rearrange("p u (h e) -> p u h e", e=9)[:, :, :, 8], 1.0))
                    st(nc.vector.tensor_scalar(rmsw[:, 0, :], W["L0_rms"][:, 0:8], float(1 / np.sqrt(np.float32(HD))), None, ALU.mult))
                    st(nc.vector.tensor_copy(rmsw[:, 1, :], W["L0_rms"][:, 8:16]))
                else:
                    for s in range(3):
                        st(nc.vector.tensor_copy(ekv[:, :, SPLIT + 4 * s:SPLIT + 4 * s + 4],
                                                 tab_mod[:, None, :].broadcast_to([P, NT * H, 4])))
                    for g in range(4):
                        st(nc.vector.tensor_scalar(vbias[:, g, :], W["L1_bv"][:, :], tab_bd[:, g:g + 1], None, ALU.mult))
                    for u in range(NU):
                        st(nc.vector.tensor_copy(vv[:, u, :, :, 8], tab_bd[:, None, :].broadcast_to([P, H, 4])))
                st.restart()

                def keep_odd(n, dst):
                    dv.wait_ge(s_turn, n + 1)
                    nc.vector.tensor_copy(dst, ps_turn[:, 1, :].bitcast(BF16).rearrange("p (r k) -> p r k", k=P)).then_inc(s_Td, 1)

                def split_q(st, i, n):
                    st(nc.vector.tensor_copy(eqv[:, :, 0:24].rearrange("p h (c e) -> p h c e", c=3),
                                             q4[:, :, None, :].broadcast_to([P, NT * H, 3, HD])))
                    st(nc.vector.tensor_tensor(rest[:, :, :], q4[:, :, :], eqv[:, :, 0:8], ALU.subtract))
                    st(nc.vector.tensor_copy(eqv[:, :, 24:40].rearrange("p h (c e) -> p h c e", c=2),
                                             rest[:, :, None, :].broadcast_to([P, NT * H, 2, HD])))
                    nc.vector.tensor_tensor(eqv[:, :, 40:48], rest[:, :, :], eqv[:, :, 24:32], ALU.subtract).then_inc(s_eq, 1)
                    dv.wait_ge(s_eq, n)

                for i in turns(dv, "vector", B):
                    nc.vector.tensor_copy(xT[:, 64:64 + T], srcT[:, bass.ds(i * T, T)]).then_inc(s_xT, 1)
                    nc.vector.tensor_copy(xT[:, 0:64], srcT[:, bass.ds(i * T + T - 64, 64)]).then_inc(s_xT, 1)
                    nc.vector.tensor_copy(xT[:, 64 + T:128 + T], srcT[:, bass.ds(i * T, 64)]).then_inc(s_xT, 1)
                    for c in range(2):
                        dv.wait_ge(s_vp, c + 1)
                        if L == 0:
                            for u in range(4):
                                ins = nc.vector.tensor_tensor(
                                    v[:, 4 * c + u, 0:36].rearrange("p (h e) -> p h e", e=9)[:, :, 0:8],
                                    ps_proj[:, c, 32 * u:32 * u + 32].rearrange("p (h e) -> p h e", e=8),
                                    W["L0_bv"][:, :].rearrange("p (h e) -> p h e", e=8), ALU.add)
                            ins.then_inc(s_v, 1)
                        else:
                            for u in range(4):
                                o = ps_proj[:, c, u * 128:(u + 1) * 128].rearrange("p (h e) -> p h e", e=8)
                                for g in range(4):
                                    ins = nc.vector.scalar_tensor_tensor(
                                        out=vv[:, 4 * c + u, :, g, 0:8], in0=o, scalar=tab_bd[:, g:g + 1],
                                        in1=vbias[:, g, :].rearrange("p (h e) -> p h e", e=8), op0=ALU.mult, op1=ALU.add)
                            ins.then_inc(s_v, 1)
                    for t in range(NT):
                        dv.wait_ge(s_qkp, t + 1)
                        for z, m in ((q4, 0), (k4, 128)):
                            nc.vector.tensor_tensor(z[:, t * H:(t + 1) * H, :].rearrange("p h e -> p (h e)"),
                                                    ps_proj[:, t % 2, m:m + 128], W[f"L{L}_bqk"][:, m:m + 128],
                                                    ALU.add).then_inc(s_qk, 1)
                    dv.wait_ge(s_qk, 2 * NT)
                    if L == 0:
                        for z, m in ((q4, 0), (k4, 1)):
                            st(nc.vector.tensor_tensor(sq[:, :, :], z[:, :, :], z[:, :, :], ALU.mult))
                            st(nc.vector.tensor_reduce(ss[:, m, :], sq[:, :, :], AX.X, ALU.add))
                        nc.vector.tensor_scalar(ss[:, :, :], ss[:, :, :], 1.0 / HD, RMS_EPS, ALU.mult, ALU.add).then_inc(s_ms, 1)
                        dv.wait_ge(s_rms, 1)
                        st(nc.vector.reciprocal(rr[:, :, :], rr[:, :, :]))
                        st(nc.vector.tensor_tensor(rt[:, :, :], rr[:, :, :], rr[:, :, :], ALU.mult))
                        st(nc.vector.tensor_tensor(rt[:, :, :], rt[:, :, :], ss[:, :, :], ALU.mult))
                        st(nc.vector.tensor_scalar(rt[:, :, :], rt[:, :, :], -0.5, 1.5, ALU.mult, ALU.add))
                        st(nc.vector.tensor_tensor(rr[:, :, :], rr[:, :, :], rt[:, :, :], ALU.mult))
                        for z, m in ((q4, 0), (k4, 1)):
                            st(nc.vector.tensor_tensor(z[:, :, :], z[:, :, :], rr[:, m, :, None].broadcast_to([P, NT * H, HD]), ALU.mult))
                            st(nc.vector.tensor_tensor(z[:, :, :], z[:, :, :], rmsw[:, m:m + 1, :].broadcast_to([P, NT * H, HD]), ALU.mult))
                    else:
                        st(nc.vector.tensor_scalar(q4[:, :, :], q4[:, :, :], float(HD) ** -0.5, None, ALU.mult))
                    st(nc.vector.tensor_copy(ekv[:, :, 0:8], k4[:, :, :]))
                    st(nc.vector.tensor_tensor(rest[:, :, :], k4[:, :, :], ekv[:, :, 0:8], ALU.subtract))
                    st(nc.vector.tensor_copy(ekv[:, :, 8:16], rest[:, :, :]))
                    nc.vector.tensor_tensor(ekv[:, :, 16:24], rest[:, :, :], ekv[:, :, 8:16], ALU.subtract).then_inc(s_ek, 1)
                    nc.vector.tensor_copy(ekv[:, :, 24:40], ekv[:, :, 0:16]).then_inc(s_dup, 1)
                    nc.vector.tensor_copy(ekv[:, :, 40:48], ekv[:, :, 0:8]).then_inc(s_dup, 1)
                    split_q(st, i, 1)
                    for t in range(1, NT, 2):
                        keep_odd(t, kT[:, :, 64 + t * P:64 + (t + 1) * P])
                    dv.wait_ge(s_T, NT // 2)
                    dv.wait_ge(s_Td, NT // 2)
                    nc.vector.tensor_copy(kT[:, :, 0:64], kT[:, :, T:T + 64]).then_inc(s_pad, 1)
                    nc.vector.tensor_copy(kT[:, :, 64 + T:128 + T], kT[:, :, 64:128]).then_inc(s_pad, 1)
                    for t in range(1, NT, 2):
                        keep_odd(NT + t, qT[:, :, t * P:(t + 1) * P])
                    for t in range(NT):
                        for hf in range(2):
                            n = 2 * t + hf
                            src = slot(n)
                            if L == 0:
                                dv.wait_ge(s_th, n + 1)
                                st(nc.vector.tensor_reduce(tsum[:, t, 8 * hf:8 * hf + 8],
                                                           th[:, n % 2, :].rearrange("p (h k) -> p h k", k=128), AX.X, ALU.add))
                                nc.vector.tensor_reduce(gm[:, t, 8 * hf:8 * hf + 8],
                                                                src.rearrange("p (h k) -> p h k", k=128), AX.X, ALU.max).then_inc(s_mx, 1)
                            else:
                                dv.wait_ge(s_sc, n + 1)
                                nc.vector.tensor_reduce(gm[:, t, 32 * hf:32 * hf + 32],
                                                                src.rearrange("p (h k) -> p h k", k=32), AX.X, ALU.max).then_inc(s_mx, 1)
                    dv.wait_ge(s_mx, 2 * NT)
                    if L == 0:
                        for t in range(NT):
                            st(nc.vector.tensor_scalar(inv[:, t, :], tsum[:, t, :], tab_nm[:, t:t + 1], 1.0 / (2 * T), ALU.add, ALU.mult))
                        st(nc.vector.tensor_scalar(inv[:, :, :], inv[:, :, :], 1.0, None, ALU.add))
                        nc.vector.reciprocal(inv[:, :, :], inv[:, :, :]).then_inc(s_inv, 1)
                        dv.wait_ge(s_sin, 1)
                        st(nc.vector.tensor_reduce(sinv[:, :], ps_proj[:, 0, 0:NT * H].rearrange("p (t h) -> p h t", h=H), AX.X, ALU.add))
                        st(nc.vector.reciprocal(sinv[:, :], sinv[:, :]))
                        st(nc.vector.tensor_tensor(fit[:, :, :], inv[:, :, :], sinv[:, None, :].broadcast_to([P, NT, H]), ALU.mult))
                        st(nc.vector.scalar_tensor_tensor(out=shift[:, :, 0:H], in0=gm[:, :, 0:H], scalar=-1.0, in1=fit[:, :, :],
                                                          op0=ALU.mult, op1=ALU.mult))
                        for par in range(2):
                            st(nc.vector.tensor_copy(
                                fits[:, :, :].rearrange("p t (f j a) -> p (t f) j a", f=2, a=2)[:, :, :, par],
                                fit[:, :, :].rearrange("p t (f a j) -> p (t f) a j", f=2, a=2)[:, :, par, :]))
                            st(nc.vector.tensor_copy(
                                shifts[:, :, 0:H].rearrange("p t (f j a) -> p t f j a", f=2, a=2)[:, :, :, :, par],
                                shift[:, :, 0:H].rearrange("p t (f a j) -> p t f a j", f=2, a=2)[:, :, :, par, :]))
                        st(nc.vector.tensor_tensor(q4[:, :, :], q4[:, :, :], fits[:, :, :].rearrange("p t h -> p (t h)")[:, :, None].broadcast_to([P, NT * H, HD]), ALU.mult))
                        rows = [shifts[:, :, 0:H]]
                    else:
                        g3 = gm[:, :, :].rearrange("p t (h g) -> p (t h) g", g=4)
                        for n, (e_, nm) in enumerate(((eA, tab_nA), (eB, tab_nB))):
                            e3 = e_[:, :, :, :].rearrange("p t h g -> p (t h) g")
                            st(nc.vector.tensor_tensor(e3, g3, nm[:, None, :].broadcast_to([P, NT * H, 4]), ALU.add))
                            st(nc.vector.tensor_reduce(mA[:, :], e3, AX.X, ALU.max))
                            nc.vector.tensor_tensor(e3, e3, mA[:, :, None].broadcast_to([P, NT * H, 4]), ALU.subtract).then_inc(s_dif, 1)
                            dv.wait_ge(s_dif, n + 1)
                        for par in range(2):
                            for f in range(2):
                                for blk, base in ((0, 3), (1, 1)):
                                    sp_ = slice(64 * blk, 64 * blk + 64)
                                    dst = shifts[sp_, :, :].rearrange("p t (f j a g) -> p t f j a g", f=2, a=2, g=4)[:, :, f, :, par, :]
                                    src = gm[sp_, :, :].rearrange("p t (f a j g) -> p t f a j g", f=2, a=2, g=4)[:, :, f, par, :, :]
                                    k = 4 - base
                                    st(nc.vector.tensor_scalar(dst[:, :, :, base:4], src[:, :, :, 0:k], -1.0, None, ALU.mult))
                                    st(nc.vector.tensor_scalar(dst[:, :, :, 0:base], src[:, :, :, k:4], -1.0, None, ALU.mult))
                    sh = shifts[:, :, 0:H * NG].rearrange("p t (h g) -> p t h g", g=NG)
                    r3 = shr[:, :, 0:H * NG].rearrange("p t (h g) -> p t h g", g=NG)
                    part = [eq[:, :, :, SPLIT + NG * s:SPLIT + NG * (s + 1)] for s in range(3)]
                    dv.wait_ge(s_turn, 2 * NT)
                    st(nc.vector.tensor_copy(part[0], sh))
                    st(nc.vector.tensor_tensor(r3, sh, part[0], ALU.subtract))
                    st(nc.vector.tensor_copy(part[1], r3))
                    st(nc.vector.tensor_tensor(part[2], r3, part[1], ALU.subtract))
                    split_q(st, i, 2)
                    for t in range(1, NT, 2):
                        keep_odd(2 * NT + t, qT[:, :, t * P:(t + 1) * P])
                    for t in range(NT):
                        dv.wait_ge(s_pv, 2 * t + 2)
                        if L == 0:
                            o = ps_turn[:, 0, 0:H * 9].rearrange("p (h e) -> p h e", e=9)
                            st(nc.vector.reciprocal(wtot[:, :], o[:, :, 8]))
                            if t > 0:
                                dv.wait_ge(s_hT, t)
                            nc.vector.tensor_tensor(head[:, :].rearrange("p (h e) -> p h e", e=8), o[:, :, 0:8],
                                                            wtot[:, :, None].broadcast_to([P, H, 8]), ALU.mult).then_inc(s_hd, 1)
                        else:
                            if t == 0:
                                dv.wait_ge(s_cof, 2)
                            st(nc.vector.tensor_copy(osb[:, 0:288], ps_turn[:, 0, 0:288]))
                            nc.vector.tensor_copy(osb[:, 288:576], ps_turn[:, 1, 0:288]).then_inc(s_osb, 1)
                            dv.wait_ge(s_osb, t + 1)
                            o = osb[:, :].rearrange("p (h g e) -> p h g e", g=4, e=9)
                            for n, (e_, al, c_, w_) in enumerate(((eA, tab_al1, cs, wtot), (eB, tab_al, cs2, wtot2))):
                                st(nc.vector.tensor_tensor(c_[:, :, :], e_[:, t, :, :], o[:, :, :, 8], ALU.mult))
                                st(nc.vector.tensor_reduce(w_[:, :], c_[:, :, :], AX.X, ALU.add))
                                st(nc.vector.reciprocal(w_[:, :], w_[:, :]))
                                st(nc.vector.tensor_scalar(w_[:, :], w_[:, :], al[:, t:t + 1], None, ALU.mult))
                                st(nc.vector.tensor_tensor(c_[:, :, :], e_[:, t, :, :], w_[:, :, None].broadcast_to([P, H, 4]), ALU.mult))
                            st(nc.vector.tensor_tensor(cs[:, :, :], cs[:, :, :], cs2[:, :, :], ALU.add))
                            st(nc.vector.tensor_tensor(wpv[:, :, :, :].rearrange("p h e g -> p h g e"), o[:, :, :, 0:8],
                                                       cs[:, :, :, None].broadcast_to([P, H, 4, 8]), ALU.mult))
                            if t > 0:
                                dv.wait_ge(s_hT, t)
                            nc.vector.tensor_reduce(head[:, :], wpv[:, :, :, :].rearrange("p h e g -> p (h e) g"), AX.X, ALU.add).then_inc(s_hd, 1)
                        dv.wait_ge(s_hd, t + 1)
                    st.restart()

            def pe(te):
                for i in turns(te, "tensor", B):
                    te.wait_ge(s_xT, 3)
                    for c in range(2):
                        for u in range(4):
                            p0 = 64 + 64 * (4 * c + u) - KOFF
                            o = ps_proj[:, c, u * NV:(u + 1) * NV]
                            ins = te.matmul(o, xT[:, p0:p0 + P], W[f"L{L}_wv"][:, :], start=True, stop=True)
                        ins.then_inc(s_vp, 1)
                    for t in range(NT):
                        if t < 2:
                            te.wait_ge(s_v, t + 1)
                        else:
                            te.wait_ge(s_qk, 2 * (t - 1))
                        o = ps_proj[:, t % 2, 0:256]
                        te.matmul(o, xT[:, 64 + t * P:64 + (t + 1) * P], W[f"L{L}_wqk"][:, :],
                                  start=True, stop=True).then_inc(s_qkp, 1)

                    def turn(src, n, t):
                        if n >= 2:
                            te.wait_ge((s_T, s_Td)[n % 2], n // 2)
                        dst = ps_turn[:, n % 2, :].bitcast(BF16)
                        for pr in range(8):
                            ins = te.transpose(dst[:, pr * P:(pr + 1) * P],
                                               src[:, t, 2 * pr:2 * pr + 2, :].rearrange("p h r -> p (h r)"), identb[:, :])
                        ins.then_inc(s_turn, 1)

                    def expert_up(j):
                        k = j % 2
                        te.wait_ge(s_ew[j % WS], 80 * (j // WS + 1))
                        if j >= 2:
                            te.wait_ge(s_ec, j - 1)
                        te.transpose(ps_score[:, k, 512:640], xg[:, j % WS, :], ident[:, :]).then_inc(s_ex, 1)
                        te.wait_ge(s_exs, j + 1)
                        for c in range(FC):
                            ins = te.matmul(ps_score[:, k, c * P:(c + 1) * P], w1[:, j % WS, c * P:(c + 1) * P], xgT[:, k, :],
                                            start=True, stop=True)
                        ins.then_inc(s_eu, 1)

                    def expert_down(j):
                        k = j % 2
                        te.wait_ge(s_eh, j + 1)
                        for c in range(FC):
                            ins = te.matmul(ps_score[:, k, 512:640], hT[:, k, c * P:(c + 1) * P], w2[:, j % WS, c * D:(c + 1) * D],
                                            start=(c == 0), stop=(c == FC - 1))
                        ins.then_inc(s_ed, 1)

                    for j in range(EARLY):
                        expert_up(j)
                        if j >= 1:
                            expert_down(j - 1)
                    expert_down(EARLY - 1)
                    te.wait_ge(s_ek, 1)
                    te.wait_ge(s_dup, 2)
                    for t in range(NT):
                        turn(ek, t, t)
                    te.wait_ge(s_eq, 1)
                    for t in range(NT):
                        turn(eq, NT + t, t)
                    te.wait_ge(s_pad, 2)
                    te.wait_ge(s_T, NT)
                    te.wait_ge(s_Td, NT)
                    for t in range(NT):
                        for hf in range(2):
                            n = 2 * t + hf
                            if n == 0:
                                te.wait_ge(s_ec, EARLY)
                            if n >= 3:
                                te.wait_ge(s_mx, n - 2)
                            bank = [slot(n)[:, 512 * par:512 * par + 512] for par in range(2)]
                            m = {0: {0: 0, 1: 1, 2: 1, 3: 1}, 1: {0: 2, 3: 3}}[L].get(t)
                            if m is not None:
                                for par in range(2):
                                    te.matmul(bank[par], identb[:, :], maskq[:, m, :], start=True, stop=False, skip_group_check=True)
                            for blk in range(2):
                                for j in range(4):
                                    for par in range(2):
                                        q0 = t * P + 64 * blk
                                        ins = te.matmul(bank[par][64 * blk:64 * blk + 64, j * P:(j + 1) * P],
                                                        qT[64 * par:64 * par + SPLIT, 4 * hf + j, q0:q0 + 64],
                                                        kT[64 * par:64 * par + SPLIT, 4 * hf + j, 64 + q0 - KOFF:64 + q0 - KOFF + P],
                                                        start=m is None, stop=True, skip_group_check=True)
                            ins.then_inc(s_sc, 1)
                    te.wait_ge(s_mx, 2 * NT)
                    expert_up(EARLY)
                    if L == 0:
                        te.wait_ge(s_inv, 1)
                        te.matmul(ps_proj[:, 0, 0:NT * H], ones[:, :], inv[:, :, :].rearrange("p t h -> p (t h)"), start=True, stop=True).then_inc(s_sin, 1)
                    for j in range(EARLY + 1, XPT):
                        expert_up(j)
                        expert_down(j - 1)
                    expert_down(XPT - 1)
                    te.wait_ge(s_eq, 2)
                    for t in range(NT):
                        turn(eq, 2 * NT + t, t)
                    te.wait_ge(s_T, 3 * NT // 2)
                    te.wait_ge(s_Td, 3 * NT // 2)
                    te.wait_ge(s_ec, XPT)

                    def probs(u):
                        if u >= 2:
                            te.wait_ge(s_p, u - 1)
                        bank = [ps_score[:, u % 2, 512 * par:512 * par + 512] for par in range(2)]
                        m = ({0: 0, 1: 1} if L == 0 else {0: 3, NU - 1: 4}).get(u, 2 if L == 0 else None)
                        if m is not None:
                            for par in range(2):
                                te.matmul(bank[par], identb[:, :], maskk[:, m, :], start=True, stop=False, skip_group_check=True)
                        for pr in range(8):
                            for par in range(2):
                                k0 = 64 + 64 * u - KOFF
                                ins = te.matmul(bank[par][:, pr * 64:pr * 64 + 64],
                                                kT[64 * par:64 * par + NK, pr, k0:k0 + P],
                                                qT[64 * par:64 * par + NK, pr, 64 * u:64 * u + 64],
                                                start=m is None, stop=True, skip_group_check=True)
                        ins.then_inc(s_st, 1)

                    def weigh(u):
                        te.wait_ge(s_p, u + 1)
                        t, blk = u // 2, u % 2
                        if blk == 0 and t >= 1:
                            te.wait_ge((s_hd if L == 0 else s_osb), t)
                        for h in range(H):
                            hf, par, j = h // 8, h // 4 % 2, h % 4
                            w_ = pT[:, u % 2, par * 512 + (4 * hf + j) * 64:par * 512 + (4 * hf + j) * 64 + 64]
                            if L == 0:
                                o = ps_turn[64 * blk:64 * blk + 64, 0, 9 * h:9 * h + 9]
                                r = v[:, u, 9 * (h // 4):9 * (h // 4) + 9]
                            else:
                                o = ps_turn[64 * blk:64 * blk + 64, hf, 36 * (h % 8):36 * (h % 8) + 36]
                                r = v[:, u, 36 * h:36 * h + 36]
                            ins = te.matmul(o, w_, r, start=True, stop=True)
                        ins.then_inc(s_pv, 1)

                    def project(t):
                        te.wait_ge(s_hd, t + 1)
                        if t >= 1:
                            te.wait_ge(s_o, t)
                        te_ins = te.transpose(ps_proj[:, 0, 0:P], head[:, :], ident[:, :])
                        te_ins.then_inc(s_hT, 1)
                        te.wait_ge(s_hTs, t + 1)
                        te.matmul(ps_proj[:, 1, 0:D], headT[:, :], W[f"L{L}_wo"][:, :], start=True, stop=False)
                        te.matmul(ps_proj[:, 1, 0:D], ones[0:1, :], W[f"L{L}_bo"][:, :], start=False, stop=True).then_inc(s_op, 1)

                    probs(0)
                    for u in range(NU):
                        if u + 1 < NU:
                            probs(u + 1)
                        if u == 0:
                            te.wait_ge(s_v, 2)
                        weigh(u)
                        if u % 2 == 1 and u >= 3:
                            project(u // 2 - 1)
                    project(NT - 1)

            def act(ac):
                for i in turns(ac, "scalar", B):
                    if L == 0:
                        ac.wait_ge(s_ms, 1)
                        nc.scalar.activation(rr[:, :, :], ss[:, :, :], ACT.Sqrt).then_inc(s_rms, 1)

                    def expert_hidden(j):
                        k = j % 2
                        ac.wait_ge(s_ex, j + 1)
                        nc.scalar.activation(xgT[:, k, :], ps_score[:, k, 512:640], ACT.Copy).then_inc(s_exs, 1)
                        ac.wait_ge(s_eu, j + 1)
                        for c in range(FC):
                            ins = nc.scalar.activation(hT[:, k, c * P:(c + 1) * P], ps_score[:, k, c * P:(c + 1) * P],
                                                       ACT.Gelu if L == 0 else ACT.Relu, bias=b1s[:, j % WS, c:c + 1])
                        ins.then_inc(s_eh, 1)

                    def expert_result(j):
                        ac.wait_ge(s_ed, j + 1)
                        if j >= 2:
                            ac.wait_ge(s_es[j % 2], 16 * (j // 2))
                        nc.scalar.activation(ys[:, j % 2, :], ps_score[:, j % 2, 512:640], ACT.Copy).then_inc(s_ec, 1)

                    for j in range(EARLY):
                        expert_hidden(j)
                        if j >= 1:
                            expert_result(j - 1)
                    expert_result(EARLY - 1)

                    def keep(n, dst):
                        ac.wait_ge(s_turn, n + 1)
                        nc.scalar.activation(dst, ps_turn[:, n % 2, :].bitcast(BF16).rearrange("p (r k) -> p r k", k=P), ACT.Copy).then_inc(s_T, 1)

                    for t in range(0, NT, 2):
                        keep(t, kT[:, :, 64 + t * P:64 + (t + 1) * P])
                    for t in range(0, NT, 2):
                        keep(NT + t, qT[:, :, t * P:(t + 1) * P])
                    if L == 0:
                        for n in range(2 * NT):
                            ac.wait_ge(s_sc, n + 1)
                            if n - 1 > 0:
                                ac.wait_ge(s_mx, n - 1)
                            nc.scalar.activation(th[:, n % 2, :], slot(n), ACT.Tanh, scale=0.5).then_inc(s_th, 1)
                    for j in range(EARLY, XPT):
                        expert_hidden(j)
                        if j > EARLY:
                            expert_result(j - 1)
                    expert_result(XPT - 1)
                    if L == 1:
                        for n, e_ in enumerate((eA, eB)):
                            ac.wait_ge(s_dif, n + 1)
                            nc.scalar.activation(e_[:, :, :, :], e_[:, :, :, :], ACT.Exp).then_inc(s_cof, 1)
                    for t in range(0, NT, 2):
                        keep(2 * NT + t, qT[:, :, t * P:(t + 1) * P])

                    def finish(t):
                        ac.wait_ge(s_hT, t + 1)
                        if t > 0:
                            ac.wait_ge(s_op, t)
                        nc.scalar.activation(headT[:, :], ps_proj[:, 0, 0:P], ACT.Copy).then_inc(s_hTs, 1)
                        ac.wait_ge(s_op, t + 1)
                        nc.scalar.activation(s_out[:, bass.ds((i * NT + t) * D, D)], ps_proj[:, 1, 0:D], ACT.Copy).then_inc(s_o, 1)

                    for u in range(NU):
                        ac.wait_ge(s_st, u + 1)
                        if u - 1 > 0:
                            ac.wait_ge(s_pv, u - 1)
                        nc.scalar.activation(pT[:, u % 2, :], ps_score[:, u % 2, :], ACT.Exp).then_inc(s_p, 1)
                        if u % 2 == 0 and u >= 4:
                            finish(u // 2 - 2)
                    finish(NT - 2)
                    finish(NT - 1)
            return Phase(vec, act, pool, pe, s_xT, s_o, B, sync)

        def mlp_phase():
            s_var = sem("m_var")
            s_rstd = sem("m_rstd")
            s_h = sem("m_h")
            s_tr = sem("m_tr")
            s_hT = sem("m_hT")
            s_up = sem("m_up")
            s_act = sem("m_act")
            s_dn = sem("m_dn")
            s_out_ = sem("m_out")
            hx = xnT[:, 0:2 * NT * D].rearrange("p (h n) -> p h n", h=2)
            hxT = xlT[:, 0:2 * T].rearrange("p (h n) -> p h n", h=2)
            hidden = [b[:, :, :].rearrange("p a (b n) -> p (a b) n", n=T) for b in (th, pT)]

            def vec(dv):
                st = Steps(dv, dve_chain)
                for i in turns(dv, "vector", B // 2):
                    both = bass.ds(i * (2 * NT * D), 2 * NT * D)
                    tile = [s_out[:, bass.ds((i * 2 * NT + t) * D, D)] for t in range(2 * NT)]
                    st(nc.vector.tensor_tensor(s_out[:, both], s_out[:, both], xn[:, both], ALU.add))
                    for t in range(2 * NT):
                        st.beside(nc.vector.bn_stats(stats[:, t, :], tile[t]))
                    st.meet()
                    for t in range(2 * NT):
                        st.beside(nc.vector.bn_aggr(mv[:, t, :], stats[:, t, :]))
                    st.meet()
                    nc.vector.tensor_scalar(var[:, :], mv[:, :, 1], LN_EPS, None, ALU.add).then_inc(s_var, 1)
                    dv.wait_ge(s_rstd, 1)
                    for t in range(2 * NT):
                        st.beside(nc.vector.tensor_scalar(hx[:, t // NT, t % NT * D:(t % NT + 1) * D], tile[t], mv[:, t, 0:1],
                                                          rstd[:, t:t + 1], ALU.subtract, ALU.mult))
                    st.meet()
                    for h in range(2):
                        h4 = hx[:, h, :].rearrange("p (t d) -> p t d", d=D)
                        st(nc.vector.tensor_tensor(h4, h4, W["L1_ln2g"][:, None, :].broadcast_to([P, NT, D]), ALU.mult))
                        nc.vector.tensor_tensor(h4, h4, W["L1_ln2b"][:, None, :].broadcast_to([P, NT, D]), ALU.add).then_inc(s_h, 1)
                    s4 = s_out[:, both].rearrange("p (t d) -> p t d", d=D)
                    st(nc.vector.tensor_tensor(s4, s4, W["L1_mb2"][:, None, :].broadcast_to([P, 2 * NT, D]), ALU.add))
                    for h in range(2):
                        dv.wait_ge(s_dn, h + 1)
                        at = bass.ds((i * 2 + h) * (NT * D), NT * D)
                        nc.vector.tensor_tensor(s_out[:, at], s_out[:, at], ps_proj[:, h, :], ALU.add).then_inc(s_out_, 1)
                    dv.wait_ge(s_out_, 2)
                    st.restart()

            def pool(po):
                for i in turns(po, "gpsimd", B // 2):
                    po.wait_ge(s_var, 1)
                    nc.gpsimd.tensor_tensor(rstd[:, :], var[:, :], neghalf[:, 0:2 * NT], ALU.pow).then_inc(s_rstd, 1)

            def pe(te):
                for i in turns(te, "tensor", B // 2):
                    for h in range(2):
                        te.wait_ge(s_h, h + 1)
                        for t in range(NT):
                            ins = te.transpose(ps_turn[:, h, t * P:(t + 1) * P], hx[:, h, t * D:(t + 1) * D], ident[:, :])
                        ins.then_inc(s_tr, 1)
                        te.wait_ge(s_hT, h + 1)
                        for c in range(FC):
                            if h == 1:
                                te.wait_ge(s_act, c + 1)
                            te.matmul(ps_score[:, c // 2, c % 2 * T:(c % 2 + 1) * T], W["L1_mw1"][:, c * P:(c + 1) * P],
                                      hxT[:, h, :], start=True, stop=True).then_inc(s_up, 1)
                    for h in range(2):
                        te.wait_ge(s_act, FC * (h + 1))
                        for t in range(NT):
                            for c in range(FC):
                                ins = te.matmul(ps_proj[:, h, t * D:(t + 1) * D], hidden[h][:, c, t * P:(t + 1) * P],
                                                W["L1_mw2"][:, c, :], start=(c == 0), stop=(c == FC - 1))
                        ins.then_inc(s_dn, 1)

            def act(ac):
                for i in turns(ac, "scalar", B // 2):
                    for h in range(2):
                        ac.wait_ge(s_tr, h + 1)
                        nc.scalar.activation(hxT[:, h, :], ps_turn[:, h, :], ACT.Copy).then_inc(s_hT, 1)
                        for c in range(FC):
                            ac.wait_ge(s_up, FC * h + c + 1)
                            nc.scalar.activation(hidden[h][:, c, :], ps_score[:, c // 2, c % 2 * T:(c % 2 + 1) * T], ACT.Gelu,
                                                 bias=W["L1_mb1"][:, c:c + 1]).then_inc(s_act, 1)
            return Phase(vec, act, pool, pe, s_var, s_out_, B // 2)

        def route_phase(L):
            s_pick = sem(f"{L}_picked")
            s_cnt = sem(f"{L}_counted")
            s_pos = sem(f"{L}_positions")
            s_exp = sem(f"{L}_tile_experts")
            s_sorted = sem(f"{L}_sorted")

            def vec(dv):
                st = Steps(dv, dve_chain)

                def first_best(dst, src):
                    st(nc.vector.tensor_reduce(best[:, :], src, AX.X, ALU.max))
                    st(nc.vector.tensor_tensor(pick8[:, :, :], src, best[:, :, None].broadcast_to([P, NTT, NE]), ALU.is_equal))
                    st(nc.vector.tensor_scalar(pick8[:, :, :], pick8[:, :, :], -100.0, 100.0, ALU.mult, ALU.add))
                    st(nc.vector.tensor_tensor(pick8[:, :, :], pick8[:, :, :], iota8[:, :, :], ALU.add))
                    st(nc.vector.tensor_reduce(dst[:, :], pick8[:, :, :], AX.X, ALU.min))

                def onehot(src):
                    return nc.vector.tensor_tensor(pick8b[:, :, :], iota8[:, :, :], src[:, :, None].broadcast_to([P, NTT, NE]), ALU.is_equal)

                first_best(pickA, gate[:, :, :])
                if L == 0:
                    st(onehot(pickA))
                    st(nc.vector.tensor_scalar(pick8b[:, :, :], pick8b[:, :, :], -3e38, None, ALU.mult))
                    st(nc.vector.tensor_tensor(pick8b[:, :, :], pick8b[:, :, :], gate[:, :, :], ALU.add))
                    first_best(pickB, pick8b[:, :, :])
                    st(nc.vector.tensor_tensor(pickA[:, :], pickA[:, :], pickB[:, :], ALU.max))
                onehot(pickA).then_inc(s_pick, 1)
                dv.wait_ge(s_cnt, 1)
                total = ps_proj[:, 1, 0:NTT * NE].rearrange("p (t e) -> p t e", e=NE)
                st(nc.vector.memset(before_tile[:, 0, :], 0.0))
                for t in range(1, NTT):
                    st(nc.vector.tensor_tensor(before_tile[:, t, :], before_tile[:, t - 1, :], total[:, t - 1, :], ALU.add))
                st(nc.vector.tensor_tensor(count8[:, :], before_tile[:, NTT - 1, :], total[:, NTT - 1, :], ALU.add))
                st(nc.vector.tensor_tensor(tiles16[:, :, :], count8[:, :, None].broadcast_to([P, NE, NTT]),
                                           step128[:, None, :].broadcast_to([P, NE, NTT]), ALU.is_gt))
                st(nc.vector.tensor_reduce(tiles8[:, :], tiles16[:, :, :], AX.X, ALU.add))
                st(nc.vector.memset(first8[:, 0:1], 0.0))
                for e in range(1, NE):
                    st(nc.vector.tensor_tensor(first8[:, e:e + 1], first8[:, e - 1:e], tiles8[:, e - 1:e], ALU.add))
                st(nc.vector.tensor_tensor(last8[:, :], first8[:, :], tiles8[:, :], ALU.add))
                st(nc.vector.tensor_tensor(reached[:, :, :], tile_no[:, :, None].broadcast_to([P, NXT, NE]),
                                           last8[:, None, :].broadcast_to([P, NXT, NE]), ALU.is_ge))
                st(nc.vector.tensor_reduce(expertf[:, :], reached[:, :, :], AX.X, ALU.add))
                nc.vector.tensor_scalar(expert[:, :], expertf[:, :], float(NE - 1), None, ALU.min).then_inc(s_exp, 1)
                st(nc.vector.tensor_scalar(first8[:, :], first8[:, :], float(P), None, ALU.mult))
                st(nc.vector.tensor_tensor(before_tile[:, :, :], before_tile[:, :, :], first8[:, None, :].broadcast_to([P, NTT, NE]), ALU.add))
                st(nc.vector.tensor_tensor(before_tile[:, :, :], before_tile[:, :, :],
                                           ps_proj[:, 0, 0:NTT * NE].rearrange("p (t e) -> p t e", e=NE), ALU.add))
                st(nc.vector.tensor_tensor(before_tile[:, :, :], before_tile[:, :, :], pick8b[:, :, :], ALU.mult))
                st(nc.vector.tensor_reduce(posf[:, :], before_tile[:, :, :], AX.X, ALU.add))
                nc.vector.tensor_copy(pos[:, :], posf[:, :]).then_inc(s_pos, 1)
                st.restart()

            def pe(te):
                te.wait_ge(s_pick, 1)
                one = pick8b[:, :, :].rearrange("p t e -> p (t e)")
                te.matmul(ps_proj[:, 0, 0:NTT * NE], earlier, one, start=True, stop=True)
                te.matmul(ps_proj[:, 1, 0:NTT * NE], ones[:, :], one, start=True, stop=True).then_inc(s_cnt, 1)

            def scatter(po):
                po.wait_ge(s_pos, 1)
                for t in range(NTT):
                    po.indirect_dma_start(out=sorted_x, out_offset=bass.IndirectOffsetOnAxis(ap=pos[:, t:t + 1], axis=0),
                                          in_=xn[:, t * D:(t + 1) * D], in_offset=None).then_inc(s_sorted, 16)
            return vec, pe, scatter, s_exp, s_sorted, s_pos

        def gather_phase(L):
            s_back = [sem(f"{L}_back{b}") for b in range(B)]

            def gather(po):
                for t in range(NTT):
                    po.indirect_dma_start(out=moe[:, t * D:(t + 1) * D], out_offset=None, in_=sorted_y,
                                          in_offset=bass.IndirectOffsetOnAxis(ap=pos[:, t:t + 1], axis=0)).then_inc(s_back[t // NT], 16)
            return gather, s_back

        def join_phase(L, s_back):
            s_e = sem(f"j{L}_e")
            s_x = sem(f"j{L}_x")
            k = 2.0 if L == 0 else 1.0

            def act(ac):
                for b in range(B):
                    at = slice(b * NT * D, (b + 1) * NT * D)
                    ac.wait_ge(s_back[b], 16 * NT)
                    nc.scalar.activation(moe[:, at], moe[:, at], ACT.Silu, scale=k).then_inc(s_e, 1)

            def vec(dv):
                st = Steps(dv, dve_chain)
                for b in range(B):
                    at = slice(b * NT * D, (b + 1) * NT * D)
                    dv.wait_ge(s_e, b + 1)
                    st(nc.vector.tensor_tensor(moe[:, at], moe[:, at], s_out[:, at], ALU.mult))
                    nc.vector.tensor_tensor(x[:, at], x[:, at], moe[:, at], ALU.add).then_inc(s_x, 1)
                dv.wait_ge(s_x, B)
                st.restart()
            return act, vec, s_x

        norm0 = norm_phase(0, None)
        route0_vec, route0_pe, scatter0, experts0, sorted0, _ = route_phase(0)
        attn0 = attention_phase(0)
        gather0, back0 = gather_phase(0)
        join0_act, join0_vec, joined0 = join_phase(0, back0)
        norm1 = norm_phase(1, joined0)
        route1_vec, route1_pe, scatter1, experts1, sorted1, _ = route_phase(1)
        attn1, mlp1 = attention_phase(1), mlp_phase()
        gather1, back1 = gather_phase(1)
        join1_act, join1_vec, joined1 = join_phase(1, back1)
        stored = sem("stored")

        @block.sync
        def _(sp):
            sync_load(sp)
            for ph, experts_known, all_sorted in ((norm0, None, None), (attn0, experts0, sorted0), (norm1, None, None),
                                                  (attn1, experts1, sorted1), (mlp1, None, None)):
                if experts_known is not None:
                    sp.wait_ge(experts_known, 1)
                    sp.wait_ge(all_sorted, 16 * NTT)
                with sp.Fori(0, ph.n) as i:
                    if ph.sync is not None:
                        ph.sync(sp, i)
                    clear_when_met(sp, ph.first, ph.last)
            for b in range(B):
                sp.wait_ge(joined1, b + 1)
                sp.dma_start(out3[:, b * NT:(b + 1) * NT, :],
                             x[:, b * NT * D:(b + 1) * NT * D].rearrange("p (n d) -> p n d", d=D)).then_inc(stored, 16)
            sp.wait_ge(stored, 16 * B)

        @block.vector
        def _(dv):
            norm0.vec(dv)
            route0_vec(dv)
            attn0.vec(dv)
            join0_vec(dv)
            norm1.vec(dv)
            route1_vec(dv)
            attn1.vec(dv)
            mlp1.vec(dv)
            join1_vec(dv)

        @block.scalar
        def _(ac):
            norm0.act(ac)
            attn0.act(ac)
            join0_act(ac)
            norm1.act(ac)
            attn1.act(ac)
            mlp1.act(ac)
            join1_act(ac)

        @block.gpsimd
        def _(po):
            pool_const(po)
            norm0.pool(po)
            scatter0(po)
            attn0.pool(po)
            gather0(po)
            norm1.pool(po)
            scatter1(po)
            attn1.pool(po)
            gather1(po)
            mlp1.pool(po)

        @block.tensor
        def _(te):
            norm0.pe(te)
            route0_pe(te)
            attn0.pe(te)
            norm1.pe(te)
            route1_pe(te)
            attn1.pe(te)
            mlp1.pe(te)


def bf16_bits(m):
    return (m.astype(np.float32).view(np.uint32) >> 16).astype(np.uint16)


def shape_constants():
    pos = np.arange(T)
    tok = (pos - ROT) % T
    c = {}
    c["ident"] = np.eye(P, dtype=np.float32)
    c["identb"] = bf16_bits(np.eye(P))
    c["iota8"] = np.broadcast_to(np.arange(NE, dtype=np.float32), (P, NTT, NE)).copy()

    def causal(u):
        q, k = 64 * u + np.arange(64), (64 * u - 64 + np.arange(P)) % T
        tq, tk = tok[q][:, None], tok[k][None, :]
        return (tk <= tq) & (tk >= tq - WIN)

    def sided(u):
        q, k = 64 * u + np.arange(64), (64 * u - 32 + np.arange(P)) % T
        end_q = (q < ROT) | (q >= T - 32)
        bad = (k[None, :] < 32) & ((k[None, :] < ROT) != end_q[:, None])
        near = (q < 64) | (q >= T - 32)
        return ~(bad & near[:, None])

    def pair(f, t):
        return np.concatenate([f(2 * t), f(2 * t + 1)])

    def penal(m, n):
        return bf16_bits(np.tile(np.where(m, 0.0, -BIG), (1, n)))

    c["maskq"] = np.stack([penal(pair(causal, 0), 4), penal(pair(causal, 1), 4),
                           penal(pair(sided, 0), 4), penal(pair(sided, 3), 4)], 1)
    c["maskk"] = np.stack([penal(causal(0).T, 8), penal(causal(1).T, 8), penal(causal(2).T, 8),
                           penal(sided(0).T, 8), penal(sided(NU - 1).T, 8)], 1)
    tab = np.zeros((P, 64), np.float32)
    al = np.linspace(0.0, 1.0, 32, dtype=np.float32)
    p = np.arange(P)
    for t in range(NT):
        tab[:, t] = (~pair(causal, t)).sum(1)
        alpha = al[p % 32].copy()
        if t == 0:
            alpha[:ROT], alpha[ROT:32] = 0.0, 1.0
        tab[:, 4 + t] = alpha
        tab[:, 8 + t] = 1 - alpha
    odd = (p // 32) % 2
    for g in range(4):
        tab[:, 12 + g] = np.where((g == odd) | (g == odd + 1), 0, -1e30)
        tab[:, 16 + g] = np.where((g == odd + 1) | (g == odd + 2), 0, -1e30)
        tab[:, 20 + g] = p // 32 == g
        tab[:, 24 + g] = p // 32 == g
    c["tab"] = tab
    c["cnst"] = np.concatenate([np.triu(np.ones((P, P)), 1), np.tile(128.0 * np.arange(NTT), (P, 1)),
                                np.tile(1.0 * np.arange(NXT), (P, 1))], 1).astype(np.float32)
    return c


def laid_out(inp):
    g = {k: np.ascontiguousarray(np.asarray(v)) for k, v in inp.items()}
    stored = [8 * hf + 4 * par + j for hf in range(2) for j in range(4) for par in range(2)]
    cols = np.array([h * HD + e for h in stored for e in range(HD)])
    a = {}
    a["x"] = np.roll(g["L0_attn_x"], ROT, axis=1)
    for L, q, k, v, o in ((0, "w_q", "w_k", "w_v", "w_o"), (1, "wq", "wk", "wv", "wproj")):
        n = f"L{L}_attn_"
        a[f"L{L}_wqk"] = np.concatenate([g[n + q][:, cols], g[n + k][:, cols]], 1)
        bq, bk, bv, bo = ("b_q", "b_k", "b_v", "b_o") if L == 0 else ("bq", "bk", "bv", "bproj")
        a[f"L{L}_bqk"] = np.concatenate([g[n + bq][cols], g[n + bk][cols]])
        a[f"L{L}_wv"], a[f"L{L}_bv"] = g[n + v], g[n + bv]
        a[f"L{L}_wo"], a[f"L{L}_bo"] = g[n + o], g[n + bo]
        f = f"L{L}_ffn_"
        a[f"L{L}_gw"] = g[f + "gate_w"] if L == 0 else g[f + "gate_w"].T
        a[f"L{L}_gb"] = g[f + "gate_b"]
        a[f"L{L}_w1e"] = g[f + "w1"].reshape(NE * P, DF)
        a[f"L{L}_w2e"] = g[f + "w2"].reshape(NE * DF, D)
        a[f"L{L}_b1e"], a[f"L{L}_b2e"] = g[f + "b1"].reshape(NE, FC, P).transpose(0, 2, 1).reshape(NE * P, FC), g[f + "b2"]
    a["L1_eb"] = g["L1_ffn_expert_bias"]
    a["L0_rms"] = np.concatenate([g["L0_attn_rms_q_w"], g["L0_attn_rms_k_w"]])
    for s, n in (("ln1g", "ln1_g"), ("ln1b", "ln1_b"), ("ln2g", "ln2_g"), ("ln2b", "ln2_b"),
                 ("mw1", "w1"), ("mb1", "b1"), ("mw2", "w2"), ("mb2", "b2")):
        a["L1_" + s] = g["L1_attn_" + n]
    a["L1_mb1"] = a["L1_mb1"].reshape(FC, P).T
    a.update(shape_constants())
    return {k: np.ascontiguousarray(v) for k, v in a.items()}


def kernel(**inputs):
    import concourse.bacc as bacc
    from concourse.bass_utils import run_bass_kernel_spmd

    arrays = laid_out(inputs)
    nc = bacc.Bacc("TRN2", target_bir_lowering=False, num_devices=1)
    aps = {n: nc.dram_tensor(f"in_{n}", v.shape, mybir.dt.from_np(v.dtype), kind="ExternalInput").ap()
           for n, v in arrays.items()}
    out = nc.dram_tensor("out", (B, T, D), F32, kind="ExternalOutput").ap()
    block_kernel(nc, aps, out, None)
    r = run_bass_kernel_spmd(nc, [{f"in_{n}": v for n, v in arrays.items()}], core_ids=[0])
    return np.roll(r.results[0]["out"], -ROT, axis=1)
```
